# Optimizing a Trainium2 kernel written in Bass

```python
import numpy as np
import jax
import jax.numpy as jnp

def _softmax(x, axis=-1):
    return jax.nn.softmax(x, axis=axis)
def _gelu(x):
    return jax.nn.gelu(x, approximate=True)
def _silu(x):
    return jax.nn.silu(x)
def _sigmoid(x):
    return jax.nn.sigmoid(x)
def _layernorm(x, axis=-1, eps=1e-5):
    m = jnp.mean(x, axis=axis, keepdims=True)
    v = jnp.var(x, axis=axis, keepdims=True)
    return (x - m) / jnp.sqrt(v + eps)
def _scatter_add(tgt, idx, src, axis=0):
    return tgt.at[idx].add(src)
def _segment_sum(src, seg, n):
    return jax.ops.segment_sum(src, seg, n)

kernel_name = 'mk_adj_preln_d4_adj_128_d466eb'

def setup_inputs(seed: int = 0):
    np.random.seed(seed)
    _w = jnp.asarray
    def _rec_inputs():
        import jax
        import jax.numpy as jnp
        _gk = jax.random.key(seed)
        x = -0.003407 + 1.001 * jax.random.normal(jax.random.fold_in(_gk, 1), (4096, 128), jnp.float32)
        _a = jax.random.bernoulli(jax.random.fold_in(_gk, 2), 0.00390625, (4096, 4096))
        _a = jnp.logical_or(_a, jnp.swapaxes(_a, -1, -2))
        _a = jnp.logical_or(_a, jnp.eye(4096, dtype=bool))
        adj = _a.astype(jnp.int32)
        return x, adj
    x, adj = _rec_inputs()
    def _L0_gnn_setup():
        import jax, jax.numpy as jnp
        import numpy as np
        N, IN_DIM, OUT_DIM, H = (1024, 128, 128, 4)
        D = OUT_DIM // H
        NEG_SLOPE = 0.2
        MASK_VAL = -1000000000.0
        LN_EPS = 1e-05
        key = jax.random.key(seed)
        k = jax.random.split(key, 8)
        h = jax.random.normal(k[0], (N, IN_DIM), dtype=jnp.float32)
        adj = jax.random.randint(k[1], (N, N), 0, 2, dtype=jnp.int32)
        adj = adj.at[jnp.arange(N), jnp.arange(N)].set(1)
        s = 1.0 / np.sqrt(IN_DIM)
        W_l = jax.random.normal(k[2], (IN_DIM, OUT_DIM), dtype=jnp.float32) * s
        W_r = jax.random.normal(k[3], (IN_DIM, OUT_DIM), dtype=jnp.float32) * s
        W_v = jax.random.normal(k[4], (IN_DIM, OUT_DIM), dtype=jnp.float32) * s
        a = jax.random.normal(k[5], (D,), dtype=jnp.float32) * (1.0 / np.sqrt(D))
        ln_g = jnp.ones((OUT_DIM,), dtype=jnp.float32)
        ln_b = jnp.zeros((OUT_DIM,), dtype=jnp.float32)
        return {'h': h, 'adj': adj, 'W_l': W_l, 'W_r': W_r, 'W_v': W_v, 'a': a, 'ln_g': ln_g, 'ln_b': ln_b}
    _L0_gnn_all = _L0_gnn_setup()
    _L0_gnn_in = {k: v for k, v in _L0_gnn_all.items() if k in ('W_l', 'W_r', 'W_v', 'a', 'ln_g', 'ln_b', )}
    del _L0_gnn_all

    def _L1_gnn_setup():
        import jax, jax.numpy as jnp
        import numpy as np
        NEG_INF = -9000000000000000.0
        LEAKY_SLOPE = 0.2
        key = jax.random.key(seed)
        k1, k2, k3, k4 = jax.random.split(key, 4)
        N, dim = (4096, 128)
        hidden = jax.random.normal(k1, (N, dim), dtype=jnp.float32)
        adj = jax.random.randint(k2, (N, N), 0, 5)
        W = jax.random.normal(k3, (4, dim), dtype=jnp.float32) * (1.0 / np.sqrt(dim))
        b = jax.random.normal(k4, (4,), dtype=jnp.float32) * 0.01
        return {'hidden': hidden, 'adj': adj, 'W': W, 'b': b}
    _L1_gnn_all = _L1_gnn_setup()
    _L1_gnn_in = {k: v for k, v in _L1_gnn_all.items() if k in ('W', 'b', )}
    del _L1_gnn_all

    def _L2_gnn_setup():
        import jax, jax.numpy as jnp
        import numpy as np
        N, IN_F, OUT_F, H = (4096, 128, 32, 4)
        key = jax.random.key(seed)
        k1, k2, k3, k4 = jax.random.split(key, 4)
        x = jax.random.normal(k1, (N, IN_F), dtype=jnp.float32)
        adj = jax.random.randint(k2, (N, N), 0, 2, dtype=jnp.int32)
        adj = jnp.maximum(adj, jnp.eye(N, dtype=jnp.int32))
        W = jax.random.normal(k3, (IN_F, OUT_F * H), dtype=jnp.float32) * 0.1
        a = jax.random.normal(k4, (H, 2 * OUT_F), dtype=jnp.float32) * 0.1
        return {'x': x, 'adj': adj, 'W': W, 'a': a}
    _L2_gnn_all = _L2_gnn_setup()
    _L2_gnn_in = {k: v for k, v in _L2_gnn_all.items() if k in ('W', 'a', )}
    del _L2_gnn_all

    def _L3_gnn_setup():
        import jax, jax.numpy as jnp
        import numpy as np
        N, D = (16384, 128)
        key = jax.random.key(seed)
        k1, k2 = jax.random.split(key)
        x = jax.random.normal(k1, (N, D), dtype=jnp.float32)
        adj = jax.random.randint(k2, (N, N), 0, 2, dtype=jnp.int32)
        return {'x': x, 'adj': adj}
    _L3_gnn_all = _L3_gnn_setup()
    _L3_gnn_in = {k: v for k, v in _L3_gnn_all.items() if k in ()}
    del _L3_gnn_all

    return {
        "x": x,
        "adj": adj,
        "L0_gnn_W_l": _L0_gnn_in["W_l"],
        "L0_gnn_W_r": _L0_gnn_in["W_r"],
        "L0_gnn_W_v": _L0_gnn_in["W_v"],
        "L0_gnn_a": _L0_gnn_in["a"],
        "L0_gnn_ln_g": _L0_gnn_in["ln_g"],
        "L0_gnn_ln_b": _L0_gnn_in["ln_b"],
        "L1_gnn_W": _L1_gnn_in["W"],
        "L1_gnn_b": _L1_gnn_in["b"],
        "L2_gnn_W": _L2_gnn_in["W"],
        "L2_gnn_a": _L2_gnn_in["a"],
    }

def reference(x, adj, L0_gnn_W_l, L0_gnn_W_r, L0_gnn_W_v, L0_gnn_a, L0_gnn_ln_g, L0_gnn_ln_b, L1_gnn_W, L1_gnn_b, L2_gnn_W, L2_gnn_a):
    import jax
    import jax.numpy as jnp
    def _L0_gnn_ref(h, adj, W_l, W_r, W_v, a, ln_g, ln_b):
        import jax, jax.numpy as jnp
        import numpy as np
        N, IN_DIM, OUT_DIM, H = (1024, 128, 128, 4)
        D = OUT_DIM // H
        NEG_SLOPE = 0.2
        MASK_VAL = -1000000000.0
        LN_EPS = 1e-05
        n = h.shape[0]
        Wlh = (h @ W_l).reshape(n, H, D)
        Wrh = (h @ W_r).reshape(n, H, D)
        pair = Wlh[:, None, :, :] + Wrh[None, :, :, :]
        pair = jnp.where(pair >= 0, pair, NEG_SLOPE * pair)
        e = jnp.einsum('ijhd,d->ijh', pair, a)
        mask = (adj != 0)[:, :, None]
        e = jnp.where(mask, e, MASK_VAL)
        alpha = jax.nn.softmax(e, axis=1)
        v = (h @ W_v).reshape(n, H, D)
        agg = jnp.einsum('ijh,jhd->ihd', alpha, v).reshape(n, OUT_DIM)
        mu = jnp.mean(agg, axis=-1, keepdims=True)
        var = jnp.mean((agg - mu) ** 2, axis=-1, keepdims=True)
        y = (agg - mu) * jax.lax.rsqrt(var + LN_EPS) * ln_g + ln_b
        return jax.nn.relu(y)

    def _L1_gnn_ref(hidden, adj, W, b):
        import jax, jax.numpy as jnp
        import numpy as np
        NEG_INF = -9000000000000000.0
        LEAKY_SLOPE = 0.2
        hw = hidden[None, :, :] * W[:, None, :]
        e = jnp.einsum('knd,md->knm', hw, hidden) + b[:, None, None]
        e = jax.nn.leaky_relu(e, negative_slope=LEAKY_SLOPE)
        neg = jnp.asarray(NEG_INF, dtype=e.dtype)
        alpha = jnp.where(adj == 1, e[0], neg)
        alpha = jnp.where(adj == 2, e[1], alpha)
        alpha = jnp.where(adj == 3, e[2], alpha)
        alpha = jnp.where(adj == 4, e[3], alpha)
        alpha = jax.nn.softmax(alpha, axis=-1)
        return alpha @ hidden

    def _L2_gnn_ref(x, adj, W, a):
        import jax, jax.numpy as jnp
        import numpy as np
        N, IN_F, OUT_F, H = (4096, 128, 32, 4)
        Wx = (x @ W).reshape(N, H, OUT_F)
        a_src, a_dst = (a[:, :OUT_F], a[:, OUT_F:])
        e_src = jnp.einsum('nhf,hf->nh', Wx, a_src)
        e_dst = jnp.einsum('nhf,hf->nh', Wx, a_dst)
        e = jax.nn.leaky_relu(e_src[:, None, :] + e_dst[None, :, :], 0.2)
        e = jnp.where((adj == 0)[:, :, None], -jnp.inf, e)
        alpha = jax.nn.softmax(e, axis=1)
        out = jnp.einsum('ijh,jhf->ihf', alpha, Wx)
        return out.reshape(N, H * OUT_F)

    def _L3_gnn_ref(x, adj):
        import jax, jax.numpy as jnp
        import numpy as np
        N, D = (16384, 128)
        a = adj.astype(x.dtype)
        return x + jnp.matmul(a, x)

    h = jnp.maximum(_layernorm(x, axis=-1), 0.0)
    x = x + _L0_gnn_ref(h, adj, L0_gnn_W_l, L0_gnn_W_r, L0_gnn_W_v, L0_gnn_a, L0_gnn_ln_g, L0_gnn_ln_b)
    h = jnp.maximum(_layernorm(x, axis=-1), 0.0)
    x = x + _L1_gnn_ref(h, adj, L1_gnn_W, L1_gnn_b)
    h = jnp.maximum(_layernorm(x, axis=-1), 0.0)
    x = x + _L2_gnn_ref(h, adj, L2_gnn_W, L2_gnn_a)
    h = jnp.maximum(_layernorm(x, axis=-1), 0.0)
    x = x + _L3_gnn_ref(h, adj)
    return x


_drawn_inputs = setup_inputs


def setup_inputs(seed=0):
    import zlib

    import numpy as np

    out = dict(_drawn_inputs(seed))
    spreads = {'L0_gnn_ln_g': (1.0, 0.2), 'L0_gnn_ln_b': (0.0, 0.1)}
    factors = {'L0_gnn_W_l': 5.126, 'L1_gnn_b': 8.0, 'L2_gnn_a': 4.155}
    for name, (base, spread) in spreads.items():
        noise = np.random.default_rng([zlib.crc32(name.encode()), seed]).standard_normal(out[name].shape)
        drawn = base * np.exp(spread * noise) if base else spread * noise
        out[name] = jnp.asarray(drawn.astype(out[name].dtype))
    for name, factor in factors.items():
        out[name] = (out[name] * factor).astype(out[name].dtype)
    return out
```

```python
from contextlib import ExitStack

import concourse.bass as bass
from concourse import mybir

F32 = mybir.dt.float32
BF16 = mybir.dt.bfloat16
I32 = mybir.dt.int32
U16 = mybir.dt.uint16
ALU = mybir.AluOpType
ACT = mybir.ActivationFunctionType
AX = mybir.AxisListType.X

P = 128
N, D = 4096, 128
T = N // P
HEADS, HD = 4, 32
LN_EPS = 1e-5
SLOPE = 0.2
SLOTS = 64
PART = 32
SEG = 64
NSEG = N // SEG
BAD_OVER = 0
MASKED = -1e30


class Count:

    def __init__(self, base):
        self.base, self.n = base, 0

    def inc(self):
        self.n += 1
        return 1

    def now(self):
        return self.base + self.n


def build(nc, x_in, adj, W_l, W_r, W_v, a0, ln_g, ln_b, W1, b1, W2, a2, out, upto=4):
    KV = 2 * D + HEADS
    kv_dram = nc.dram_tensor("kv_rows", [N, KV], F32, kind="Internal").ap()
    flag_dram = nc.dram_tensor("flag_rows", [2, P], F32, kind="Internal").ap()
    with ExitStack() as ctx:
        def sem(name):
            return ctx.enter_context(nc.semaphore(name))

        def sb(name, shape, dt=F32, where=ctx):
            return where.enter_context(nc.sbuf_tensor(name, shape, dt))

        def ps(name, shape, dt=F32, where=ctx):
            return where.enter_context(nc.psum_tensor(name, shape, dt))

        xs = sb("xs", [P, T, D])
        rows = sb("rows", [P, T, D])
        cols = sb("cols", [P, N])
        ident = sb("ident", [P, P])
        ones = sb("ones", [P, P])
        hrow = [sb(f"hrow{i}", [P, D]) for i in range(2)]
        hcol = [sb(f"hcol{i}", [P, P]) for i in range(2)]
        bst = sb("bst", [P, T, 6])
        mv = sb("mv", [P, T, 2])
        std = sb("std", [P, T])
        rstd = sb("rstd", [P, T])
        nmr = sb("nmr", [P, T])
        flags = sb("flags", [P, 2], I32)
        top0 = sb("top0", [P, T])
        nan = sb("nan", [P, T])
        wlrv = sb("wlrv", [P, 3 * D])
        arow = sb("arow", [P, D])
        grow = sb("grow", [P, D])
        brow = sb("brow", [P, D])

        x_loaded, w_loaded, consts = sem("x_loaded"), sem("w_loaded"), sem("consts")
        waited = sem("waited")
        block_sems = {}

        def layer_sems(n, names):
            block_sems[n] = {k: sem(f"L{n}_{k}") for k in names.split()}
            return block_sems[n]

        prep_sems = [layer_sems(f"{n}prep", "own var stats hrow_ready hT_ready hcol_ready w_ready w_out"
                                + " lin arow" * (n == 0)) for n in range(4)]
        layer_done = [sem(f"layer_done{n}") for n in range(4)]
        s = layer_sems(0, "adj_in0 adj_in1 adj_free squared own lists gathered0 gathered1 kl_sum kl_act kl_used "
                          "flag_own flag_rows flag_sum e_ready p_ready v_scaled summed0 summed1 sums_read flags_out flags "
                          "kvs_stored0 kvs_stored1")
        kvs_stored = [s["kvs_stored0"], s["kvs_stored1"]]
        adj_in = [s["adj_in0"], s["adj_in1"]]
        gathered = [s["gathered0"], s["gathered1"]]
        part_summed = [s["summed0"], s["summed1"]]

        z0 = ExitStack()
        ga = [sb(f"gathered_part{q}", [P, PART, KV], F32, z0) for q in range(2)]
        kl = sb("kl", [P, PART, D], F32, z0)
        adjt = [sb(f"adj_tile{i}", [P, N], I32, z0) for i in range(2)]
        key = sb("key", [P, N], U16, z0)
        iota = sb("iota", [P, N], U16, z0)
        cand = sb("cand", [P, NSEG * 8], F32, z0)
        top = sb("top", [P, SLOTS], F32, z0)
        idx = [sb(f"idx{i}", [P, SLOTS], I32, z0) for i in range(2)]
        mb = [sb(f"slot_mask{i}", [P, SLOTS], F32, z0) for i in range(2)]
        E = sb("E", [P, PART, HEADS], F32, z0)
        Pr = sb("Pr", [P, PART, HEADS], F32, z0)
        mx = [[sb(f"mx{p}{q}", [P, HEADS], F32, z0) for q in range(2)] for p in range(2)]
        cm = sb("cm", [P, HEADS], F32, z0)
        dm = [sb(f"dm{p}", [P, HEADS], F32, z0) for p in range(2)]
        sc = [sb(f"sc{p}", [P, HEADS], F32, z0) for p in range(2)]
        sm = [[sb(f"sm{p}{q}", [P, HEADS], F32, z0) for q in range(2)] for p in range(2)]
        o0 = sb("o0", [P, D], F32, z0)
        o1 = sb("o1", [P, D], F32, z0)
        den = sb("den", [P, HEADS], F32, z0)
        ksum = sb("ksum", [P, T], F32, z0)
        tsum = sb("tsum", [P, T], F32, z0)
        sq = sb("sq", [P, T], F32, z0)
        kvs = [sb(f"kvs{i}", [P, KV], F32, z0) for i in range(2)]
        lin = sb("lin", [P, 2, D], F32, z0)
        li = sb("li", [P, T, HEADS], F32, z0)
        sqj = sb("sqj", [P, N], BF16, z0)
        mhalf = sb("mhalf", [P, 1], F32, z0)
        odd = sb("odd", [P, 3, T], F32, z0)
        fl = sb("fl", [P, 3], F32, z0)
        on = sb("on", [P, PART], F32, z0)
        off = sb("off", [P, PART], F32, z0)
        z0.close()

        z1 = ExitStack()
        adj1 = [sb(f"adj1_{i}", [P, N], I32, z1) for i in range(2)]
        mask1 = [sb(f"mask1_{i}", [P, N], BF16, z1) for i in range(2)]
        Z1 = [sb(f"Z1_{i}", [P, N], F32, z1) for i in range(2)]
        P1 = [sb(f"P1_{i}", [P, N], F32, z1) for i in range(2)]
        pT1 = sb("pT1", [P, N], F32, z1)
        hs = [sb(f"hs{i}", [P, P], F32, z1) for i in range(2)]
        w1c = sb("w1c", [P, 4], F32, z1)
        b1c = sb("b1c", [P, 4], F32, z1)
        zm = [sb(f"zm{i}", [P, 1], F32, z1) for i in range(2)]
        nm = [sb(f"nm{i}", [P, 1], F32, z1) for i in range(2)]
        rs = [sb(f"rs{i}", [P, 1], F32, z1) for i in range(2)]
        ri = sb("ri", [P, 1], F32, z1)
        z1.close()
        z2 = ExitStack()
        adj2 = sb("adj2", [P, N], I32, z2)
        mask2 = sb("mask2", [P, N], BF16, z2)
        Z2 = [sb(f"Z2_{i}", [P, N], F32, z2) for i in range(2)]
        pT2 = sb("pT2", [P, N], F32, z2)
        dbc = sb("dbc", [P, HEADS, N], F32, z2)
        w2s = sb("w2s", [P, D + HEADS], F32, z2)
        asd = sb("asd", [P, HEADS, 2, HD], F32, z2)
        wa = sb("wa", [P, D], F32, z2)
        wd = sb("wd", [P, HEADS], F32, z2)
        wrep = sb("wrep", [P, HEADS, P], F32, z2)
        si = sb("si", [P, T, HEADS], F32, z2)
        zm2 = [sb(f"zm2_{i}", [P, 1], F32, z2) for i in range(2)]
        nm2 = [sb(f"nm2_{i}", [P, 1], F32, z2) for i in range(2)]
        rs2 = [sb(f"rs2_{i}", [P, 1], F32, z2) for i in range(2)]
        ri2 = sb("ri2", [P, 1], F32, z2)
        z2.close()

        pz = ExitStack()
        pS = [ps(f"pS{i}", [P, 512], F32, pz) for i in range(2)]
        pX = [ps(f"pX{i}", [P, 512], F32, pz) for i in range(4)]
        pO = [ps(f"pO{i}", [P, 512], F32, pz) for i in range(2)]
        pz.close()
        pz = ExitStack()
        pT = [ps(f"prep_T{i}", [P, P], F32, pz) for i in range(2)]
        pW = [ps(f"prep_W{i}", [P, 3 * D], F32, pz) for i in range(2)]
        pz.close()
        pz = ExitStack()
        pK = [ps(f"pK{i}", [P, 8, D], F32, pz) for i in range(2)]
        pA = [ps(f"pA{i}", [P, 4, D], F32, pz) for i in range(2)]
        pz.close()

        adj_v = adj.rearrange("(t p) j -> t p j", p=P)

        def adj_tile(t):
            return adj_v[t, :, :] if isinstance(t, int) else adj_v[bass.ds(t, 1), :, :].rearrange("a p j -> (a p) j")

        block = ctx.enter_context(nc.Block())

        def row_stats_vector(v, src, q):
            with v.Fori(0, T) as t:
                v.bn_stats(bst[:, t, :], src[:, t, :]).then_inc(q["own"], 1)
            v.wait_ge(q["own"], T)
            for t in range(T):
                v.bn_aggr(mv[:, t, :], bst[:, t, :]).then_inc(q["own"], 1)
            v.wait_ge(q["own"], 2 * T)
            v.tensor_scalar(std[:, :], mv[:, :, 1], LN_EPS, None, ALU.add).then_inc(q["var"], 1)
            v.wait_ge(q["var"], 2)
            v.reciprocal(rstd[:, :], std[:, :]).then_inc(q["own"], 1)
            v.wait_ge(q["own"], 2 * T + 1)
            v.scalar_tensor_tensor(nmr[:, :], mv[:, :, 0], -1.0, rstd[:, :], ALU.mult, ALU.mult)\
             .then_inc(q["stats"], 1)

        def root_scalar(a, q):
            a.wait_ge(q["var"], 1)
            a.activation(std[:, :], std[:, :], ACT.Sqrt).then_inc(q["var"], 1)

        def prep_vector(v, n):
            q = prep_sems[n]

            def weights(u, p):
                t = 2 * u + p
                v.wait_ge(q["w_ready"], t + 1)
                if n == 2:
                    v.tensor_copy(rows[:, t, :], pW[p][:, 0:D])
                    v.tensor_copy(si[:, t, :], pW[p][:, D:D + HEADS]).then_inc(q["w_out"], 1)
                if n == 0:
                    if not isinstance(u, int):
                        v.wait_ge(kvs_stored[p], 16 * u)
                    v.tensor_copy(cols[:, bass.ts(t, D)], pW[p][:, 0:D])
                    v.tensor_copy(kvs[p][:, 0:2 * D], pW[p][:, D:3 * D])
                    v.wait_ge(q["lin"], 2 * t)
                    v.tensor_tensor(lin[:, :, :], pW[p][:, 0:2 * D].rearrange("p (a d) -> p a d", a=2),
                                    arow[:, :].unsqueeze(1).to_broadcast([P, 2, D]), ALU.mult).then_inc(q["lin"], 1)
                    v.wait_ge(q["lin"], 2 * t + 1)
                    v.tensor_reduce(li[:, t, :], lin[:, 0, :].rearrange("p (h d) -> p h d", h=HEADS), AX, ALU.add)
                    v.tensor_reduce(kvs[p][:, 2 * D:KV], lin[:, 1, :].rearrange("p (h d) -> p h d", h=HEADS),
                                    AX, ALU.add).then_inc(q["lin"], 1)
                    v.wait_ge(q["lin"], 2 * t + 2)
                    v.tensor_scalar(li[:, t, :], li[:, t, :], SLOPE / (1 - SLOPE), None, ALU.mult)
                    v.tensor_scalar(kvs[p][:, 2 * D:KV], kvs[p][:, 2 * D:KV], SLOPE / (1 - SLOPE), None, ALU.mult)\
                     .then_inc(q["w_out"], 1)

            row_stats_vector(v, xs, q)
            if n in (0, 2):
                weights(0, 0)
                weights(0, 1)
                with v.Fori(1, T // 2) as u:
                    weights(u, 0)
                    weights(u, 1)

        def prep_scalar(a, n):
            q = prep_sems[n]

            def tile(u, p):
                t = 2 * u + p
                a.wait_ge(q["hT_ready"], t)
                a.activation(hrow[p][:, :], xs[:, t, :], ACT.Relu, bias=nmr[:, bass.ds(t, 1)], scale=rstd[:, bass.ds(t, 1)])\
                 .then_inc(q["hrow_ready"], 1)
                if n in (1, 3):
                    a.wait_ge(q["hrow_ready"], t + 1)
                    a.copy(rows[:, t, :], hrow[p][:, :])

            def turned(u, p):
                t = 2 * u + p
                a.wait_ge(q["hT_ready"], t + 1)
                if n in (0, 2):
                    a.wait_ge(q["w_ready"], t)
                    a.copy(hcol[p][:, :], pT[p][:, :]).then_inc(q["hcol_ready"], 1)
                    if n == 2:
                        a.copy(cols[:, bass.ts(t, P)], pT[p][:, :])
                else:
                    a.copy(cols[:, bass.ts(t, P)], pT[p][:, :]).then_inc(q["hcol_ready"], 1)
            root_scalar(a, q)
            a.wait_ge(q["stats"], 1)
            with a.Fori(0, T // 2) as u:
                for p in range(2):
                    tile(u, p)
                    turned(u, p)

        def prep_tensor(e, n):
            q = prep_sems[n]
            with e.Fori(0, T // 2) as u:
                for p in range(2):
                    t = 2 * u + p
                    e.wait_ge(q["hrow_ready"], t + 1)
                    e.wait_ge(q["hcol_ready"], t)
                    e.transpose(pT[p][:, :], hrow[p][:, :], ident[:, :]).then_inc(q["hT_ready"], 1)
                    if n in (0, 2):
                        w = wlrv[:, :] if n == 0 else w2s[:, :]
                        e.wait_ge(q["hcol_ready"], t + 1)
                        e.wait_ge(q["w_out"], t)
                        e.matmul(pW[p][:, 0:3 * D if n == 0 else D + HEADS], hcol[p][:, :], w, start=True, stop=True)\
                         .then_inc(q["w_ready"], 1)

        own0 = 3 + 8 * 2 + 4

        OWN_LIST = 2 + 15 + 1
        OWN_A = 5
        OWN_FIN = 8
        OWN_TILE = OWN_LIST + 2 * (OWN_A + 1) + OWN_FIN

        def settled(eng):
            eng.sem_inc(waited, 1)

        def list_vector(v, u, p, c):
            t = 2 * u + p
            v.wait_ge(adj_in[p], 16 * (u + 1))
            v.scalar_tensor_tensor(key[:, :], adjt[p][:, :], 0.0, iota[:, :], ALU.not_equal, ALU.mult,
                                   accum_out=ksum[:, bass.ds(t, 1)]).then_inc(s["own"], c.inc())
            v.wait_ge(s["own"], c.now())
            v.sem_inc(s["adj_free"], 1)
            for g in range(NSEG):
                ins = v.max(cand[:, 8 * g:8 * g + 8], key[:, SEG * g:SEG * (g + 1)])
            ins.then_inc(s["own"], c.inc())
            for r in range(SLOTS // 8):
                v.wait_ge(s["own"], c.now())
                settled(v)
                v.max(top[:, 8 * r:8 * r + 8], cand[:, :]).then_inc(s["own"], c.inc())
                if r < SLOTS // 8 - 1:
                    v.wait_ge(s["own"], c.now())
                    settled(v)
                    v.match_replace(cand[:, :], top[:, 8 * r:8 * r + 8], cand[:, :], 0.0)\
                     .then_inc(s["own"], c.inc())
            v.wait_ge(s["own"], c.now())
            if u_ge1(u):
                for q in range(2):
                    v.wait_ge(gathered[q], 16 * PART * (t - 1))
            v.tensor_scalar(idx[p][:, :], top[:, :], -1.0, float(N), ALU.mult, ALU.add)
            v.tensor_scalar(mb[p][:, :], top[:, :], 0.0, MASKED, ALU.is_equal, ALU.mult)
            v.tensor_copy(top0[:, bass.ds(t, 1)], top[:, 0:1])
            v.tensor_reduce(tsum[:, bass.ds(t, 1)], top[:, :], AX, ALU.add).then_inc(s["lists"], 1)

        def u_ge1(u):
            return not (isinstance(u, int) and u == 0)

        def bc(ap, shape):
            return ap.to_broadcast(shape)

        def a_vector(v, u, p, q, c):
            t = 2 * u + p
            seq = 2 * t + q
            v.wait_ge(s["kl_act"], 4 * (seq + 1))
            v.tensor_tensor(kl[:, :, :], kl[:, :, :], arow[:, :].unsqueeze(1).to_broadcast([P, PART, D]), ALU.mult)\
             .then_inc(s["own"], c.inc())
            v.wait_ge(s["own"], c.now())
            v.tensor_reduce(E[:, :, :], kl[:, :, :].rearrange("p s (h d) -> p s h d", h=HEADS), AX, ALU.add)\
             .then_inc(s["kl_used"], 1)
            v.wait_ge(s["kl_used"], seq + 1)
            v.wait_ge(s["lists"], t + 1)
            v.tensor_tensor(E[:, :, :], E[:, :, :], ga[q][:, :, 2 * D:KV], ALU.add).then_inc(s["own"], c.inc())
            v.wait_ge(s["own"], c.now())
            v.tensor_tensor(E[:, :, :], E[:, :, :], li[:, t, :].unsqueeze(1).to_broadcast([P, PART, HEADS]), ALU.add)\
             .then_inc(s["own"], c.inc())
            v.wait_ge(s["own"], c.now())
            v.tensor_tensor(E[:, :, :], E[:, :, :],
                            mb[p][:, q * PART:(q + 1) * PART].unsqueeze(2).to_broadcast([P, PART, HEADS]), ALU.add)\
             .then_inc(s["own"], c.inc())
            v.wait_ge(s["own"], c.now())
            m_out = mx[p][0] if q == 0 else cm
            v.tensor_reduce(m_out[:, :], E[:, :, :].rearrange("p s h -> p h s"), AX, ALU.max)\
             .then_inc(s["own"], c.inc())
            v.wait_ge(s["own"], c.now())
            if q == 1:
                v.tensor_tensor(mx[p][1][:, :], mx[p][0][:, :], cm[:, :], ALU.max).then_inc(s["own"], c.inc())
                v.wait_ge(s["own"], c.now())
                v.tensor_tensor(dm[p][:, :], mx[p][0][:, :], mx[p][1][:, :], ALU.subtract)
            v.tensor_tensor(E[:, :, :], E[:, :, :], mx[p][q][:, :].unsqueeze(1).to_broadcast([P, PART, HEADS]),
                            ALU.subtract).then_inc(s["e_ready"], 1)

        def b_vector(v, u, p, q):
            t = 2 * u + p
            seq = 2 * t + q
            v.wait_ge(s["p_ready"], seq + 1)
            V = ga[q][:, :, D:2 * D].rearrange("p s (h d) -> p s h d", h=HEADS)
            v.tensor_tensor(V, V, Pr[:, :, :].unsqueeze(3).to_broadcast([P, PART, HEADS, HD]), ALU.mult)\
             .then_inc(s["v_scaled"], 1)
            v.tensor_reduce(sm[p][q][:, :], Pr[:, :, :].rearrange("p s h -> p h s"), AX, ALU.add)\
             .then_inc(s["own_b"], 1)

        def fin_vector(v, u, p, c):
            t = 2 * u + p
            v.wait_ge(s["own_b"], 2 * (t + 1))
            v.wait_ge(s["p_scale"], t + 1)
            v.wait_ge(part_summed[0], t + 1)
            v.wait_ge(part_summed[1], t + 1)
            v.tensor_reduce(o0[:, :], pA[0][:, :, :].rearrange("p k d -> p d k"), AX, ALU.add)
            v.tensor_reduce(o1[:, :], pA[1][:, :, :].rearrange("p k d -> p d k"), AX, ALU.add)\
             .then_inc(s["sums_read"], 1)
            v.tensor_tensor(den[:, :], sm[p][0][:, :], sc[p][:, :], ALU.mult).then_inc(s["own"], c.inc())
            v.wait_ge(s["sums_read"], t + 1)
            o0h = o0[:, :].rearrange("p (h d) -> p h d", h=HEADS)
            v.tensor_tensor(o0h, o0h, sc[p][:, :].unsqueeze(2).to_broadcast([P, HEADS, HD]), ALU.mult)\
             .then_inc(s["own"], c.inc())
            v.wait_ge(s["own"], c.now())
            v.tensor_tensor(den[:, :], den[:, :], sm[p][1][:, :], ALU.add).then_inc(s["own"], c.inc())
            v.tensor_tensor(o0[:, :], o0[:, :], o1[:, :], ALU.add).then_inc(s["own"], c.inc())
            v.wait_ge(s["own"], c.now())
            v.reciprocal(den[:, :], den[:, :]).then_inc(s["own"], c.inc())
            v.wait_ge(s["own"], c.now())
            v.tensor_tensor(rows[:, t, :].rearrange("p (h d) -> p h d", h=HEADS), o0h,
                            den[:, :].unsqueeze(2).to_broadcast([P, HEADS, HD]), ALU.mult).then_inc(s["own"], c.inc())

        s["own_b"] = sem("L0_own_b")
        NL, NA0, NA1, NF = 17, 5, 6, 6
        NB = NL + NA0 + NA1 + NF

        def l0_vector(v):
            for p in range(2):
                v.wait_ge(consts, 4)
            list_vector(v, 0, 0, Count(0))
            list_vector(v, 0, 1, Count(NL))

            def tile(u, p, first=False, last=False):
                t = 2 * u + p
                c = Count(2 * NL + NB * t)
                up, pp = (u, 0) if p == 1 else (u - 1, 1)
                a_vector(v, u, p, 0, c)
                b_vector(v, u, p, 0)
                if not first:
                    fin_vector(v, up, pp, c)
                else:
                    c.n += NF
                    v.sem_inc(s["own"], NF)
                a_vector(v, u, p, 1, c)
                if not last:
                    list_vector(v, u + 1, p, c)
                else:
                    c.n += NL
                    v.sem_inc(s["own"], NL)
                b_vector(v, u, p, 1)
                assert c.n == NB, c.n
            tile(0, 0, first=True)
            tile(0, 1)
            with v.Fori(1, T // 2 - 1) as u:
                tile(u, 0)
                tile(u, 1)
            tile(T // 2 - 1, 0, last=True)
            tile(T // 2 - 1, 1, last=True)
            c = Count(2 * NL + NB * T)
            fin_vector(v, T // 2 - 1, 1, c)
            v.wait_ge(s["own"], c.now())

        def l0_scalar(a):
            a.wait_ge(consts, 4)

            def square(u, p):
                t = 2 * u + p
                a.wait_ge(adj_in[p], 16 * (u + 1))
                a.wait_ge(s["squared"], t)
                a.activation(sqj[:, :], adjt[p][:, :], ACT.Square, bias=mhalf[:, 0:1],
                             accum_out=sq[:, bass.ds(t, 1)]).then_inc(s["squared"], 1)

            def tile(u, p, last=False):
                t = 2 * u + p
                for q in range(2):
                    seq = 2 * t + q
                    a.wait_ge(s["kl_used"], seq)
                    for g in range(4):
                        a.wait_ge(s["kl_sum"], 4 * seq + g + 1)
                        a.activation(kl[:, 8 * g:8 * g + 8, :], pK[g % 2][:, :, :], ACT.Relu)\
                         .then_inc(s["kl_act"], 1)
                    if q == 1 and not last:
                        square(u + 1, p)
                    a.wait_ge(s["e_ready"], seq + 1)
                    a.activation(Pr[:, :, :], E[:, :, :], ACT.Exp).then_inc(s["p_ready"], 1)
                    if q == 1:
                        a.activation(sc[p][:, :], dm[p][:, :], ACT.Exp).then_inc(s["p_scale"], 1)
            square(0, 0)
            square(0, 1)
            with a.Fori(0, T // 2 - 1) as u:
                tile(u, 0)
                tile(u, 1)
            tile(T // 2 - 1, 0, last=True)
            tile(T // 2 - 1, 1, last=True)

        s["p_scale"] = sem("L0_p_scale")

        def l0_tensor(e):
            def sums(u, p, q):
                t = 2 * u + p
                seq = 2 * t + q
                e.wait_ge(gathered[q], 16 * PART * (t + 1))
                wl = cols[:, bass.ts(t, D)].unsqueeze(1).to_broadcast([P, 4, D])
                for g in range(4):
                    if not (isinstance(t, int) and t == 0 and q == 0 and g < 2):
                        e.wait_ge(s["kl_act"], 4 * seq + g - 1)
                    for b in range(2):
                        k = 8 * g + 4 * b
                        e.matmul(pK[g % 2][:, 4 * b:4 * b + 4, :], ident[:, :], ga[q][:, k:k + 4, 0:D],
                                 start=True, stop=False)
                        ins = e.matmul(pK[g % 2][:, 4 * b:4 * b + 4, :], ident[:, :], wl, start=False, stop=True)
                    ins.then_inc(s["kl_sum"], 1)

            def total(u, p, q):
                t = 2 * u + p
                e.wait_ge(s["v_scaled"], 2 * t + q + 1)
                e.wait_ge(s["sums_read"], t)
                for k in range(PART // 4):
                    ins = e.matmul(pA[q][:, :, :], ident[:, :], ga[q][:, 4 * k:4 * k + 4, D:2 * D],
                                   start=(k == 0), stop=(k == PART // 4 - 1))
                ins.then_inc(part_summed[q], 1)

            def tile(u, p):
                for q in range(2):
                    sums(u, p, q)
                    total(u, p, q)
            tile(0, 0)
            tile(0, 1)
            with e.Fori(1, T // 2) as u:
                tile(u, 0)
                tile(u, 1)

        def l0_gpsimd(g):
            with g.Fori(0, T // 2) as u:
                for p in range(2):
                    t = 2 * u + p
                    g.wait_ge(s["lists"], t + 1)
                    for q in range(2):
                        g.wait_ge(part_summed[q], t)
                        settled(g)
                        for k in range(PART):
                            g.indirect_dma_start(
                                out=ga[q][:, k, :], out_offset=None, in_=kv_dram[:, :],
                                in_offset=bass.IndirectOffsetOnAxis(ap=idx[p][:, q * PART + k:q * PART + k + 1], axis=0),
                                bounds_check=N - 1, oob_is_err=False).then_inc(gathered[q], 16)

        def l0_sync(y):
            adj_v = adj.rearrange("(t p) j -> t p j", p=P)
            for p in range(2):
                y.dma_start(adjt[p][:, :], adj_v[p, :, :]).then_inc(adj_in[p], 16)
            with y.Fori(1, T // 2) as u:
                for p in range(2):
                    t = 2 * u + p
                    y.wait_ge(s["adj_free"], t - 1)
                    y.wait_ge(s["squared"], t - 1)
                    y.dma_start(adjt[p][:, :], adj_v[bass.ds(t, 1), :, :].rearrange("a p j -> (a p) j"))\
                     .then_inc(adj_in[p], 16)

        def flags_vector(v):
            v.wait_ge(s["squared"], T)
            v.tensor_tensor(odd[:, 0, :], ksum[:, :], tsum[:, :], ALU.not_equal)
            v.tensor_scalar(odd[:, 1, :], top0[:, :], 0.0, None, ALU.is_equal)
            v.tensor_scalar(odd[:, 2, :], sq[:, :], N / 4, None, ALU.not_equal).then_inc(s["flag_own"], 1)
            v.wait_ge(s["flag_own"], 1)
            v.tensor_reduce(fl[:, :], odd[:, :, :], AX, ALU.max).then_inc(s["flag_rows"], 1)
            v.wait_ge(s["flag_sum"], 1)
            v.tensor_copy(fl[:, 0:3], pA[1][:, 0, 0:3]).then_inc(s["flag_own"], 1)
            v.wait_ge(s["flag_own"], 2)
            v.tensor_tensor(flags[:, 0:1], fl[:, 0:1], fl[:, 1:2], ALU.add)
            v.tensor_copy(flags[:, 1:2], fl[:, 2:3]).then_inc(s["flags"], 1)

        def flags_tensor(e):
            e.wait_ge(s["flag_rows"], 1)
            e.matmul(pA[1][:, 0, 0:3], ones[:, :], fl[:, 0:3], start=True, stop=True).then_inc(s["flag_sum"], 1)

        def flag(eng, k):
            eng.wait_ge(s["flags"], 1)
            return eng.value_load(flags[0:1, k:k + 1], min_val=0, max_val=2 * N)

        d0 = layer_sems("0dense", "adj in0 in1 kl_sum kl_act own e_ready p_ready v_scaled summed done masks masks2")
        CH = N // (2 * PART)
        D_STEPS = 18

        def dense_parts(eng, tile_start, part, tile_end):
            with eng.Fori(0, T) as t:
                tile_start(t)
                with eng.Fori(0, CH) as c:
                    for q in range(2):
                        part(t, c, q, 2 * (CH * t + c) + q)
                tile_end(t)

        def dense_sync(y):
            def start(t):
                y.wait_ge(d0["done"], t)
                y.dma_start(adjt[0][:, :], adj_tile(t)).then_inc(d0["adj"], 16)

            def part(t, c, q, seq):
                y.wait_ge(d0["summed"], seq)
                src = kv_dram[bass.ds(c * (2 * PART) + q * PART, PART), :].rearrange("s d -> (s d)")
                y.dma_start(ga[q][:, :, :].rearrange("p s d -> p (s d)"),
                            src.unsqueeze(0).to_broadcast([P, PART * KV])).then_inc(d0[f"in{q}"], 16)
            dense_parts(y, start, part, lambda t: None)

        def dense_tensor(e):
            def part(t, c, q, seq):
                e.wait_ge(d0[f"in{q}"], 16 * (CH * t + c + 1))
                wl = cols[:, bass.ts(t, D)].unsqueeze(1).to_broadcast([P, 4, D])
                for g in range(4):
                    e.wait_ge(d0["kl_act"], 4 * seq + g)
                    for b in range(2):
                        k = 8 * g + 4 * b
                        e.matmul(pK[g % 2][:, 4 * b:4 * b + 4, :], ident[:, :], ga[q][:, k:k + 4, 0:D],
                                 start=True, stop=False)
                        ins = e.matmul(pK[g % 2][:, 4 * b:4 * b + 4, :], ident[:, :], wl, start=False, stop=True)
                    ins.then_inc(d0["kl_sum"], 1)
                e.wait_ge(d0["v_scaled"], seq + 1)
                for k in range(PART // 4):
                    ins = e.matmul(pA[q][:, :, :], ident[:, :], ga[q][:, 4 * k:4 * k + 4, D:2 * D],
                                   start=(k == 0), stop=(k == PART // 4 - 1))
                ins.then_inc(d0["summed"], 1)
            dense_parts(e, lambda t: None, part, lambda t: None)

        def dense_scalar(a):
            def part(t, c, q, seq):
                for g in range(4):
                    a.wait_ge(d0["kl_sum"], 4 * seq + g + 1)
                    a.activation(kl[:, 8 * g:8 * g + 8, :], pK[g % 2][:, :, :], ACT.Relu).then_inc(d0["kl_act"], 1)
                a.wait_ge(d0["e_ready"], seq + 1)
                a.activation(Pr[:, :, :], E[:, :, :], ACT.Exp)
                a.activation(sc[0][:, :], dm[0][:, :], ACT.Exp).then_inc(d0["p_ready"], 1)
            dense_parts(a, lambda t: None, part, lambda t: None)

        def dense_vector(v):
            m, total = mx[0][0], sm[0][0]
            o0h = o0[:, :].rearrange("p (h d) -> p h d", h=HEADS)

            def start(t):
                v.memset(m[:, :], -3e38)
                v.memset(total[:, :], 0.0)
                v.memset(o0[:, :], 0.0).then_inc(d0["masks"], 1)
                v.wait_ge(d0["adj"], 16 * (t + 1))
                v.wait_ge(d0["masks"], t + 1)
                settled(v)

            def part(t, c, q, seq):
                k = Count(D_STEPS * seq)
                own = d0["own"]

                def last():
                    v.wait_ge(own, k.now())
                wide = [P, PART, HEADS]
                v.tensor_scalar(on[:, :], adjt[0][:, bass.ds(c * (2 * PART) + q * PART, PART)], 0.0, None,
                                ALU.not_equal).then_inc(own, k.inc())
                last()
                v.tensor_scalar(off[:, :], on[:, :], -1.0, 1e9, ALU.add, ALU.mult).then_inc(own, k.inc())
                v.wait_ge(d0["kl_act"], 4 * (seq + 1))
                v.tensor_tensor(kl[:, :, :], kl[:, :, :], arow[:, :].unsqueeze(1).to_broadcast([P, PART, D]),
                                ALU.mult).then_inc(own, k.inc())
                last()
                v.tensor_reduce(E[:, :, :], kl[:, :, :].rearrange("p s (h d) -> p s h d", h=HEADS), AX, ALU.add)\
                 .then_inc(own, k.inc())
                for other, op in ((ga[q][:, :, 2 * D:KV], ALU.add),
                                  (li[:, t, :].unsqueeze(1).to_broadcast(wide), ALU.add),
                                  (on[:, :].unsqueeze(2).to_broadcast(wide), ALU.mult),
                                  (off[:, :].unsqueeze(2).to_broadcast(wide), ALU.add)):
                    last()
                    v.tensor_tensor(E[:, :, :], E[:, :, :], other, op).then_inc(own, k.inc())
                last()
                v.tensor_reduce(cm[:, :], E[:, :, :].rearrange("p s h -> p h s"), AX, ALU.max).then_inc(own, k.inc())
                last()
                v.tensor_tensor(cm[:, :], cm[:, :], m[:, :], ALU.max).then_inc(own, k.inc())
                last()
                v.tensor_tensor(dm[0][:, :], m[:, :], cm[:, :], ALU.subtract).then_inc(own, k.inc())
                last()
                v.tensor_copy(m[:, :], cm[:, :])
                v.tensor_tensor(E[:, :, :], E[:, :, :], cm[:, :].unsqueeze(1).to_broadcast(wide), ALU.subtract)\
                 .then_inc(d0["e_ready"], 1)
                v.wait_ge(d0["p_ready"], seq + 1)
                V = ga[q][:, :, D:2 * D].rearrange("p s (h d) -> p s h d", h=HEADS)
                v.tensor_tensor(V, V, Pr[:, :, :].unsqueeze(3).to_broadcast([P, PART, HEADS, HD]), ALU.mult)\
                 .then_inc(d0["v_scaled"], 1)
                v.tensor_reduce(sm[0][1][:, :], Pr[:, :, :].rearrange("p s h -> p h s"), AX, ALU.add)
                v.tensor_tensor(total[:, :], total[:, :], sc[0][:, :], ALU.mult).then_inc(own, k.inc())
                last()
                v.tensor_tensor(total[:, :], total[:, :], sm[0][1][:, :], ALU.add)
                v.tensor_tensor(o0h, o0h, sc[0][:, :].unsqueeze(2).to_broadcast([P, HEADS, HD]), ALU.mult)\
                 .then_inc(own, k.inc())
                v.wait_ge(d0["summed"], seq + 1)
                v.tensor_reduce(o1[:, :], pA[q][:, :, :].rearrange("p k d -> p d k"), AX, ALU.add)\
                 .then_inc(own, k.inc())
                last()
                v.tensor_tensor(o0[:, :], o0[:, :], o1[:, :], ALU.add).then_inc(own, k.inc())
                last()
                v.sem_inc(own, D_STEPS - k.n)

            def end(t):
                v.reciprocal(den[:, :], total[:, :]).then_inc(d0["masks2"], 1)
                v.wait_ge(d0["masks2"], t + 1)
                v.tensor_tensor(rows[:, t, :].rearrange("p (h d) -> p h d", h=HEADS), o0h,
                                den[:, :].unsqueeze(2).to_broadcast([P, HEADS, HD]), ALU.mult)\
                 .then_inc(d0["done"], 1)
                v.wait_ge(d0["done"], t + 1)
            dense_parts(v, start, part, end)

        end_sems = layer_sems("0end", "own var stats tile")

        def l0_end_vector(v):
            row_stats_vector(v, rows, end_sems)
            v.wait_ge(end_sems["stats"], 1)

            def tile(u, p):
                t = 2 * u + p
                c = Count(4 * t)
                v.wait_ge(end_sems["tile"], c.now())
                v.tensor_scalar(hrow[p][:, :], rows[:, t, :], rstd[:, bass.ds(t, 1)], nmr[:, bass.ds(t, 1)],
                                ALU.mult, ALU.add).then_inc(end_sems["tile"], c.inc())
                v.wait_ge(end_sems["tile"], c.now())
                v.tensor_tensor(hrow[p][:, :], hrow[p][:, :], grow[:, :], ALU.mult).then_inc(end_sems["tile"], c.inc())
                v.wait_ge(end_sems["tile"], c.now())
                v.tensor_tensor(hrow[p][:, :], hrow[p][:, :], brow[:, :], ALU.add).then_inc(end_sems["tile"], c.inc())
                v.wait_ge(end_sems["tile"], c.now())
                v.scalar_tensor_tensor(xs[:, t, :], hrow[p][:, :], 0.0, xs[:, t, :], ALU.max, ALU.add)\
                 .then_inc(end_sems["tile"], c.inc())
            with v.Fori(0, T // 2) as u:
                tile(u, 0)
                tile(u, 1)
            v.wait_ge(end_sems["tile"], 4 * T)
            v.sem_inc(layer_done[0], 1)

        GROUPS = T // 4

        def evac_no(g, act_groups):
            mine = g in act_groups
            return mine, sum((k in act_groups) == mine for k in range(g + 1))

        def tail_tensor(e, L, seq, pbuf, pT_, rhs, out_ap, act_groups):
            nA, nV = len(act_groups), GROUPS - len(act_groups)

            def emptied(g):
                mine, k = evac_no(g, act_groups)
                e.wait_ge(L["evA"] if mine else L["evV"], (nA if mine else nV) * seq + k)

            def turn(g):
                if g >= 4:
                    emptied(g - 4)
                for k in range(4):
                    j = 4 * g + k
                    ins = e.transpose(pX[g % 4][:, k * P:(k + 1) * P], pbuf[:, j * P:(j + 1) * P], ident[:, :])
                ins.then_inc(L["turned"], 1)

            e.wait_ge(L["p_ready"], seq + 1)
            for g in range(4):
                turn(g)
            e.wait_ge(L["o_read"], seq)
            for g in range(GROUPS):
                emptied(g)
                for k in range(4):
                    j = 4 * g + k
                    ins = e.matmul(out_ap, pT_[:, j * P:(j + 1) * P], rhs(j), start=(j == 0), stop=(j == T - 1))
                if g + 4 < GROUPS:
                    turn(g + 4)
            ins.then_inc(L["o_ready"], 1)

        def tail_evac(eng, copy, L, seq, pT_, act_groups, is_act):
            for g in range(GROUPS):
                if (g in act_groups) == is_act:
                    eng.wait_ge(L["turned"], GROUPS * seq + g + 1)
                    copy(pT_[:, g * 512:(g + 1) * 512], pX[g % 4][:, :]).then_inc(L["evA" if is_act else "evV"], 1)

        TAIL = "p_ready turned evA evV o_ready o_read"

        def pairs(eng, tile):
            with eng.Fori(0, T // 2 - 1) as u:
                tile(u, 0, False)
                tile(u, 1, False)
            tile(T // 2 - 1, 0, True)
            tile(T // 2 - 1, 1, True)

        L1 = layer_sems(1, TAIL + " adj0 adj1 mask w_in hs_ready s_ready z_ready zmax leaky own nmax rcp fin")
        L1_ACT = (1, 3, 5, 7)
        NEG1 = -9e15

        def l1_sync(y):
            y.wait_ge(layer_done[0], 1)
            y.dma_start(w1c[:, :], W1.rearrange("k d -> d k"), allow_slow_non_contiguous=True).then_inc(L1["w_in"], 16)
            y.dma_start(b1c[:, :], b1.unsqueeze(0).to_broadcast([P, 4])).then_inc(L1["w_in"], 16)
            with y.If(flag(y, 1) > 0):
                any_sync(y)
            with y.Else():
                binary_sync(y)

        def binary_sync(y):
            for p in range(2):
                y.dma_start(adj1[p][:, :], adj_tile(p)).then_inc(L1[f"adj{p}"], 16)
            with y.Fori(1, T // 2) as u:
                for p in range(2):
                    t = 2 * u + p
                    y.wait_ge(L1["mask"], t - 1)
                    y.dma_start(adj1[p][:, :], adj_tile(t)).then_inc(L1[f"adj{p}"], 16)

        def l1_vector(v):
            def mask(u, p):
                v.wait_ge(L1[f"adj{p}"], 16 * (u + 1))
                v.tensor_scalar(mask1[p][:, :], adj1[p][:, :], 1.0, NEG1, ALU.not_equal, ALU.mult)\
                 .then_inc(L1["mask"], 1)

            def scores(u, p):
                t = 2 * u + p
                v.wait_ge(L1["z_ready"], GROUPS * (t + 1))
                v.wait_ge(L1["mask"], t + 1)
                settled(v)
                v.tensor_tensor_reduce(Z1[p][:, :], Z1[p][:, :], mask1[p][:, :], 1.0, -3e38, ALU.add, ALU.max,
                                       zm[p][:, :]).then_inc(L1["zmax"], 1)
                v.wait_ge(L1["zmax"], t + 1)
                v.scalar_tensor_tensor(Z1[p][:, :], Z1[p][:, :], SLOPE, Z1[p][:, :], ALU.mult, ALU.max)
                v.scalar_tensor_tensor(nm[p][:, :], zm[p][:, :], SLOPE, zm[p][:, :], ALU.mult, ALU.max)\
                 .then_inc(L1["own"], 1)
                v.wait_ge(L1["own"], t + 1)
                v.tensor_scalar(nm[p][:, :], nm[p][:, :], -1.0, None, ALU.mult).then_inc(L1["leaky"], 1)

            def finish(u, p):
                t = 2 * u + p
                v.wait_ge(L1["p_ready"], t + 1)
                v.reciprocal(ri[:, :], rs[p][:, :]).then_inc(L1["rcp"], 1)
                v.wait_ge(L1["rcp"], t + 1)
                v.wait_ge(L1["o_ready"], t + 1)
                v.scalar_tensor_tensor(xs[:, t, :], pO[p][:, 0:D], ri[:, 0:1], xs[:, t, :], ALU.mult, ALU.add)\
                 .then_inc(L1["o_read"], 1)

            def tile(u, p, last):
                t = 2 * u + p
                if not (last and p == 1):
                    scores(u + p, 1 - p)
                tail_evac(v, v.tensor_copy, L1, t, pT1, L1_ACT, False)
                if not last:
                    mask(u + 1, p)
                finish(u, p)
            mask(0, 0)
            mask(0, 1)
            scores(0, 0)
            pairs(v, tile)
            v.wait_ge(L1["o_read"], T)
            v.sem_inc(layer_done[1], 1)

        def l1_scalar(a):
            def lhs(u, p):
                t = 2 * u + p
                if not (isinstance(u, int) and u == 0):
                    a.wait_ge(L1["s_ready"], GROUPS * (t - 1))
                a.activation(hs[p][:, :], cols[:, bass.ts(t, P)], ACT.Copy, scale=w1c[:, 0:1])\
                 .then_inc(L1["hs_ready"], 1)

            def evac_scores(u, p):
                t = 2 * u + p
                if not (isinstance(u, int) and u == 0):
                    a.wait_ge(L1["p_ready"], t - 1)
                for c in range(GROUPS):
                    a.wait_ge(L1["s_ready"], GROUPS * t + c + 1)
                    a.activation(Z1[p][:, c * 512:(c + 1) * 512], pS[c % 2][:, :], ACT.Identity, bias=b1c[:, 0:1])\
                     .then_inc(L1["z_ready"], 1)

            def exps(u, p):
                t = 2 * u + p
                a.wait_ge(L1["leaky"], t + 1)
                if not (isinstance(u, int) and u == 0):
                    a.wait_ge(L1["turned"], GROUPS * (t - 1))
                    a.wait_ge(L1["rcp"], t - 1)
                a.activation(P1[p][:, :], Z1[p][:, :], ACT.Exp, bias=nm[p][:, 0:1], accum_out=rs[p][:, 0:1])\
                 .then_inc(L1["p_ready"], 1)

            def tile(u, p, last):
                t = 2 * u + p
                if not last:
                    lhs(u + 1, p)
                    evac_scores(u + 1, p)
                tail_evac(a, a.copy, L1, t, pT1, L1_ACT, True)
                if not (last and p == 1):
                    exps(u + p, 1 - p)
            for p in range(2):
                lhs(0, p)
                evac_scores(0, p)
            exps(0, 0)
            pairs(a, tile)

        def l1_tensor(e):
            def scores(u, p):
                t = 2 * u + p
                e.wait_ge(L1["hs_ready"], t + 1)
                for c in range(GROUPS):
                    if not (isinstance(t, int) and t == 0 and c < 2):
                        e.wait_ge(L1["z_ready"], GROUPS * t + c - 1)
                    e.matmul(pS[c % 2][:, :], hs[p][:, :], cols[:, c * 512:(c + 1) * 512], start=True, stop=True)\
                     .then_inc(L1["s_ready"], 1)

            def tile(u, p, last):
                if not last:
                    scores(u + 1, p)
                tail_tensor(e, L1, 2 * u + p, P1[p], pT1, lambda j: rows[:, j, :], pO[p][:, 0:D], L1_ACT)
            scores(0, 0)
            scores(0, 1)
            pairs(e, tile)

        G1 = layer_sems("1any", TAIL + " adj hs_ready s_ready z_ready used sum own done")
        G1_STEPS = 14

        def any_sync(y):
            with y.Fori(0, T) as t:
                y.wait_ge(G1["o_read"], t)
                y.dma_start(adj1[0][:, :], adj_tile(t)).then_inc(G1["adj"], 16)

        def any_tensor(e):
            with e.Fori(0, T) as t:
                for k in range(4):
                    e.wait_ge(G1["hs_ready"], 4 * t + k + 1)
                    for c in range(GROUPS):
                        if k or c >= 2:
                            e.wait_ge(G1["z_ready"], GROUPS * (4 * t + k) + c - 1)
                        e.matmul(pS[c % 2][:, :], hs[0][:, :], cols[:, c * 512:(c + 1) * 512], start=True, stop=True)\
                         .then_inc(G1["s_ready"], 1)
                tail_tensor(e, G1, t, P1[0], pT1, lambda j: rows[:, j, :], pO[0][:, 0:D], L1_ACT)

        def any_scalar(a):
            with a.Fori(0, T) as t:
                for k in range(4):
                    a.wait_ge(G1["s_ready"], GROUPS * (4 * t + k))
                    settled(a)
                    a.activation(hs[0][:, :], cols[:, bass.ts(t, P)], ACT.Copy, scale=w1c[:, k:k + 1])\
                     .then_inc(G1["hs_ready"], 1)
                    a.wait_ge(G1["used"], 4 * t + k)
                    for c in range(GROUPS):
                        a.wait_ge(G1["s_ready"], GROUPS * (4 * t + k) + c + 1)
                        a.activation(Z1[0][:, c * 512:(c + 1) * 512], pS[c % 2][:, :], ACT.Identity,
                                     bias=b1c[:, k:k + 1]).then_inc(G1["z_ready"], 1)
                a.wait_ge(G1["sum"], t + 1)
                a.activation(P1[0][:, :], Z1[1][:, :], ACT.Exp, accum_out=rs[0][:, 0:1]).then_inc(G1["p_ready"], 1)
                tail_evac(a, a.copy, G1, t, pT1, L1_ACT, True)

        def any_vector(v):
            alpha, tmp, own = Z1[1], P1[1], G1["own"]
            with v.Fori(0, T) as t:
                k = Count(G1_STEPS * t)
                v.wait_ge(G1["adj"], 16 * (t + 1))
                v.tensor_scalar(alpha[:, :], adj1[0][:, :], 1.0, None, ALU.is_ge)
                v.tensor_scalar(tmp[:, :], adj1[0][:, :], 4.0, None, ALU.is_le).then_inc(own, k.inc())
                v.wait_ge(own, k.now())
                v.tensor_tensor(alpha[:, :], alpha[:, :], tmp[:, :], ALU.mult).then_inc(own, k.inc())
                v.wait_ge(own, k.now())
                v.tensor_scalar(alpha[:, :], alpha[:, :], -1.0, -NEG1, ALU.add, ALU.mult).then_inc(own, k.inc())
                for j in range(4):
                    v.wait_ge(G1["z_ready"], GROUPS * (4 * t + j + 1))
                    v.wait_ge(own, k.now())
                    v.scalar_tensor_tensor(tmp[:, :], Z1[0][:, :], SLOPE, Z1[0][:, :], ALU.mult, ALU.max)\
                     .then_inc(G1["used"], 1)
                    v.wait_ge(G1["used"], 4 * t + j + 1)
                    v.scalar_tensor_tensor(tmp[:, :], adj1[0][:, :], float(j + 1), tmp[:, :], ALU.is_equal, ALU.mult)\
                     .then_inc(own, k.inc())
                    v.wait_ge(own, k.now())
                    v.tensor_tensor(alpha[:, :], alpha[:, :], tmp[:, :], ALU.add).then_inc(own, k.inc())
                v.wait_ge(own, k.now())
                v.tensor_reduce(zm[0][:, :], alpha[:, :], AX, ALU.max).then_inc(own, k.inc())
                v.wait_ge(own, k.now())
                v.tensor_scalar(alpha[:, :], alpha[:, :], zm[0][:, 0:1], None, ALU.subtract).then_inc(G1["sum"], 1)
                tail_evac(v, v.tensor_copy, G1, t, pT1, L1_ACT, False)
                v.wait_ge(G1["p_ready"], t + 1)
                v.reciprocal(ri[:, :], rs[0][:, :]).then_inc(own, k.inc())
                v.wait_ge(own, k.now())
                v.wait_ge(G1["o_ready"], t + 1)
                v.scalar_tensor_tensor(xs[:, t, :], pO[0][:, 0:D], ri[:, 0:1], xs[:, t, :], ALU.mult, ALU.add)\
                 .then_inc(G1["o_read"], 1)
                v.sem_inc(own, G1_STEPS - k.n)
            v.wait_ge(G1["o_read"], T)
            v.sem_inc(layer_done[1], 1)

        L2 = layer_sems(2, TAIL + " adj mask w_in wmade d_ready d_outV d_outA z_in own zmax leaky rcp nan")
        L2_ACT = (1, 2, 4, 5, 7)
        P2 = cols

        def l2_sync(y):
            y.wait_ge(layer_done[1], 1)
            y.dma_start(w2s[:, 0:D], W2).then_inc(L2["w_in"], 16)
            y.dma_start(asd[:, :, :, :].rearrange("p h a f -> p (h a f)"),
                        a2.rearrange("h f -> (h f)").unsqueeze(0).to_broadcast([P, 2 * D])).then_inc(L2["w_in"], 16)
            y.dma_start(adj2[:, :], adj_tile(0)).then_inc(L2["adj"], 16)
            with y.Fori(1, T) as t:
                y.wait_ge(L2["mask"], t)
                y.dma_start(adj2[:, :], adj_tile(t)).then_inc(L2["adj"], 16)

        def l2_weights_vector(v):
            c = Count(0)
            v.wait_ge(L2["w_in"], 32)
            for side, to in ((0, w2s[:, D:D + HEADS]), (1, wd[:, :])):
                v.wait_ge(L2["wmade"], c.now())
                v.tensor_tensor(wa[:, :].rearrange("p (h f) -> p h f", h=HEADS),
                                w2s[:, 0:D].rearrange("p (h f) -> p h f", h=HEADS), asd[:, :, side, :], ALU.mult)\
                 .then_inc(L2["wmade"], c.inc())
                v.wait_ge(L2["wmade"], c.now())
                v.tensor_reduce(to, wa[:, :].rearrange("p (h f) -> p h f", h=HEADS), AX, ALU.add)\
                 .then_inc(L2["wmade"], c.inc())
            v.wait_ge(L2["wmade"], c.now())
            for h in range(HEADS):
                ins = v.tensor_scalar(wrep[:, h, :], ones[:, :], wd[:, h:h + 1], None, ALU.mult)
            ins.then_inc(L2["wmade"], c.inc())

        def l2_vector(v):
            for k in range(HEADS * GROUPS):
                if k % 2 == 0:
                    v.wait_ge(L2["d_ready"], k + 1)
                    v.tensor_copy(dbc[:, k // GROUPS, (k % GROUPS) * 512:(k % GROUPS + 1) * 512], pX[k % 4][:, :])\
                     .then_inc(L2["d_outV"], 1)

            def mask(t):
                v.wait_ge(L2["adj"], 16 * (t + 1))
                v.tensor_scalar(mask2[:, :], adj2[:, :], 0.0, MASKED, ALU.is_equal, ALU.mult)\
                 .then_inc(L2["mask"], 1)

            def scores(t, h):
                seq, p = HEADS * t + h, h % 2
                if h == 0:
                    v.wait_ge(L2["mask"], t + 1)
                v.wait_ge(L2["z_in"], seq + 1)
                v.scalar_tensor_tensor(Z2[p][:, :], Z2[p][:, :], SLOPE, Z2[p][:, :], ALU.mult, ALU.max)\
                 .then_inc(L2["own"], 1)
                v.wait_ge(L2["own"], seq + 1)
                settled(v)
                v.tensor_tensor_reduce(Z2[p][:, :], Z2[p][:, :], mask2[:, :], 1.0, -3e38, ALU.add, ALU.max,
                                       zm2[p][:, :]).then_inc(L2["zmax"], 1)
                v.wait_ge(L2["zmax"], seq + 1)
                v.tensor_scalar(nm2[p][:, :], zm2[p][:, :], -1.0, None, ALU.mult).then_inc(L2["leaky"], 1)

            def finish(t, h):
                seq, p = HEADS * t + h, h % 2
                v.wait_ge(L2["p_ready"], seq + 1)
                v.reciprocal(ri2[:, :], rs2[p][:, :]).then_inc(L2["rcp"], 1)
                v.wait_ge(L2["rcp"], seq + 1)
                v.wait_ge(L2["o_ready"], seq + 1)
                xh = xs[:, t, h * HD:(h + 1) * HD]
                v.scalar_tensor_tensor(xh, pO[p][:, 0:HD], ri2[:, 0:1], xh, ALU.mult, ALU.add)\
                 .then_inc(L2["o_read"], 1)

            def tile(t, last):
                for h in range(HEADS):
                    if h < HEADS - 1:
                        scores(t, h + 1)
                    elif not last:
                        scores(t + 1, 0)
                    tail_evac(v, v.tensor_copy, L2, HEADS * t + h, pT2, L2_ACT, False)
                    if h == HEADS - 2 and not last:
                        mask(t + 1)
                    finish(t, h)
            mask(0)
            scores(0, 0)
            with v.Fori(0, T - 1) as t:
                tile(t, False)
            tile(T - 1, True)
            c = Count(0)
            v.tensor_scalar(nan[:, :], top0[:, :], 0.0, 1e38, ALU.is_equal, ALU.mult).then_inc(L2["nan"], c.inc())
            v.wait_ge(L2["nan"], c.now())
            v.tensor_scalar(nan[:, :], nan[:, :], 1e38, None, ALU.mult).then_inc(L2["nan"], c.inc())
            v.wait_ge(L2["nan"], c.now())
            v.tensor_tensor(nan[:, :], nan[:, :], nan[:, :], ALU.subtract).then_inc(L2["nan"], c.inc())
            v.wait_ge(L2["nan"], c.now())
            v.wait_ge(L2["o_read"], HEADS * T)
            v.tensor_tensor(xs[:, :, :], xs[:, :, :], nan[:, :].unsqueeze(2).to_broadcast([P, T, D]), ALU.add)\
             .then_inc(layer_done[2], 1)
            v.wait_ge(layer_done[2], 1)

        def l2_scalar(a):
            for k in range(HEADS * GROUPS):
                if k % 2 == 1:
                    a.wait_ge(L2["d_ready"], k + 1)
                    a.copy(dbc[:, k // GROUPS, (k % GROUPS) * 512:(k % GROUPS + 1) * 512], pX[k % 4][:, :])\
                     .then_inc(L2["d_outA"], 1)

            def sums(t, h):
                a.activation(Z2[h % 2][:, :], dbc[:, h, :], ACT.Identity, bias=si[:, t, h:h + 1])\
                 .then_inc(L2["z_in"], 1)

            def exps(t, h, first):
                seq, p = HEADS * t + h, h % 2
                a.wait_ge(L2["leaky"], seq + 1)
                if not (first and h == 0):
                    a.wait_ge(L2["turned"], GROUPS * seq)
                if not (first and h < 2):
                    a.wait_ge(L2["rcp"], seq - 1)
                a.activation(P2[:, :], Z2[p][:, :], ACT.Exp, bias=nm2[p][:, 0:1], accum_out=rs2[p][:, 0:1])\
                 .then_inc(L2["p_ready"], 1)

            def tile(t, first, last):
                for h in range(HEADS):
                    if h < HEADS - 2 or not last:
                        a.wait_ge(L2["p_ready"], HEADS * t + h + 1)
                        sums(*((t, h + 2) if h < HEADS - 2 else (t + 1, h - 2)))
                    tail_evac(a, a.copy, L2, HEADS * t + h, pT2, L2_ACT, True)
                    if h < HEADS - 1:
                        exps(t, h + 1, first)
                    elif not last:
                        exps(t + 1, 0, False)
            a.wait_ge(L2["d_outV"], HEADS * GROUPS // 2)
            a.wait_ge(L2["d_outA"], HEADS * GROUPS // 2)
            a.wait_ge(prep_sems[2]["w_out"], T)
            sums(0, 0)
            sums(0, 1)
            exps(0, 0, True)
            tile(0, True, False)
            with a.Fori(1, T - 1) as t:
                tile(t, False, False)
            tile(T - 1, False, True)

        def l2_tensor(e):
            e.wait_ge(prep_sems[2]["w_out"], T)
            for k in range(HEADS * GROUPS):
                if k >= 4:
                    e.wait_ge(L2["d_outA" if k % 2 else "d_outV"], (k - 4) // 2 + 1)
                e.matmul(pX[k % 4][:, :], wrep[:, k // GROUPS, :], cols[:, (k % GROUPS) * 512:(k % GROUPS + 1) * 512],
                         start=True, stop=True).then_inc(L2["d_ready"], 1)
            with e.Fori(0, T) as t:
                for h in range(HEADS):
                    tail_tensor(e, L2, HEADS * t + h, P2, pT2, lambda j: rows[:, j, h * HD:(h + 1) * HD],
                                pO[h % 2][:, 0:HD], L2_ACT)

        L3 = layer_sems(3, TAIL + " adj0 adj1 own")
        L3_ACT = (0, 1, 3, 4, 6, 7)

        def l3_sync(y):
            y.wait_ge(layer_done[2], 1)
            for p in range(2):
                y.dma_start(adj1[p][:, :], adj_tile(p)).then_inc(L3[f"adj{p}"], 16)
            with y.Fori(1, T // 2) as u:
                for p in range(2):
                    t = 2 * u + p
                    y.wait_ge(L3["p_ready"], t - 1)
                    y.dma_start(adj1[p][:, :], adj_tile(t)).then_inc(L3[f"adj{p}"], 16)

        def l3_vector(v):
            def cast(u, p):
                t = 2 * u + p
                v.wait_ge(L3[f"adj{p}"], 16 * (u + 1))
                if not (isinstance(u, int) and u == 0):
                    v.wait_ge(L3["turned"], GROUPS * (t - 1))
                v.tensor_copy(P1[p][:, :], adj1[p][:, :]).then_inc(L3["p_ready"], 1)

            def tile(u, p, last):
                t = 2 * u + p
                if not (last and p == 1):
                    cast(u + p, 1 - p)
                v.tensor_tensor(xs[:, t, :], xs[:, t, :], rows[:, t, :], ALU.add).then_inc(L3["own"], 1)
                tail_evac(v, v.tensor_copy, L3, t, pT1, L3_ACT, False)
                v.wait_ge(L3["own"], t + 1)
                v.wait_ge(L3["o_ready"], t + 1)
                v.tensor_tensor(xs[:, t, :], pO[p][:, 0:D], xs[:, t, :], ALU.add).then_inc(L3["o_read"], 1)
            v.wait_ge(prep_sems[3]["hcol_ready"], T)
            cast(0, 0)
            pairs(v, tile)

        def l3_scalar(a):
            pairs(a, lambda u, p, last: tail_evac(a, a.copy, L3, 2 * u + p, pT1, L3_ACT, True))

        def l3_tensor(e):
            pairs(e, lambda u, p, last: tail_tensor(e, L3, 2 * u + p, P1[p], pT1, lambda j: rows[:, j, :],
                                                    pO[p][:, 0:D], L3_ACT))

        @block.sync
        def _(y):
            y.dma_start(xs[:, :, :], x_in.rearrange("(t p) d -> p t d", p=P)).then_inc(x_loaded, 16)
            for i, w in enumerate((W_l, W_r, W_v)):
                y.dma_start(wlrv[:, i * D:(i + 1) * D], w).then_inc(w_loaded, 16)
            for h in range(HEADS):
                y.dma_start(arow[:, h * HD:(h + 1) * HD], a0.unsqueeze(0).to_broadcast([P, HD])).then_inc(w_loaded, 16)
            y.dma_start(grow[:, :], ln_g.unsqueeze(0).to_broadcast([P, D])).then_inc(w_loaded, 16)
            y.dma_start(brow[:, :], ln_b.unsqueeze(0).to_broadcast([P, D])).then_inc(w_loaded, 16)
            q = prep_sems[0]
            kv_v = kv_dram.rearrange("(t p) d -> t p d", p=P)
            with y.Fori(0, T // 2) as u:
                for p in range(2):
                    t = 2 * u + p
                    y.wait_ge(q["w_out"], t + 1)
                    y.dma_start(kv_v[bass.ds(t, 1), :, :].rearrange("a p d -> (a p) d"), kvs[p][:, :])\
                     .then_inc(kvs_stored[p], 16)
            l0_sync(y)
            with y.If(flag(y, 0) > BAD_OVER):
                dense_sync(y)
            last = layer_done[0]
            if upto > 1:
                l1_sync(y)
            if upto > 2:
                l2_sync(y)
            if upto > 3:
                l3_sync(y)
                y.wait_ge(L3["o_read"], T)
            else:
                y.wait_ge(layer_done[upto - 1], 1)
            y.dma_start(out.rearrange("(t p) d -> p t d", p=P), xs[:, :, :]).then_inc(s["flags_out"], 16)
            y.wait_ge(s["flags_out"], 16)

        @block.gpsimd
        def _(g):
            g.memset(ident[:, :], 0.0).then_inc(consts, 1)
            g.memset(ones[:, :], 1.0)
            g.memset(mhalf[:, :], -0.5)
            g.wait_ge(consts, 1)
            g.affine_select(out=ident[:, :], in_=ident[:, :], compare_op=ALU.not_equal, fill=1.0,
                            base=0, pattern=[[-1, P]], channel_multiplier=1).then_inc(consts, 1)
            g.iota(iota[:, :], [[-1, N]], base=N, channel_multiplier=0).then_inc(consts, 1)
            g.memset(ga[0][:, :, :], 0.0)
            g.memset(ga[1][:, :, :], 0.0).then_inc(consts, 1)
            g.wait_ge(consts, 4)
            for p in range(2):
                g.wait_ge(kvs_stored[p], 16 * (T // 2))
            l0_gpsimd(g)
        @block.vector
        def _(v):
            v.wait_ge(x_loaded, 16)
            v.wait_ge(w_loaded, 16 * 9)
            v.tensor_scalar(arow[:, :], arow[:, :], 1 - SLOPE, None, ALU.mult).then_inc(prep_sems[0]["arow"], 1)
            v.wait_ge(prep_sems[0]["arow"], 1)
            prep_vector(v, 0)
            l0_vector(v)
            flags_vector(v)
            with v.If(flag(v, 0) > BAD_OVER):
                dense_vector(v)
            l0_end_vector(v)
            if upto > 1:
                prep_vector(v, 1)
                with v.If(flag(v, 1) > 0):
                    any_vector(v)
                with v.Else():
                    l1_vector(v)
            if upto > 2:
                l2_weights_vector(v)
                prep_vector(v, 2)
                l2_vector(v)
            if upto > 3:
                prep_vector(v, 3)
                l3_vector(v)

        @block.scalar
        def _(a):
            a.wait_ge(x_loaded, 16)
            prep_scalar(a, 0)
            l0_scalar(a)
            with a.If(flag(a, 0) > BAD_OVER):
                dense_scalar(a)
            root_scalar(a, end_sems)
            if upto > 1:
                prep_scalar(a, 1)
                a.wait_ge(L1["w_in"], 32)
                a.wait_ge(prep_sems[1]["hcol_ready"], T)
                with a.If(flag(a, 1) > 0):
                    any_scalar(a)
                with a.Else():
                    l1_scalar(a)
            if upto > 2:
                prep_scalar(a, 2)
                l2_scalar(a)
            if upto > 3:
                prep_scalar(a, 3)
                l3_scalar(a)

        @block.tensor
        def _(e):
            e.wait_ge(consts, 4)
            e.wait_ge(w_loaded, 16 * 9)
            prep_tensor(e, 0)
            l0_tensor(e)
            flags_tensor(e)
            with e.If(flag(e, 0) > BAD_OVER):
                dense_tensor(e)
            if upto > 1:
                prep_tensor(e, 1)
                e.wait_ge(prep_sems[1]["hcol_ready"], T)
                with e.If(flag(e, 1) > 0):
                    any_tensor(e)
                with e.Else():
                    l1_tensor(e)
            if upto > 2:
                e.wait_ge(L2["wmade"], 5)
                prep_tensor(e, 2)
                l2_tensor(e)
            if upto > 3:
                prep_tensor(e, 3)
                e.wait_ge(prep_sems[3]["hcol_ready"], T)
                l3_tensor(e)


_INS = ["x", "adj", "L0_gnn_W_l", "L0_gnn_W_r", "L0_gnn_W_v", "L0_gnn_a", "L0_gnn_ln_g", "L0_gnn_ln_b",
        "L1_gnn_W", "L1_gnn_b", "L2_gnn_W", "L2_gnn_a"]


def kernel(**inputs):
    import numpy as _np
    import concourse.bacc as _bacc
    from concourse import mybir as _mybir
    from concourse.bass_utils import run_bass_kernel_spmd as _run

    nc = _bacc.Bacc("TRN2", target_bir_lowering=False, num_devices=1)
    arrays, args = {}, []
    for name in _INS:
        a = _np.ascontiguousarray(inputs[name])
        arrays[f"in_{name}_dram"] = a
        args.append(nc.dram_tensor(f"in_{name}_dram", a.shape, _mybir.dt.from_np(a.dtype), kind="ExternalInput").ap())
    o = nc.dram_tensor("out_0_dram", (N, D), F32, kind="ExternalOutput").ap()
    build(nc, *args, o)
    r = _run(nc, [arrays], core_ids=[0])
    return r.results[0]["out_0_dram"]
```

```python
from contextlib import ExitStack

import concourse.bass as bass
from concourse import mybir

F32 = mybir.dt.float32
BF16 = mybir.dt.bfloat16
I32 = mybir.dt.int32
U16 = mybir.dt.uint16
ALU = mybir.AluOpType
ACT = mybir.ActivationFunctionType
AX = mybir.AxisListType.X

P = 128
N, D = 4096, 128
T = N // P
HEADS, HD = 4, 32
LN_EPS = 1e-5
SLOPE = 0.2
SLOTS = 64
PART = 32
SEG = 64
NSEG = N // SEG
BAD_OVER = 0
MASKED = -1e30


class Count:

    def __init__(self, base):
        self.base, self.n = base, 0

    def inc(self):
        self.n += 1
        return 1

    def now(self):
        return self.base + self.n


def build(nc, x_in, adj, W_l, W_r, W_v, a0, ln_g, ln_b, W1, b1, W2, a2, out, upto=4):
    KV = 2 * D + HEADS
    kv_dram = nc.dram_tensor("kv_rows", [N, KV], F32, kind="Internal").ap()
    flag_dram = nc.dram_tensor("flag_rows", [2, P], F32, kind="Internal").ap()
    with ExitStack() as ctx:
        def sem(name):
            return ctx.enter_context(nc.semaphore(name))

        def sb(name, shape, dt=F32, where=ctx):
            return where.enter_context(nc.sbuf_tensor(name, shape, dt))

        def ps(name, shape, dt=F32, where=ctx):
            return where.enter_context(nc.psum_tensor(name, shape, dt))

        xs = sb("xs", [P, T, D])
        rows = sb("rows", [P, T, D])
        cols = sb("cols", [P, N])
        ident = sb("ident", [P, P])
        ones = sb("ones", [P, P])
        hrow = [sb(f"hrow{i}", [P, D]) for i in range(2)]
        hcol = [sb(f"hcol{i}", [P, P]) for i in range(2)]
        bst = sb("bst", [P, T, 6])
        mv = sb("mv", [P, T, 2])
        std = sb("std", [P, T])
        rstd = sb("rstd", [P, T])
        nmr = sb("nmr", [P, T])
        flags = sb("flags", [P, 2], I32)
        top0 = sb("top0", [P, T])
        nan = sb("nan", [P, T])
        wlrv = sb("wlrv", [P, 3 * D])
        arow = sb("arow", [P, D])
        grow = sb("grow", [P, D])
        brow = sb("brow", [P, D])

        x_loaded, w_loaded, consts = sem("x_loaded"), sem("w_loaded"), sem("consts")
        waited = sem("waited")
        block_sems = {}

        def layer_sems(n, names):
            block_sems[n] = {k: sem(f"L{n}_{k}") for k in names.split()}
            return block_sems[n]

        prep_sems = [layer_sems(f"{n}prep", "own var stats hrow_ready hT_ready hcol_ready w_ready w_out"
                                + " lin arow" * (n == 0)) for n in range(4)]
        layer_done = [sem(f"layer_done{n}") for n in range(4)]
        s = layer_sems(0, "adj_in0 adj_in1 adj_free squared own lists kl_sum kl_act kl_used "
                          "flag_own flag_rows flag_sum e_ready p_ready v_scaled sums_read flags_out flags "
                          "kvs_stored0 kvs_stored1")
        kvs_stored = [s["kvs_stored0"], s["kvs_stored1"]]
        adj_in = [s["adj_in0"], s["adj_in1"]]
        gathered = [[sem(f"L0_gathered{q}{g}") for g in range(4)] for q in range(2)]
        summed = [sem(f"L0_summed{g}") for g in range(4)]

        z0 = ExitStack()
        ga = [sb(f"gathered_part{q}", [P, PART, KV], F32, z0) for q in range(2)]
        kl = sb("kl", [P, PART, D], F32, z0)
        adjt = [sb(f"adj_tile{i}", [P, N], I32, z0) for i in range(2)]
        key = sb("key", [P, N], U16, z0)
        iota = sb("iota", [P, N], U16, z0)
        cand = sb("cand", [P, NSEG * 8], F32, z0)
        top = sb("top", [P, SLOTS], F32, z0)
        idx = [sb(f"idx{i}", [P, SLOTS], I32, z0) for i in range(2)]
        mb = [sb(f"slot_mask{i}", [P, SLOTS], F32, z0) for i in range(2)]
        E = sb("E", [P, PART, HEADS], F32, z0)
        Pr = sb("Pr", [P, PART, HEADS], F32, z0)
        mx = [[sb(f"mx{p}{q}", [P, HEADS], F32, z0) for q in range(2)] for p in range(2)]
        cm = sb("cm", [P, HEADS], F32, z0)
        dm = [sb(f"dm{p}", [P, HEADS], F32, z0) for p in range(2)]
        sc = [sb(f"sc{p}", [P, HEADS], F32, z0) for p in range(2)]
        sm = [[sb(f"sm{p}{q}", [P, HEADS], F32, z0) for q in range(2)] for p in range(2)]
        o0 = sb("o0", [P, D], F32, z0)
        o1 = sb("o1", [P, D], F32, z0)
        den = sb("den", [P, HEADS], F32, z0)
        ksum = sb("ksum", [P, T], F32, z0)
        tsum = sb("tsum", [P, T], F32, z0)
        sq = sb("sq", [P, T], F32, z0)
        kvs = [sb(f"kvs{i}", [P, KV], F32, z0) for i in range(2)]
        lin = sb("lin", [P, 2, D], F32, z0)
        li = sb("li", [P, T, HEADS], F32, z0)
        sqj = sb("sqj", [P, N], BF16, z0)
        mhalf = sb("mhalf", [P, 1], F32, z0)
        odd = sb("odd", [P, 3, T], F32, z0)
        fl = sb("fl", [P, 3], F32, z0)
        on = sb("on", [P, PART], F32, z0)
        off = sb("off", [P, PART], F32, z0)
        z0.close()

        pT_ring = sb("pT_ring", [P, 4 * 512])
        z1 = ExitStack()
        adj1 = [sb(f"adj1_{i}", [P, N], I32, z1) for i in range(2)]
        mask1 = [sb(f"mask1_{i}", [P, N], BF16, z1) for i in range(2)]
        Z1 = [sb(f"Z1_{i}", [P, N], F32, z1) for i in range(2)]
        P1 = [sb(f"P1_{i}", [P, N], F32, z1) for i in range(2)]
        hs = [sb(f"hs{i}", [P, P], F32, z1) for i in range(2)]
        w1c = sb("w1c", [P, 4], F32, z1)
        b1c = sb("b1c", [P, 4], F32, z1)
        zm = [sb(f"zm{i}", [P, 1], F32, z1) for i in range(2)]
        nm = [sb(f"nm{i}", [P, 1], F32, z1) for i in range(2)]
        rs = [sb(f"rs{i}", [P, 1], F32, z1) for i in range(2)]
        ri = sb("ri", [P, 1], F32, z1)
        z1.close()
        z2 = ExitStack()
        adj2 = sb("adj2", [P, N], I32, z2)
        mask2 = sb("mask2", [P, N], BF16, z2)
        Z2 = [sb(f"Z2_{i}", [P, N], F32, z2) for i in range(2)]
        P2b = sb("P2b", [P, N], F32, z2)
        dbc = sb("dbc", [P, HEADS, N], F32, z2)
        w2s = sb("w2s", [P, D + HEADS], F32, z2)
        asd = sb("asd", [P, HEADS, 2, HD], F32, z2)
        wa = sb("wa", [P, D], F32, z2)
        wd = sb("wd", [P, HEADS], F32, z2)
        wrep = sb("wrep", [P, HEADS, P], F32, z2)
        si = sb("si", [P, T, HEADS], F32, z2)
        zm2 = [sb(f"zm2_{i}", [P, 1], F32, z2) for i in range(2)]
        nm2 = [sb(f"nm2_{i}", [P, 1], F32, z2) for i in range(2)]
        rs2 = [sb(f"rs2_{i}", [P, HEADS], F32, z2) for i in range(2)]
        ri2 = sb("ri2", [P, HEADS], F32, z2)
        z2.close()

        pz = ExitStack()
        pS = [ps(f"pS{i}", [P, 512], F32, pz) for i in range(2)]
        pX = [ps(f"pX{i}", [P, 512], F32, pz) for i in range(4)]
        pO = [ps(f"pO{i}", [P, 512], F32, pz) for i in range(2)]
        pz.close()
        pz = ExitStack()
        pT = [ps(f"prep_T{i}", [P, P], F32, pz) for i in range(2)]
        pW = [ps(f"prep_W{i}", [P, 3 * D], F32, pz) for i in range(2)]
        pz.close()
        pz = ExitStack()
        pK = [ps(f"pK{i}", [P, 8, D], F32, pz) for i in range(2)]
        pA = [ps(f"pA{i}", [P, 4, D], F32, pz) for i in range(2)]
        pz.close()

        adj_v = adj.rearrange("(t p) j -> t p j", p=P)

        def adj_tile(t):
            return adj_v[t, :, :] if isinstance(t, int) else adj_v[bass.ds(t, 1), :, :].rearrange("a p j -> (a p) j")

        block = ctx.enter_context(nc.Block())

        def row_stats_vector(v, src, q):
            with v.Fori(0, T) as t:
                v.bn_stats(bst[:, t, :], src[:, t, :]).then_inc(q["own"], 1)
            v.wait_ge(q["own"], T)
            for t in range(T):
                v.bn_aggr(mv[:, t, :], bst[:, t, :]).then_inc(q["own"], 1)
            v.wait_ge(q["own"], 2 * T)
            v.tensor_scalar(std[:, :], mv[:, :, 1], LN_EPS, None, ALU.add).then_inc(q["var"], 1)
            v.wait_ge(q["var"], 2)
            v.reciprocal(rstd[:, :], std[:, :]).then_inc(q["own"], 1)
            v.wait_ge(q["own"], 2 * T + 1)
            v.scalar_tensor_tensor(nmr[:, :], mv[:, :, 0], -1.0, rstd[:, :], ALU.mult, ALU.mult)\
             .then_inc(q["stats"], 1)

        def root_scalar(a, q):
            a.wait_ge(q["var"], 1)
            a.activation(std[:, :], std[:, :], ACT.Sqrt).then_inc(q["var"], 1)

        def prep_vector(v, n):
            q = prep_sems[n]

            def weights(u, p):
                t = 2 * u + p
                v.wait_ge(q["w_ready"], t + 1)
                if n == 2:
                    v.tensor_copy(rows[:, t, :], pW[p][:, 0:D])
                    v.tensor_copy(si[:, t, :], pW[p][:, D:D + HEADS]).then_inc(q["w_out"], 1)
                if n == 0:
                    if not isinstance(u, int):
                        v.wait_ge(kvs_stored[p], 16 * u)
                    v.tensor_copy(cols[:, bass.ts(t, D)], pW[p][:, 0:D])
                    v.tensor_copy(kvs[p][:, 0:2 * D], pW[p][:, D:3 * D])
                    v.wait_ge(q["lin"], 2 * t)
                    v.tensor_tensor(lin[:, :, :], pW[p][:, 0:2 * D].rearrange("p (a d) -> p a d", a=2),
                                    arow[:, :].unsqueeze(1).to_broadcast([P, 2, D]), ALU.mult).then_inc(q["lin"], 1)
                    v.wait_ge(q["lin"], 2 * t + 1)
                    v.tensor_reduce(li[:, t, :], lin[:, 0, :].rearrange("p (h d) -> p h d", h=HEADS), AX, ALU.add)
                    v.tensor_reduce(kvs[p][:, 2 * D:KV], lin[:, 1, :].rearrange("p (h d) -> p h d", h=HEADS),
                                    AX, ALU.add).then_inc(q["lin"], 1)
                    v.wait_ge(q["lin"], 2 * t + 2)
                    v.tensor_scalar(li[:, t, :], li[:, t, :], SLOPE / (1 - SLOPE), None, ALU.mult)
                    v.tensor_scalar(kvs[p][:, 2 * D:KV], kvs[p][:, 2 * D:KV], SLOPE / (1 - SLOPE), None, ALU.mult)\
                     .then_inc(q["w_out"], 1)

            row_stats_vector(v, xs, q)
            if n in (0, 2):
                weights(0, 0)
                weights(0, 1)
                with v.Fori(1, T // 2) as u:
                    weights(u, 0)
                    weights(u, 1)

        def prep_scalar(a, n):
            q = prep_sems[n]

            def tile(u, p):
                t = 2 * u + p
                a.wait_ge(q["hT_ready"], t)
                a.activation(hrow[p][:, :], xs[:, t, :], ACT.Relu, bias=nmr[:, bass.ds(t, 1)], scale=rstd[:, bass.ds(t, 1)])\
                 .then_inc(q["hrow_ready"], 1)
                if n in (1, 3):
                    a.wait_ge(q["hrow_ready"], t + 1)
                    a.copy(rows[:, t, :], hrow[p][:, :])

            def turned(u, p):
                t = 2 * u + p
                a.wait_ge(q["hT_ready"], t + 1)
                if n in (0, 2):
                    a.wait_ge(q["w_ready"], t)
                    a.copy(hcol[p][:, :], pT[p][:, :]).then_inc(q["hcol_ready"], 1)
                    if n == 2:
                        a.copy(cols[:, bass.ts(t, P)], pT[p][:, :])
                else:
                    a.copy(cols[:, bass.ts(t, P)], pT[p][:, :]).then_inc(q["hcol_ready"], 1)
            root_scalar(a, q)
            a.wait_ge(q["stats"], 1)
            with a.Fori(0, T // 2) as u:
                for p in range(2):
                    tile(u, p)
                    turned(u, p)

        def prep_tensor(e, n):
            q = prep_sems[n]
            with e.Fori(0, T // 2) as u:
                for p in range(2):
                    t = 2 * u + p
                    e.wait_ge(q["hrow_ready"], t + 1)
                    e.wait_ge(q["hcol_ready"], t)
                    e.transpose(pT[p][:, :], hrow[p][:, :], ident[:, :]).then_inc(q["hT_ready"], 1)
                    if n in (0, 2):
                        w = wlrv[:, :] if n == 0 else w2s[:, :]
                        e.wait_ge(q["hcol_ready"], t + 1)
                        e.wait_ge(q["w_out"], t)
                        e.matmul(pW[p][:, 0:3 * D if n == 0 else D + HEADS], hcol[p][:, :], w, start=True, stop=True)\
                         .then_inc(q["w_ready"], 1)

        own0 = 3 + 8 * 2 + 4

        OWN_LIST = 2 + 15 + 1
        OWN_A = 5
        OWN_FIN = 8
        OWN_TILE = OWN_LIST + 2 * (OWN_A + 1) + OWN_FIN

        def settled(eng):
            eng.sem_inc(waited, 1)

        EARLY = 5 * NSEG // 8

        def list_early(v, u, p, c):
            t = 2 * u + p
            v.wait_ge(adj_in[p], 16 * (u + 1))
            v.scalar_tensor_tensor(key[:, :], adjt[p][:, :], 0.0, iota[:, :], ALU.not_equal, ALU.mult,
                                   accum_out=ksum[:, bass.ds(t, 1)]).then_inc(s["own"], c.inc())
            v.wait_ge(s["own"], c.now())
            v.sem_inc(s["adj_free"], 1)
            for g in range(EARLY):
                ins = v.max(cand[:, 8 * g:8 * g + 8], key[:, SEG * g:SEG * (g + 1)])
            ins.then_inc(s["own"], c.inc())

        def list_late(v, u, p, c):
            t = 2 * u + p
            for g in range(EARLY, NSEG):
                ins = v.max(cand[:, 8 * g:8 * g + 8], key[:, SEG * g:SEG * (g + 1)])
            ins.then_inc(s["own"], c.inc())
            for r in range(SLOTS // 8):
                v.wait_ge(s["own"], c.now())
                settled(v)
                v.max(top[:, 8 * r:8 * r + 8], cand[:, :]).then_inc(s["own"], c.inc())
                if r < SLOTS // 8 - 1:
                    v.wait_ge(s["own"], c.now())
                    settled(v)
                    v.match_replace(cand[:, :], top[:, 8 * r:8 * r + 8], cand[:, :], 0.0)\
                     .then_inc(s["own"], c.inc())
            v.wait_ge(s["own"], c.now())
            if u_ge1(u):
                for q, g in [(q, g) for q in range(2) for g in range(4)]:
                    v.wait_ge(gathered[q][g], 16 * 8 * (t - 1))
            v.tensor_scalar(idx[p][:, :], top[:, :], -1.0, float(N), ALU.mult, ALU.add)
            v.tensor_scalar(mb[p][:, :], top[:, :], 0.0, MASKED, ALU.is_equal, ALU.mult)
            v.tensor_copy(top0[:, bass.ds(t, 1)], top[:, 0:1])
            v.tensor_reduce(tsum[:, bass.ds(t, 1)], top[:, :], AX, ALU.add).then_inc(s["lists"], 1)

        def u_ge1(u):
            return not (isinstance(u, int) and u == 0)

        def bc(ap, shape):
            return ap.to_broadcast(shape)

        def a_vector(v, u, p, q, c):
            t = 2 * u + p
            seq = 2 * t + q
            v.wait_ge(s["kl_act"], 4 * (seq + 1))
            v.tensor_tensor(kl[:, :, :], kl[:, :, :], arow[:, :].unsqueeze(1).to_broadcast([P, PART, D]), ALU.mult)\
             .then_inc(s["own"], c.inc())
            v.wait_ge(s["own"], c.now())
            v.tensor_reduce(E[:, :, :], kl[:, :, :].rearrange("p s (h d) -> p s h d", h=HEADS), AX, ALU.add)\
             .then_inc(s["kl_used"], 1)
            v.wait_ge(s["kl_used"], seq + 1)
            v.wait_ge(s["lists"], t + 1)
            v.tensor_tensor(E[:, :, :], E[:, :, :], ga[q][:, :, 2 * D:KV], ALU.add).then_inc(s["own"], c.inc())
            v.wait_ge(s["own"], c.now())
            v.tensor_tensor(E[:, :, :], E[:, :, :], li[:, t, :].unsqueeze(1).to_broadcast([P, PART, HEADS]), ALU.add)\
             .then_inc(s["own"], c.inc())
            v.wait_ge(s["own"], c.now())
            v.tensor_tensor(E[:, :, :], E[:, :, :],
                            mb[p][:, q * PART:(q + 1) * PART].unsqueeze(2).to_broadcast([P, PART, HEADS]), ALU.add)\
             .then_inc(s["own"], c.inc())
            v.wait_ge(s["own"], c.now())
            m_out = mx[p][0] if q == 0 else cm
            v.tensor_reduce(m_out[:, :], E[:, :, :].rearrange("p s h -> p h s"), AX, ALU.max)\
             .then_inc(s["own"], c.inc())
            v.wait_ge(s["own"], c.now())
            if q == 1:
                v.tensor_tensor(mx[p][1][:, :], mx[p][0][:, :], cm[:, :], ALU.max).then_inc(s["own"], c.inc())
                v.wait_ge(s["own"], c.now())
                v.tensor_tensor(dm[p][:, :], mx[p][0][:, :], mx[p][1][:, :], ALU.subtract)
            v.tensor_tensor(E[:, :, :], E[:, :, :], mx[p][q][:, :].unsqueeze(1).to_broadcast([P, PART, HEADS]),
                            ALU.subtract).then_inc(s["e_ready"], 1)

        def b_vector(v, u, p, q):
            t = 2 * u + p
            seq = 2 * t + q
            v.wait_ge(s["p_ready"], seq + 1)
            for g in range(4):
                V = ga[q][:, 8 * g:8 * g + 8, D:2 * D].rearrange("p s (h d) -> p s h d", h=HEADS)
                v.tensor_tensor(V, V, Pr[:, 8 * g:8 * g + 8, :].unsqueeze(3).to_broadcast([P, 8, HEADS, HD]),
                                ALU.mult).then_inc(s["v_scaled"], 1)
            v.tensor_reduce(sm[p][q][:, :], Pr[:, :, :].rearrange("p s h -> p h s"), AX, ALU.add)\
             .then_inc(s["own_b"], 1)

        def fin_vector(v, u, p, c):
            t = 2 * u + p
            v.wait_ge(s["own_b"], 2 * (t + 1))
            v.wait_ge(s["p_scale"], t + 1)
            v.wait_ge(summed[3], 2 * (t + 1) + 1)
            v.tensor_reduce(o0[:, :], pA[0][:, :, :].rearrange("p k d -> p d k"), AX, ALU.add)
            v.tensor_reduce(o1[:, :], pA[1][:, :, :].rearrange("p k d -> p d k"), AX, ALU.add)\
             .then_inc(s["sums_read"], 1)
            v.tensor_tensor(den[:, :], sm[p][0][:, :], sc[p][:, :], ALU.mult).then_inc(s["own"], c.inc())
            v.wait_ge(s["sums_read"], t + 1)
            o0h = o0[:, :].rearrange("p (h d) -> p h d", h=HEADS)
            v.tensor_tensor(o0h, o0h, sc[p][:, :].unsqueeze(2).to_broadcast([P, HEADS, HD]), ALU.mult)\
             .then_inc(s["own"], c.inc())
            v.wait_ge(s["own"], c.now())
            v.tensor_tensor(den[:, :], den[:, :], sm[p][1][:, :], ALU.add).then_inc(s["own"], c.inc())
            v.tensor_tensor(o0[:, :], o0[:, :], o1[:, :], ALU.add).then_inc(s["own"], c.inc())
            v.wait_ge(s["own"], c.now())
            v.reciprocal(den[:, :], den[:, :]).then_inc(s["own"], c.inc())
            v.wait_ge(s["own"], c.now())
            v.tensor_tensor(rows[:, t, :].rearrange("p (h d) -> p h d", h=HEADS), o0h,
                            den[:, :].unsqueeze(2).to_broadcast([P, HEADS, HD]), ALU.mult).then_inc(s["own"], c.inc())

        s["own_b"] = sem("L0_own_b")
        NL_EARLY, NL_LATE, NA0, NA1, NF = 2, 16, 5, 6, 6
        NL = NL_EARLY + NL_LATE
        NB = NL + NA0 + NA1 + NF

        def l0_vector(v):
            for p in range(2):
                v.wait_ge(consts, 4)
            for p in range(2):
                c = Count(NL * p)
                list_early(v, 0, p, c)
                list_late(v, 0, p, c)

            def tile(u, p, first=False, last=False):
                t = 2 * u + p
                c = Count(2 * NL + NB * t)
                up, pp = (u, 0) if p == 1 else (u - 1, 1)
                a_vector(v, u, p, 0, c)
                if not last:
                    list_early(v, u + 1, p, c)
                else:
                    c.n += NL_EARLY
                    v.sem_inc(s["own"], NL_EARLY)
                b_vector(v, u, p, 0)
                if not first:
                    fin_vector(v, up, pp, c)
                else:
                    c.n += NF
                    v.sem_inc(s["own"], NF)
                a_vector(v, u, p, 1, c)
                if not last:
                    list_late(v, u + 1, p, c)
                else:
                    c.n += NL_LATE
                    v.sem_inc(s["own"], NL_LATE)
                b_vector(v, u, p, 1)
                assert c.n == NB, c.n
            tile(0, 0, first=True)
            tile(0, 1)
            with v.Fori(1, T // 2 - 1) as u:
                tile(u, 0)
                tile(u, 1)
            tile(T // 2 - 1, 0, last=True)
            tile(T // 2 - 1, 1, last=True)
            c = Count(2 * NL + NB * T)
            fin_vector(v, T // 2 - 1, 1, c)
            v.wait_ge(s["own"], c.now())

        def l0_scalar(a):
            a.wait_ge(consts, 4)

            def square(u, p):
                t = 2 * u + p
                a.wait_ge(adj_in[p], 16 * (u + 1))
                a.wait_ge(s["squared"], t)
                a.activation(sqj[:, :], adjt[p][:, :], ACT.Square, bias=mhalf[:, 0:1],
                             accum_out=sq[:, bass.ds(t, 1)]).then_inc(s["squared"], 1)

            def relu(seq, g):
                a.wait_ge(s["kl_sum"], 4 * seq + g + 1)
                a.activation(kl[:, 8 * g:8 * g + 8, :], pK[g % 2][:, :, :], ACT.Relu).then_inc(s["kl_act"], 1)

            def tile(u, p, last=False):
                t = 2 * u + p
                for q in range(2):
                    seq = 2 * t + q
                    end = last and p == 1 and q == 1
                    if not end:
                        a.wait_ge(s["kl_used"], seq + 1)
                        relu(seq + 1, 0)
                    a.wait_ge(s["e_ready"], seq + 1)
                    a.activation(Pr[:, :, :], E[:, :, :], ACT.Exp).then_inc(s["p_ready"], 1)
                    if q == 1:
                        a.activation(sc[p][:, :], dm[p][:, :], ACT.Exp).then_inc(s["p_scale"], 1)
                    if not end:
                        relu(seq + 1, 1)
                    if q == 0 and not last:
                        square(u + 1, p)
                    if not end:
                        relu(seq + 1, 2)
                        relu(seq + 1, 3)
            square(0, 0)
            square(0, 1)
            for g in range(4):
                relu(0, g)
            with a.Fori(0, T // 2 - 1) as u:
                tile(u, 0)
                tile(u, 1)
            tile(T // 2 - 1, 0, last=True)
            tile(T // 2 - 1, 1, last=True)

        s["p_scale"] = sem("L0_p_scale")

        def l0_tensor(e):
            def sums(t, q, groups):
                seq = 2 * t + q
                wl = cols[:, bass.ts(t, D)].unsqueeze(1).to_broadcast([P, 4, D])
                for g in groups:
                    e.wait_ge(gathered[q][g], 16 * 8 * (t + 1))
                    if not (isinstance(t, int) and t == 0 and q == 0 and g < 2):
                        e.wait_ge(s["kl_act"], 4 * seq + g - 1)
                    for b in range(2):
                        k = 8 * g + 4 * b
                        e.matmul(pK[g % 2][:, 4 * b:4 * b + 4, :], ident[:, :], ga[q][:, k:k + 4, 0:D],
                                 start=True, stop=False)
                        ins = e.matmul(pK[g % 2][:, 4 * b:4 * b + 4, :], ident[:, :], wl, start=False, stop=True)
                    ins.then_inc(s["kl_sum"], 1)

            def total(t, q):
                e.wait_ge(s["sums_read"], t)
                for g in range(4):
                    e.wait_ge(s["v_scaled"], 4 * (2 * t + q) + g + 1)
                    for k in (2 * g, 2 * g + 1):
                        ins = e.matmul(pA[q][:, :, :], ident[:, :], ga[q][:, 4 * k:4 * k + 4, D:2 * D],
                                       start=(k == 0), stop=(k == PART // 4 - 1))
                    ins.then_inc(summed[g], 1)

            def tile(t, last=False):
                for q in range(2):
                    nxt = (t, 1) if q == 0 else None if last else (t + 1, 0)
                    if nxt:
                        sums(*nxt, range(0, 3))
                    total(t, q)
                    if nxt:
                        sums(*nxt, range(3, 4))
            for g in range(4):
                e.sem_inc(summed[g], 1)
            sums(0, 0, range(4))
            with e.Fori(0, T - 1) as t:
                tile(t)
            tile(T - 1, last=True)

        def l0_gpsimd(g):
            with g.Fori(0, T // 2) as u:
                for p in range(2):
                    t = 2 * u + p
                    g.wait_ge(s["lists"], t + 1)
                    for q, k0 in [(q, k0) for q in range(2) for k0 in range(0, PART, 8)]:
                        g.wait_ge(summed[k0 // 8], 2 * t + q)
                        settled(g)
                        for k in range(k0, k0 + 8):
                            g.indirect_dma_start(
                                out=ga[q][:, k, :], out_offset=None, in_=kv_dram[:, :],
                                in_offset=bass.IndirectOffsetOnAxis(ap=idx[p][:, q * PART + k:q * PART + k + 1], axis=0),
                                bounds_check=N - 1, oob_is_err=False).then_inc(gathered[q][k0 // 8], 16)

        def l0_sync(y):
            adj_v = adj.rearrange("(t p) j -> t p j", p=P)
            for p in range(2):
                y.dma_start(adjt[p][:, :], adj_v[p, :, :]).then_inc(adj_in[p], 16)
            with y.Fori(1, T // 2) as u:
                for p in range(2):
                    t = 2 * u + p
                    y.wait_ge(s["adj_free"], t - 1)
                    y.wait_ge(s["squared"], t - 1)
                    y.dma_start(adjt[p][:, :], adj_v[bass.ds(t, 1), :, :].rearrange("a p j -> (a p) j"))\
                     .then_inc(adj_in[p], 16)

        def flags_vector(v):
            v.wait_ge(s["squared"], T)
            v.tensor_tensor(odd[:, 0, :], ksum[:, :], tsum[:, :], ALU.not_equal)
            v.tensor_scalar(odd[:, 1, :], top0[:, :], 0.0, None, ALU.is_equal)
            v.tensor_scalar(odd[:, 2, :], sq[:, :], N / 4, None, ALU.not_equal).then_inc(s["flag_own"], 1)
            v.wait_ge(s["flag_own"], 1)
            v.tensor_reduce(fl[:, :], odd[:, :, :], AX, ALU.max).then_inc(s["flag_rows"], 1)
            v.wait_ge(s["flag_sum"], 1)
            v.tensor_copy(fl[:, 0:3], pA[1][:, 0, 0:3]).then_inc(s["flag_own"], 1)
            v.wait_ge(s["flag_own"], 2)
            v.tensor_tensor(flags[:, 0:1], fl[:, 0:1], fl[:, 1:2], ALU.add)
            v.tensor_copy(flags[:, 1:2], fl[:, 2:3]).then_inc(s["flags"], 1)

        def flags_tensor(e):
            e.wait_ge(s["flag_rows"], 1)
            e.matmul(pA[1][:, 0, 0:3], ones[:, :], fl[:, 0:3], start=True, stop=True).then_inc(s["flag_sum"], 1)

        def flag(eng, k):
            eng.wait_ge(s["flags"], 1)
            return eng.value_load(flags[0:1, k:k + 1], min_val=0, max_val=2 * N)

        d0 = layer_sems("0dense", "adj in0 in1 kl_sum kl_act own e_ready p_ready v_scaled summed done masks masks2")
        CH = N // (2 * PART)
        D_STEPS = 18

        def dense_parts(eng, tile_start, part, tile_end):
            with eng.Fori(0, T) as t:
                tile_start(t)
                with eng.Fori(0, CH) as c:
                    for q in range(2):
                        part(t, c, q, 2 * (CH * t + c) + q)
                tile_end(t)

        def dense_sync(y):
            def start(t):
                y.wait_ge(d0["done"], t)
                y.dma_start(adjt[0][:, :], adj_tile(t)).then_inc(d0["adj"], 16)

            def part(t, c, q, seq):
                y.wait_ge(d0["summed"], seq)
                src = kv_dram[bass.ds(c * (2 * PART) + q * PART, PART), :].rearrange("s d -> (s d)")
                y.dma_start(ga[q][:, :, :].rearrange("p s d -> p (s d)"),
                            src.unsqueeze(0).to_broadcast([P, PART * KV])).then_inc(d0[f"in{q}"], 16)
            dense_parts(y, start, part, lambda t: None)

        def dense_tensor(e):
            def part(t, c, q, seq):
                e.wait_ge(d0[f"in{q}"], 16 * (CH * t + c + 1))
                wl = cols[:, bass.ts(t, D)].unsqueeze(1).to_broadcast([P, 4, D])
                for g in range(4):
                    e.wait_ge(d0["kl_act"], 4 * seq + g)
                    for b in range(2):
                        k = 8 * g + 4 * b
                        e.matmul(pK[g % 2][:, 4 * b:4 * b + 4, :], ident[:, :], ga[q][:, k:k + 4, 0:D],
                                 start=True, stop=False)
                        ins = e.matmul(pK[g % 2][:, 4 * b:4 * b + 4, :], ident[:, :], wl, start=False, stop=True)
                    ins.then_inc(d0["kl_sum"], 1)
                e.wait_ge(d0["v_scaled"], seq + 1)
                for k in range(PART // 4):
                    ins = e.matmul(pA[q][:, :, :], ident[:, :], ga[q][:, 4 * k:4 * k + 4, D:2 * D],
                                   start=(k == 0), stop=(k == PART // 4 - 1))
                ins.then_inc(d0["summed"], 1)
            dense_parts(e, lambda t: None, part, lambda t: None)

        def dense_scalar(a):
            def part(t, c, q, seq):
                for g in range(4):
                    a.wait_ge(d0["kl_sum"], 4 * seq + g + 1)
                    a.activation(kl[:, 8 * g:8 * g + 8, :], pK[g % 2][:, :, :], ACT.Relu).then_inc(d0["kl_act"], 1)
                a.wait_ge(d0["e_ready"], seq + 1)
                a.activation(Pr[:, :, :], E[:, :, :], ACT.Exp)
                a.activation(sc[0][:, :], dm[0][:, :], ACT.Exp).then_inc(d0["p_ready"], 1)
            dense_parts(a, lambda t: None, part, lambda t: None)

        def dense_vector(v):
            m, total = mx[0][0], sm[0][0]
            o0h = o0[:, :].rearrange("p (h d) -> p h d", h=HEADS)

            def start(t):
                v.memset(m[:, :], -3e38)
                v.memset(total[:, :], 0.0)
                v.memset(o0[:, :], 0.0).then_inc(d0["masks"], 1)
                v.wait_ge(d0["adj"], 16 * (t + 1))
                v.wait_ge(d0["masks"], t + 1)
                settled(v)

            def part(t, c, q, seq):
                k = Count(D_STEPS * seq)
                own = d0["own"]

                def last():
                    v.wait_ge(own, k.now())
                wide = [P, PART, HEADS]
                v.tensor_scalar(on[:, :], adjt[0][:, bass.ds(c * (2 * PART) + q * PART, PART)], 0.0, None,
                                ALU.not_equal).then_inc(own, k.inc())
                last()
                v.tensor_scalar(off[:, :], on[:, :], -1.0, 1e9, ALU.add, ALU.mult).then_inc(own, k.inc())
                v.wait_ge(d0["kl_act"], 4 * (seq + 1))
                v.tensor_tensor(kl[:, :, :], kl[:, :, :], arow[:, :].unsqueeze(1).to_broadcast([P, PART, D]),
                                ALU.mult).then_inc(own, k.inc())
                last()
                v.tensor_reduce(E[:, :, :], kl[:, :, :].rearrange("p s (h d) -> p s h d", h=HEADS), AX, ALU.add)\
                 .then_inc(own, k.inc())
                for other, op in ((ga[q][:, :, 2 * D:KV], ALU.add),
                                  (li[:, t, :].unsqueeze(1).to_broadcast(wide), ALU.add),
                                  (on[:, :].unsqueeze(2).to_broadcast(wide), ALU.mult),
                                  (off[:, :].unsqueeze(2).to_broadcast(wide), ALU.add)):
                    last()
                    v.tensor_tensor(E[:, :, :], E[:, :, :], other, op).then_inc(own, k.inc())
                last()
                v.tensor_reduce(cm[:, :], E[:, :, :].rearrange("p s h -> p h s"), AX, ALU.max).then_inc(own, k.inc())
                last()
                v.tensor_tensor(cm[:, :], cm[:, :], m[:, :], ALU.max).then_inc(own, k.inc())
                last()
                v.tensor_tensor(dm[0][:, :], m[:, :], cm[:, :], ALU.subtract).then_inc(own, k.inc())
                last()
                v.tensor_copy(m[:, :], cm[:, :])
                v.tensor_tensor(E[:, :, :], E[:, :, :], cm[:, :].unsqueeze(1).to_broadcast(wide), ALU.subtract)\
                 .then_inc(d0["e_ready"], 1)
                v.wait_ge(d0["p_ready"], seq + 1)
                V = ga[q][:, :, D:2 * D].rearrange("p s (h d) -> p s h d", h=HEADS)
                v.tensor_tensor(V, V, Pr[:, :, :].unsqueeze(3).to_broadcast([P, PART, HEADS, HD]), ALU.mult)\
                 .then_inc(d0["v_scaled"], 1)
                v.tensor_reduce(sm[0][1][:, :], Pr[:, :, :].rearrange("p s h -> p h s"), AX, ALU.add)
                v.tensor_tensor(total[:, :], total[:, :], sc[0][:, :], ALU.mult).then_inc(own, k.inc())
                last()
                v.tensor_tensor(total[:, :], total[:, :], sm[0][1][:, :], ALU.add)
                v.tensor_tensor(o0h, o0h, sc[0][:, :].unsqueeze(2).to_broadcast([P, HEADS, HD]), ALU.mult)\
                 .then_inc(own, k.inc())
                v.wait_ge(d0["summed"], seq + 1)
                v.tensor_reduce(o1[:, :], pA[q][:, :, :].rearrange("p k d -> p d k"), AX, ALU.add)\
                 .then_inc(own, k.inc())
                last()
                v.tensor_tensor(o0[:, :], o0[:, :], o1[:, :], ALU.add).then_inc(own, k.inc())
                last()
                v.sem_inc(own, D_STEPS - k.n)

            def end(t):
                v.reciprocal(den[:, :], total[:, :]).then_inc(d0["masks2"], 1)
                v.wait_ge(d0["masks2"], t + 1)
                v.tensor_tensor(rows[:, t, :].rearrange("p (h d) -> p h d", h=HEADS), o0h,
                                den[:, :].unsqueeze(2).to_broadcast([P, HEADS, HD]), ALU.mult)\
                 .then_inc(d0["done"], 1)
                v.wait_ge(d0["done"], t + 1)
            dense_parts(v, start, part, end)

        end_sems = layer_sems("0end", "own var stats tile")

        def l0_end_vector(v):
            row_stats_vector(v, rows, end_sems)
            v.wait_ge(end_sems["stats"], 1)

            def tile(u, p):
                t = 2 * u + p
                c = Count(4 * t)
                v.wait_ge(end_sems["tile"], c.now())
                v.tensor_scalar(hrow[p][:, :], rows[:, t, :], rstd[:, bass.ds(t, 1)], nmr[:, bass.ds(t, 1)],
                                ALU.mult, ALU.add).then_inc(end_sems["tile"], c.inc())
                v.wait_ge(end_sems["tile"], c.now())
                v.tensor_tensor(hrow[p][:, :], hrow[p][:, :], grow[:, :], ALU.mult).then_inc(end_sems["tile"], c.inc())
                v.wait_ge(end_sems["tile"], c.now())
                v.tensor_tensor(hrow[p][:, :], hrow[p][:, :], brow[:, :], ALU.add).then_inc(end_sems["tile"], c.inc())
                v.wait_ge(end_sems["tile"], c.now())
                v.scalar_tensor_tensor(xs[:, t, :], hrow[p][:, :], 0.0, xs[:, t, :], ALU.max, ALU.add)\
                 .then_inc(end_sems["tile"], c.inc())
            with v.Fori(0, T // 2) as u:
                tile(u, 0)
                tile(u, 1)
            v.wait_ge(end_sems["tile"], 4 * T)
            v.sem_inc(layer_done[0], 1)

        GROUPS = T // 4

        def turn(e, pbuf, g):
            for k in range(4):
                j = 4 * g + k
                ins = e.transpose(pX[g % 4][:, k * P:(k + 1) * P], pbuf[:, j * P:(j + 1) * P], ident[:, :])
            return ins

        def tail_start(e, L, pbuf):
            e.wait_ge(L["p_ready"], 1)
            for g in range(4):
                turn(e, pbuf, g).then_inc(L["turned"], 1)

        def tail_tensor(e, L, seq, pbuf, pnext, product, signals=True):
            for g in range(GROUPS):
                e.wait_ge(L["evac"], GROUPS * seq + g + 1)
                for k in range(4):
                    j = 4 * g + k
                    ins = product(j, pT_ring[:, (j % 16) * P:(j % 16 + 1) * P])
                if g == GROUPS - 1 and signals:
                    ins.then_inc(L["o_ready"], 1)
                if g + 4 < GROUPS:
                    turn(e, pbuf, g + 4).then_inc(L["turned"], 1)
                elif pnext is not None:
                    if g + 4 == GROUPS:
                        e.wait_ge(L["p_ready"], seq + 2)
                    turn(e, pnext, g + 4 - GROUPS).then_inc(L["turned"], 1)

        def tail_evac(a, L, seq, half):
            for g in range(4 * half, 4 * half + 4):
                a.wait_ge(L["turned"], GROUPS * seq + g + 1)
                at = (g % 4) * 512
                a.copy(pT_ring[:, at:at + 512], pX[g % 4][:, :]).then_inc(L["evac"], 1)

        def product_rows(e, bank):
            return lambda j, pT: e.matmul(bank[:, 0:D], pT, rows[:, j, :], start=(j == 0), stop=(j == T - 1))

        TAIL = "p_ready turned evac o_ready o_read"

        def pairs(eng, tile):
            with eng.Fori(0, T // 2 - 1) as u:
                tile(u, 0, False)
                tile(u, 1, False)
            tile(T // 2 - 1, 0, True)
            tile(T // 2 - 1, 1, True)

        def peeled_pairs(eng, tile):
            tile(0, 0, False)
            tile(0, 1, False)
            with eng.Fori(1, T // 2 - 1) as u:
                tile(u, 0, False)
                tile(u, 1, False)
            tile(T // 2 - 1, 0, True)
            tile(T // 2 - 1, 1, True)

        def below(value, least):
            return isinstance(value, int) and value < least

        L1 = layer_sems(1, TAIL + " adj0 adj1 mask w_in hs_ready s_ready z_ready zmax leaky own nmax rcp fin")
        NEG1 = -9e15

        def l1_sync(y):
            y.wait_ge(layer_done[0], 1)
            y.dma_start(w1c[:, :], W1.rearrange("k d -> d k"), allow_slow_non_contiguous=True).then_inc(L1["w_in"], 16)
            y.dma_start(b1c[:, :], b1.unsqueeze(0).to_broadcast([P, 4])).then_inc(L1["w_in"], 16)
            with y.If(flag(y, 1) > 0):
                any_sync(y)
            with y.Else():
                binary_sync(y)

        def binary_sync(y):
            for p in range(2):
                y.dma_start(adj1[p][:, :], adj_tile(p)).then_inc(L1[f"adj{p}"], 16)
            with y.Fori(1, T // 2) as u:
                for p in range(2):
                    t = 2 * u + p
                    y.wait_ge(L1["mask"], t - 1)
                    y.dma_start(adj1[p][:, :], adj_tile(t)).then_inc(L1[f"adj{p}"], 16)

        def l1_vector(v):
            def mask(u, p):
                v.wait_ge(L1[f"adj{p}"], 16 * (u + 1))
                v.tensor_scalar(mask1[p][:, :], adj1[p][:, :], 1.0, NEG1, ALU.not_equal, ALU.mult)\
                 .then_inc(L1["mask"], 1)

            def scores(u, p):
                t = 2 * u + p
                v.wait_ge(L1["z_ready"], GROUPS * (t + 1))
                v.wait_ge(L1["mask"], t + 1)
                settled(v)
                v.tensor_tensor_reduce(Z1[p][:, :], Z1[p][:, :], mask1[p][:, :], 1.0, -3e38, ALU.add, ALU.max,
                                       zm[p][:, :]).then_inc(L1["zmax"], 1)
                v.wait_ge(L1["zmax"], t + 1)
                v.scalar_tensor_tensor(Z1[p][:, :], Z1[p][:, :], SLOPE, Z1[p][:, :], ALU.mult, ALU.max)
                v.scalar_tensor_tensor(nm[p][:, :], zm[p][:, :], SLOPE, zm[p][:, :], ALU.mult, ALU.max)\
                 .then_inc(L1["own"], 1)
                v.wait_ge(L1["own"], t + 1)
                v.tensor_scalar(nm[p][:, :], nm[p][:, :], -1.0, None, ALU.mult).then_inc(L1["leaky"], 1)

            def finish(u, p):
                t = 2 * u + p
                v.wait_ge(L1["p_ready"], t + 1)
                v.wait_ge(L1["o_read"], t)
                v.reciprocal(ri[:, :], rs[p][:, :]).then_inc(L1["rcp"], 1)
                v.wait_ge(L1["rcp"], t + 1)
                v.wait_ge(L1["o_ready"], t + 1)
                v.scalar_tensor_tensor(xs[:, t, :], pO[p][:, 0:D], ri[:, 0:1], xs[:, t, :], ALU.mult, ALU.add)\
                 .then_inc(L1["o_read"], 1)

            def tile(u, p, last):
                t = 2 * u + p
                if not (last and p == 1):
                    scores(u + p, 1 - p)
                if not last:
                    mask(u + 1, p)
                finish(u, p)
            mask(0, 0)
            mask(0, 1)
            scores(0, 0)
            pairs(v, tile)
            v.wait_ge(L1["o_read"], T)
            v.sem_inc(layer_done[1], 1)

        def l1_scalar(a):
            def lhs(u, p):
                t = 2 * u + p
                if not (isinstance(u, int) and u == 0):
                    a.wait_ge(L1["s_ready"], GROUPS * (t - 1))
                a.activation(hs[p][:, :], cols[:, bass.ts(t, P)], ACT.Copy, scale=w1c[:, 0:1])\
                 .then_inc(L1["hs_ready"], 1)

            def evac_scores(u, p):
                t = 2 * u + p
                if not (isinstance(u, int) and u == 0):
                    a.wait_ge(L1["p_ready"], t - 1)
                for c in range(GROUPS):
                    a.wait_ge(L1["s_ready"], GROUPS * t + c + 1)
                    a.activation(Z1[p][:, c * 512:(c + 1) * 512], pS[c % 2][:, :], ACT.Identity, bias=b1c[:, 0:1])\
                     .then_inc(L1["z_ready"], 1)

            def exps(u, p):
                t = 2 * u + p
                a.wait_ge(L1["leaky"], t + 1)
                if not (isinstance(u, int) and u == 0):
                    a.wait_ge(L1["turned"], GROUPS * (t - 1))
                    a.wait_ge(L1["rcp"], t - 1)
                a.activation(P1[p][:, :], Z1[p][:, :], ACT.Exp, bias=nm[p][:, 0:1], accum_out=rs[p][:, 0:1])\
                 .then_inc(L1["p_ready"], 1)

            def tile(u, p, last):
                t = 2 * u + p
                tail_evac(a, L1, t, 0)
                if not last:
                    lhs(u + 1, p)
                    evac_scores(u + 1, p)
                if not (last and p == 1):
                    exps(u + p, 1 - p)
                tail_evac(a, L1, t, 1)
            for p in range(2):
                lhs(0, p)
                evac_scores(0, p)
            exps(0, 0)
            pairs(a, tile)

        def l1_tensor(e):
            def scores(u, p):
                t = 2 * u + p
                e.wait_ge(L1["hs_ready"], t + 1)
                for c in range(GROUPS):
                    if not (isinstance(t, int) and t == 0 and c < 2):
                        e.wait_ge(L1["z_ready"], GROUPS * t + c - 1)
                    e.matmul(pS[c % 2][:, :], hs[p][:, :], cols[:, c * 512:(c + 1) * 512], start=True, stop=True)\
                     .then_inc(L1["s_ready"], 1)

            def tile(u, p, last):
                if not last:
                    scores(u + 1, p)
                e.wait_ge(L1["o_read"], 2 * u + p)
                tail_tensor(e, L1, 2 * u + p, P1[p], None if last and p else P1[1 - p], product_rows(e, pO[p]))
            scores(0, 0)
            scores(0, 1)
            tail_start(e, L1, P1[0])
            pairs(e, tile)

        G1 = layer_sems("1any", TAIL + " adj hs_ready s_ready z_ready used sum own done")
        G1_STEPS = 14

        def any_sync(y):
            with y.Fori(0, T) as t:
                y.wait_ge(G1["o_read"], t)
                y.dma_start(adj1[0][:, :], adj_tile(t)).then_inc(G1["adj"], 16)

        def any_tensor(e):
            with e.Fori(0, T) as t:
                for k in range(4):
                    e.wait_ge(G1["hs_ready"], 4 * t + k + 1)
                    for c in range(GROUPS):
                        if k or c >= 2:
                            e.wait_ge(G1["z_ready"], GROUPS * (4 * t + k) + c - 1)
                        e.matmul(pS[c % 2][:, :], hs[0][:, :], cols[:, c * 512:(c + 1) * 512], start=True, stop=True)\
                         .then_inc(G1["s_ready"], 1)
                e.wait_ge(G1["p_ready"], t + 1)
                for g in range(4):
                    turn(e, P1[0], g).then_inc(G1["turned"], 1)
                e.wait_ge(G1["o_read"], t)
                tail_tensor(e, G1, t, P1[0], None, product_rows(e, pO[0]))

        def any_scalar(a):
            with a.Fori(0, T) as t:
                for k in range(4):
                    a.wait_ge(G1["s_ready"], GROUPS * (4 * t + k))
                    settled(a)
                    a.activation(hs[0][:, :], cols[:, bass.ts(t, P)], ACT.Copy, scale=w1c[:, k:k + 1])\
                     .then_inc(G1["hs_ready"], 1)
                    a.wait_ge(G1["used"], 4 * t + k)
                    for c in range(GROUPS):
                        a.wait_ge(G1["s_ready"], GROUPS * (4 * t + k) + c + 1)
                        a.activation(Z1[0][:, c * 512:(c + 1) * 512], pS[c % 2][:, :], ACT.Identity,
                                     bias=b1c[:, k:k + 1]).then_inc(G1["z_ready"], 1)
                a.wait_ge(G1["sum"], t + 1)
                a.activation(P1[0][:, :], Z1[1][:, :], ACT.Exp, accum_out=rs[0][:, 0:1]).then_inc(G1["p_ready"], 1)
                tail_evac(a, G1, t, 0)
                tail_evac(a, G1, t, 1)

        def any_vector(v):
            alpha, tmp, own = Z1[1], P1[1], G1["own"]
            with v.Fori(0, T) as t:
                k = Count(G1_STEPS * t)
                v.wait_ge(G1["adj"], 16 * (t + 1))
                v.tensor_scalar(alpha[:, :], adj1[0][:, :], 1.0, None, ALU.is_ge)
                v.tensor_scalar(tmp[:, :], adj1[0][:, :], 4.0, None, ALU.is_le).then_inc(own, k.inc())
                v.wait_ge(own, k.now())
                v.tensor_tensor(alpha[:, :], alpha[:, :], tmp[:, :], ALU.mult).then_inc(own, k.inc())
                v.wait_ge(own, k.now())
                v.tensor_scalar(alpha[:, :], alpha[:, :], -1.0, -NEG1, ALU.add, ALU.mult).then_inc(own, k.inc())
                for j in range(4):
                    v.wait_ge(G1["z_ready"], GROUPS * (4 * t + j + 1))
                    v.wait_ge(own, k.now())
                    v.scalar_tensor_tensor(tmp[:, :], Z1[0][:, :], SLOPE, Z1[0][:, :], ALU.mult, ALU.max)\
                     .then_inc(G1["used"], 1)
                    v.wait_ge(G1["used"], 4 * t + j + 1)
                    v.scalar_tensor_tensor(tmp[:, :], adj1[0][:, :], float(j + 1), tmp[:, :], ALU.is_equal, ALU.mult)\
                     .then_inc(own, k.inc())
                    v.wait_ge(own, k.now())
                    v.tensor_tensor(alpha[:, :], alpha[:, :], tmp[:, :], ALU.add).then_inc(own, k.inc())
                v.wait_ge(own, k.now())
                v.tensor_reduce(zm[0][:, :], alpha[:, :], AX, ALU.max).then_inc(own, k.inc())
                v.wait_ge(own, k.now())
                v.tensor_scalar(alpha[:, :], alpha[:, :], zm[0][:, 0:1], None, ALU.subtract).then_inc(G1["sum"], 1)
                v.wait_ge(G1["p_ready"], t + 1)
                v.reciprocal(ri[:, :], rs[0][:, :]).then_inc(own, k.inc())
                v.wait_ge(own, k.now())
                v.wait_ge(G1["o_ready"], t + 1)
                v.scalar_tensor_tensor(xs[:, t, :], pO[0][:, 0:D], ri[:, 0:1], xs[:, t, :], ALU.mult, ALU.add)\
                 .then_inc(G1["o_read"], 1)
                v.sem_inc(own, G1_STEPS - k.n)
            v.wait_ge(G1["o_read"], T)
            v.sem_inc(layer_done[1], 1)

        L2 = layer_sems(2, TAIL + " adj mask w_in wmade d_ready d_outV d_outA z_in own zmax leaky rcp scaled "
                        "oT_in o_turned nan")
        P2 = [cols, P2b]
        oT, scaled = hcol, hrow

        def l2_sync(y):
            y.wait_ge(layer_done[1], 1)
            y.dma_start(w2s[:, 0:D], W2).then_inc(L2["w_in"], 16)
            y.dma_start(asd[:, :, :, :].rearrange("p h a f -> p (h a f)"),
                        a2.rearrange("h f -> (h f)").unsqueeze(0).to_broadcast([P, 2 * D])).then_inc(L2["w_in"], 16)
            y.dma_start(adj2[:, :], adj_tile(0)).then_inc(L2["adj"], 16)
            with y.Fori(1, T) as t:
                y.wait_ge(L2["mask"], t)
                y.dma_start(adj2[:, :], adj_tile(t)).then_inc(L2["adj"], 16)

        def l2_weights_vector(v):
            c = Count(0)
            v.wait_ge(L2["w_in"], 32)
            for side, to in ((0, w2s[:, D:D + HEADS]), (1, wd[:, :])):
                v.wait_ge(L2["wmade"], c.now())
                v.tensor_tensor(wa[:, :].rearrange("p (h f) -> p h f", h=HEADS),
                                w2s[:, 0:D].rearrange("p (h f) -> p h f", h=HEADS), asd[:, :, side, :], ALU.mult)\
                 .then_inc(L2["wmade"], c.inc())
                v.wait_ge(L2["wmade"], c.now())
                v.tensor_reduce(to, wa[:, :].rearrange("p (h f) -> p h f", h=HEADS), AX, ALU.add)\
                 .then_inc(L2["wmade"], c.inc())
            v.wait_ge(L2["wmade"], c.now())
            for h in range(HEADS):
                ins = v.tensor_scalar(wrep[:, h, :], ones[:, :], wd[:, h:h + 1], None, ALU.mult)
            ins.then_inc(L2["wmade"], c.inc())

        def l2_vector(v):
            for k in range(HEADS * GROUPS):
                if k % 2 == 0:
                    v.wait_ge(L2["d_ready"], k + 1)
                    v.tensor_copy(dbc[:, k // GROUPS, (k % GROUPS) * 512:(k % GROUPS + 1) * 512], pX[k % 4][:, :])\
                     .then_inc(L2["d_outV"], 1)

            def mask(t):
                v.wait_ge(L2["adj"], 16 * (t + 1))
                v.tensor_scalar(mask2[:, :], adj2[:, :], 0.0, MASKED, ALU.is_equal, ALU.mult)\
                 .then_inc(L2["mask"], 1)

            def leaky(t, h):
                seq, p = HEADS * t + h, h % 2
                v.wait_ge(L2["z_in"], seq + 1)
                v.scalar_tensor_tensor(Z2[p][:, :], Z2[p][:, :], SLOPE, Z2[p][:, :], ALU.mult, ALU.max)\
                 .then_inc(L2["own"], 1)

            def masked(t, h):
                seq, p = HEADS * t + h, h % 2
                if h == 0:
                    v.wait_ge(L2["mask"], t + 1)
                v.wait_ge(L2["own"], seq + 1)
                settled(v)
                v.tensor_tensor_reduce(Z2[p][:, :], Z2[p][:, :], mask2[:, :], 1.0, -3e38, ALU.add, ALU.max,
                                       zm2[p][:, :]).then_inc(L2["zmax"], 1)
                v.wait_ge(L2["zmax"], seq + 1)
                v.tensor_scalar(nm2[p][:, :], zm2[p][:, :], -1.0, None, ALU.mult).then_inc(L2["leaky"], 1)

            def finish(t, p):
                v.wait_ge(L2["p_ready"], HEADS * (t + 1))
                v.wait_ge(L2["o_read"], t)
                v.reciprocal(ri2[:, :], rs2[p][:, :]).then_inc(L2["rcp"], 1)
                v.wait_ge(L2["rcp"], t + 1)
                v.wait_ge(L2["o_turned"], t + 1)
                v.tensor_tensor(scaled[p][:, :].rearrange("p (h f) -> p h f", h=HEADS),
                                pS[p][:, 0:D].rearrange("p (h f) -> p h f", h=HEADS),
                                ri2[:, :].unsqueeze(2).to_broadcast([P, HEADS, HD]), ALU.mult)\
                 .then_inc(L2["scaled"], 1)
                v.wait_ge(L2["scaled"], t + 1)
                v.tensor_tensor(xs[:, t, :], scaled[p][:, :], xs[:, t, :], ALU.add).then_inc(L2["o_read"], 1)

            def tile(u, p, last):
                t = 2 * u + p
                last = last and p == 1
                for h in range(HEADS):
                    nxt = (t, h + 2) if h < HEADS - 2 else None if last else (t + 1, h - 2)
                    if h == HEADS - 2 and not last:
                        mask(t + 1)
                    if nxt:
                        leaky(*nxt)
                        masked(*nxt)
                    if h == 2 and not below(t, 1):
                        finish(t - 1, 1 - p)
            mask(0)
            for h in range(2):
                leaky(0, h)
                masked(0, h)
            peeled_pairs(v, tile)
            finish(T - 1, 1)
            c = Count(0)
            v.tensor_scalar(nan[:, :], top0[:, :], 0.0, 1e38, ALU.is_equal, ALU.mult).then_inc(L2["nan"], c.inc())
            v.wait_ge(L2["nan"], c.now())
            v.tensor_scalar(nan[:, :], nan[:, :], 1e38, None, ALU.mult).then_inc(L2["nan"], c.inc())
            v.wait_ge(L2["nan"], c.now())
            v.tensor_tensor(nan[:, :], nan[:, :], nan[:, :], ALU.subtract).then_inc(L2["nan"], c.inc())
            v.wait_ge(L2["nan"], c.now())
            v.wait_ge(L2["o_read"], T)
            v.tensor_tensor(xs[:, :, :], xs[:, :, :], nan[:, :].unsqueeze(2).to_broadcast([P, T, D]), ALU.add)\
             .then_inc(layer_done[2], 1)
            v.wait_ge(layer_done[2], 1)

        def l2_scalar(a):
            for k in range(HEADS * GROUPS):
                if k % 2 == 1:
                    a.wait_ge(L2["d_ready"], k + 1)
                    a.copy(dbc[:, k // GROUPS, (k % GROUPS) * 512:(k % GROUPS + 1) * 512], pX[k % 4][:, :])\
                     .then_inc(L2["d_outA"], 1)

            def sums(t, h):
                a.activation(Z2[h % 2][:, :], dbc[:, h, :], ACT.Identity, bias=si[:, t, h:h + 1])\
                 .then_inc(L2["z_in"], 1)

            def exps(t, h, q):
                seq, p = HEADS * t + h, h % 2
                a.wait_ge(L2["leaky"], seq + 1)
                if not below(seq, 2):
                    a.wait_ge(L2["turned"], GROUPS * (seq - 1))
                if not below(t, 2) and h == 0:
                    a.wait_ge(L2["rcp"], t - 1)
                a.activation(P2[p][:, :], Z2[p][:, :], ACT.Exp, bias=nm2[p][:, 0:1], accum_out=rs2[q][:, h:h + 1])\
                 .then_inc(L2["p_ready"], 1)

            def result(t, p):
                a.wait_ge(L2["o_ready"], t + 1)
                a.wait_ge(L2["o_turned"], t)
                a.copy(oT[p][:, :], pO[p][:, 0:P]).then_inc(L2["oT_in"], 1)

            def tile(u, p, last):
                t = 2 * u + p
                last = last and p == 1
                for h in range(HEADS):
                    tail_evac(a, L2, HEADS * t + h, 0)
                    if h == 0 and not below(t, 1):
                        result(t - 1, 1 - p)
                    if h < HEADS - 1:
                        exps(t, h + 1, p)
                    elif not last:
                        exps(t + 1, 0, 1 - p)
                    tail_evac(a, L2, HEADS * t + h, 1)
                    if not (last and h > 0):
                        a.wait_ge(L2["p_ready"], HEADS * t + h + 2)
                        sums(*((t, h + 3) if h < 1 else (t + 1, h - 1)))
            a.wait_ge(L2["d_outV"], HEADS * GROUPS // 2)
            a.wait_ge(L2["d_outA"], HEADS * GROUPS // 2)
            a.wait_ge(prep_sems[2]["w_out"], T)
            sums(0, 0)
            sums(0, 1)
            exps(0, 0, 0)
            a.wait_ge(L2["p_ready"], 1)
            sums(0, 2)
            peeled_pairs(a, tile)
            result(T - 1, 1)

        def l2_tensor(e):
            e.wait_ge(prep_sems[2]["w_out"], T)
            for k in range(HEADS * GROUPS):
                if k >= 4:
                    e.wait_ge(L2["d_outA" if k % 2 else "d_outV"], (k - 4) // 2 + 1)
                e.matmul(pX[k % 4][:, :], wrep[:, k // GROUPS, :], cols[:, (k % GROUPS) * 512:(k % GROUPS + 1) * 512],
                         start=True, stop=True).then_inc(L2["d_ready"], 1)

            def turn_result(t, p):
                e.wait_ge(L2["oT_in"], t + 1)
                e.wait_ge(L2["o_read"], t)
                e.transpose(pS[p][:, 0:P], oT[p][:, :], ident[:, :]).then_inc(L2["o_turned"], 1)

            def tile(u, p, last):
                t = 2 * u + p
                last = last and p == 1
                if not below(t, 2):
                    e.wait_ge(L2["oT_in"], t - 1)
                for h in range(HEADS):
                    if h == 1 and not below(t, 1):
                        turn_result(t - 1, 1 - p)
                    f = slice(h * HD, (h + 1) * HD)
                    tail_tensor(e, L2, HEADS * t + h, P2[h % 2], None if last and h == HEADS - 1 else P2[1 - h % 2],
                                lambda j, pT: e.matmul(pO[p][f, 0:P], rows[:, j, f], pT, start=(j == 0),
                                                       stop=(j == T - 1)), h == HEADS - 1)
            tail_start(e, L2, P2[0])
            peeled_pairs(e, tile)
            turn_result(T - 1, 1)

        L3 = layer_sems(3, TAIL + " adj0 adj1 own")

        def l3_sync(y):
            y.wait_ge(layer_done[2], 1)
            for p in range(2):
                y.dma_start(adj1[p][:, :], adj_tile(p)).then_inc(L3[f"adj{p}"], 16)
            with y.Fori(1, T // 2) as u:
                for p in range(2):
                    t = 2 * u + p
                    y.wait_ge(L3["p_ready"], t - 1)
                    y.dma_start(adj1[p][:, :], adj_tile(t)).then_inc(L3[f"adj{p}"], 16)

        def l3_vector(v):
            def cast(u, p):
                t = 2 * u + p
                v.wait_ge(L3[f"adj{p}"], 16 * (u + 1))
                if not (isinstance(u, int) and u == 0):
                    v.wait_ge(L3["turned"], GROUPS * (t - 1))
                v.tensor_copy(P1[p][:, :], adj1[p][:, :]).then_inc(L3["p_ready"], 1)

            def tile(u, p, last):
                t = 2 * u + p
                if not (last and p == 1):
                    cast(u + p, 1 - p)
                v.tensor_tensor(xs[:, t, :], xs[:, t, :], rows[:, t, :], ALU.add).then_inc(L3["own"], 1)
                v.wait_ge(L3["own"], t + 1)
                v.wait_ge(L3["o_ready"], t + 1)
                v.tensor_tensor(xs[:, t, :], pO[p][:, 0:D], xs[:, t, :], ALU.add).then_inc(L3["o_read"], 1)
            v.wait_ge(prep_sems[3]["hcol_ready"], T)
            cast(0, 0)
            pairs(v, tile)

        def l3_scalar(a):
            def tile(u, p, last):
                tail_evac(a, L3, 2 * u + p, 0)
                tail_evac(a, L3, 2 * u + p, 1)
            pairs(a, tile)

        def l3_tensor(e):
            tail_start(e, L3, P1[0])

            def tile(u, p, last):
                e.wait_ge(L3["o_read"], 2 * u + p)
                tail_tensor(e, L3, 2 * u + p, P1[p], None if last and p else P1[1 - p], product_rows(e, pO[p]))
            pairs(e, tile)

        @block.sync
        def _(y):
            y.dma_start(xs[:, :, :], x_in.rearrange("(t p) d -> p t d", p=P)).then_inc(x_loaded, 16)
            for i, w in enumerate((W_l, W_r, W_v)):
                y.dma_start(wlrv[:, i * D:(i + 1) * D], w).then_inc(w_loaded, 16)
            for h in range(HEADS):
                y.dma_start(arow[:, h * HD:(h + 1) * HD], a0.unsqueeze(0).to_broadcast([P, HD])).then_inc(w_loaded, 16)
            y.dma_start(grow[:, :], ln_g.unsqueeze(0).to_broadcast([P, D])).then_inc(w_loaded, 16)
            y.dma_start(brow[:, :], ln_b.unsqueeze(0).to_broadcast([P, D])).then_inc(w_loaded, 16)
            q = prep_sems[0]
            kv_v = kv_dram.rearrange("(t p) d -> t p d", p=P)
            with y.Fori(0, T // 2) as u:
                for p in range(2):
                    t = 2 * u + p
                    y.wait_ge(q["w_out"], t + 1)
                    y.dma_start(kv_v[bass.ds(t, 1), :, :].rearrange("a p d -> (a p) d"), kvs[p][:, :])\
                     .then_inc(kvs_stored[p], 16)
            l0_sync(y)
            with y.If(flag(y, 0) > BAD_OVER):
                dense_sync(y)
            last = layer_done[0]
            if upto > 1:
                l1_sync(y)
            if upto > 2:
                l2_sync(y)
            if upto > 3:
                l3_sync(y)
                y.wait_ge(L3["o_read"], T)
            else:
                y.wait_ge(layer_done[upto - 1], 1)
            y.dma_start(out.rearrange("(t p) d -> p t d", p=P), xs[:, :, :]).then_inc(s["flags_out"], 16)
            y.wait_ge(s["flags_out"], 16)

        @block.gpsimd
        def _(g):
            g.memset(ident[:, :], 0.0).then_inc(consts, 1)
            g.memset(ones[:, :], 1.0)
            g.memset(mhalf[:, :], -0.5)
            g.wait_ge(consts, 1)
            g.affine_select(out=ident[:, :], in_=ident[:, :], compare_op=ALU.not_equal, fill=1.0,
                            base=0, pattern=[[-1, P]], channel_multiplier=1).then_inc(consts, 1)
            g.iota(iota[:, :], [[-1, N]], base=N, channel_multiplier=0).then_inc(consts, 1)
            g.memset(ga[0][:, :, :], 0.0)
            g.memset(ga[1][:, :, :], 0.0).then_inc(consts, 1)
            g.wait_ge(consts, 4)
            for p in range(2):
                g.wait_ge(kvs_stored[p], 16 * (T // 2))
            l0_gpsimd(g)
        @block.vector
        def _(v):
            v.wait_ge(x_loaded, 16)
            v.wait_ge(w_loaded, 16 * 9)
            v.tensor_scalar(arow[:, :], arow[:, :], 1 - SLOPE, None, ALU.mult).then_inc(prep_sems[0]["arow"], 1)
            v.wait_ge(prep_sems[0]["arow"], 1)
            prep_vector(v, 0)
            l0_vector(v)
            flags_vector(v)
            with v.If(flag(v, 0) > BAD_OVER):
                dense_vector(v)
            l0_end_vector(v)
            if upto > 1:
                prep_vector(v, 1)
                with v.If(flag(v, 1) > 0):
                    any_vector(v)
                with v.Else():
                    l1_vector(v)
            if upto > 2:
                l2_weights_vector(v)
                prep_vector(v, 2)
                l2_vector(v)
            if upto > 3:
                prep_vector(v, 3)
                l3_vector(v)

        @block.scalar
        def _(a):
            a.wait_ge(x_loaded, 16)
            prep_scalar(a, 0)
            l0_scalar(a)
            with a.If(flag(a, 0) > BAD_OVER):
                dense_scalar(a)
            root_scalar(a, end_sems)
            if upto > 1:
                prep_scalar(a, 1)
                a.wait_ge(L1["w_in"], 32)
                a.wait_ge(prep_sems[1]["hcol_ready"], T)
                with a.If(flag(a, 1) > 0):
                    any_scalar(a)
                with a.Else():
                    l1_scalar(a)
            if upto > 2:
                prep_scalar(a, 2)
                l2_scalar(a)
            if upto > 3:
                prep_scalar(a, 3)
                l3_scalar(a)

        @block.tensor
        def _(e):
            e.wait_ge(consts, 4)
            e.wait_ge(w_loaded, 16 * 9)
            prep_tensor(e, 0)
            l0_tensor(e)
            flags_tensor(e)
            with e.If(flag(e, 0) > BAD_OVER):
                dense_tensor(e)
            if upto > 1:
                prep_tensor(e, 1)
                e.wait_ge(prep_sems[1]["hcol_ready"], T)
                with e.If(flag(e, 1) > 0):
                    any_tensor(e)
                with e.Else():
                    l1_tensor(e)
            if upto > 2:
                e.wait_ge(L2["wmade"], 5)
                prep_tensor(e, 2)
                l2_tensor(e)
            if upto > 3:
                prep_tensor(e, 3)
                e.wait_ge(prep_sems[3]["hcol_ready"], T)
                l3_tensor(e)


_INS = ["x", "adj", "L0_gnn_W_l", "L0_gnn_W_r", "L0_gnn_W_v", "L0_gnn_a", "L0_gnn_ln_g", "L0_gnn_ln_b",
        "L1_gnn_W", "L1_gnn_b", "L2_gnn_W", "L2_gnn_a"]


def kernel(**inputs):
    import numpy as _np
    import concourse.bacc as _bacc
    from concourse import mybir as _mybir
    from concourse.bass_utils import run_bass_kernel_spmd as _run

    nc = _bacc.Bacc("TRN2", target_bir_lowering=False, num_devices=1)
    arrays, args = {}, []
    for name in _INS:
        a = _np.ascontiguousarray(inputs[name])
        arrays[f"in_{name}_dram"] = a
        args.append(nc.dram_tensor(f"in_{name}_dram", a.shape, _mybir.dt.from_np(a.dtype), kind="ExternalInput").ap())
    o = nc.dram_tensor("out_0_dram", (N, D), F32, kind="ExternalOutput").ap()
    build(nc, *args, o)
    r = _run(nc, [arrays], core_ids=[0])
    return r.results[0]["out_0_dram"]
```

```python
from contextlib import ExitStack

import concourse.bass as bass
from concourse import mybir

F32 = mybir.dt.float32
BF16 = mybir.dt.bfloat16
I32 = mybir.dt.int32
U16 = mybir.dt.uint16
ALU = mybir.AluOpType
ACT = mybir.ActivationFunctionType
AX = mybir.AxisListType.X

P = 128
N, D = 4096, 128
T = N // P
HEADS, HD = 4, 32
LN_EPS = 1e-5
SLOPE = 0.2
SQ = 8
SLOTS = 64
GR = SLOTS // 8
PART = 32
SEG = 64
NSEG = N // SEG
BAD_OVER = 0
MASKED = -1e30


class Count:

    def __init__(self, base):
        self.base, self.n = base, 0

    def inc(self):
        self.n += 1
        return 1

    def now(self):
        return self.base + self.n


def build(nc, x_in, adj, W_l, W_r, W_v, a0, ln_g, ln_b, W1, b1, W2, a2, out):
    KV = 2 * D + HEADS
    kv_dram = nc.dram_tensor("kv_rows", [N, KV], F32, kind="Internal").ap()
    with ExitStack() as ctx:
        def sem(name):
            return ctx.enter_context(nc.semaphore(name))

        def sb(name, shape, dt=F32, where=ctx):
            return where.enter_context(nc.sbuf_tensor(name, shape, dt))

        def ps(name, shape, dt=F32, where=ctx):
            return where.enter_context(nc.psum_tensor(name, shape, dt))

        xs = sb("xs", [P, T, D])
        rows = sb("rows", [P, T, D])
        cols = sb("cols", [P, N])
        ident = sb("ident", [P, P])
        ones = sb("ones", [P, P])
        hrow = [sb(f"hrow{i}", [P, D]) for i in range(2)]
        hcol = [sb(f"hcol{i}", [P, P]) for i in range(2)]
        bst = sb("bst", [P, T, 6])
        mv = sb("mv", [P, T, 2])
        std = sb("std", [P, T])
        rstd = sb("rstd", [P, T])
        nmr = sb("nmr", [P, T])
        flags = sb("flags", [P, 2], I32)
        top0 = sb("top0", [P, T])
        nan = sb("nan", [P, T])
        arow = sb("arow", [P, D])
        grow = sb("grow", [P, D])
        brow = sb("brow", [P, D])

        x_loaded, w_loaded, consts = sem("x_loaded"), sem("w_loaded"), sem("consts")
        waited = sem("waited")

        def layer_sems(n, names):
            return {k: sem(f"L{n}_{k}") for k in names.split()}

        prep_sems = [layer_sems(f"{n}prep", "own var stats hrow_ready" + " hT_ready hcol_ready" * (n < 3)
                                + " w_ready w_out" * (n in (0, 2)) + " lin arow w_copied" * (n == 0)) for n in range(4)]
        layer_done = [sem(f"layer_done{n}") for n in range(4)]
        s = layer_sems(0, "adj_in0 adj_in1 adj_free squared own lists kl_sum kl_act kl_used "
                          "counted count_own need need_used flag_own flag_rows flag_sum e_ready p_ready "
                          "v_scaled sums_read flags kvs_stored0 kvs_stored1")
        stored = sem("stored")
        kvs_stored = [s["kvs_stored0"], s["kvs_stored1"]]
        adj_in = [s["adj_in0"], s["adj_in1"]]
        gathered = [[sem(f"L0_gathered{q}{g}") for g in range(4)] for q in range(2)]
        summed = [sem(f"L0_summed{g}") for g in range(4)]

        z0 = ExitStack()
        ga = [sb(f"gathered_part{q}", [P, PART, KV], F32, z0) for q in range(2)]
        kl0 = sb("kl0", [P, PART, D], F32, z0)
        zk = ExitStack()
        kvs = [sb(f"kvs{i}", [P, KV], F32, zk) for i in range(2)]
        lin = sb("lin", [P, 2, D], F32, zk)
        alin = sb("alin", [P, D], F32, zk)
        wlrv = sb("wlrv", [P, 3 * D], F32, zk)
        zk.close()
        kl = [kl0, sb("kl1", [P, PART, D], F32, z0)]
        adjt = [sb(f"adj_tile{i}", [P, N], I32, z0) for i in range(2)]
        key = sb("key", [P, N], U16, z0)
        iota = sb("iota", [P, N], U16, z0)
        cand = sb("cand", [P, NSEG * 8], F32, z0)
        top = sb("top", [P, SLOTS], F32, z0)
        idx = [sb(f"idx{i}", [P, SLOTS], I32, z0) for i in range(2)]
        mb = [sb(f"slot_mask{i}", [P, SLOTS], F32, z0) for i in range(2)]
        E = sb("E", [P, PART, HEADS], F32, z0)
        Pr = sb("Pr", [P, PART, HEADS], F32, z0)
        mx = [[sb(f"mx{p}{q}", [P, HEADS], F32, z0) for q in range(2)] for p in range(2)]
        cm = sb("cm", [P, HEADS], F32, z0)
        dm = [sb(f"dm{p}", [P, HEADS], F32, z0) for p in range(2)]
        sc = [sb(f"sc{p}", [P, HEADS], F32, z0) for p in range(2)]
        sm = [[sb(f"sm{p}{q}", [P, HEADS], F32, z0) for q in range(2)] for p in range(2)]
        o0 = sb("o0", [P, D], F32, z0)
        o1 = sb("o1", [P, D], F32, z0)
        den = sb("den", [P, HEADS], F32, z0)
        ksum = sb("ksum", [P, T], F32, z0)
        tsum = sb("tsum", [P, T], F32, z0)
        sq = sb("sq", [P, SQ, T], F32, z0)
        li = sb("li", [P, T, HEADS], F32, z0)
        mhalf = sb("mhalf", [P, 1], F32, z0)
        odd = sb("odd", [P, 2, T], F32, z0)
        needed = [sb(f"needed{i}", [P, GR], F32, z0) for i in range(2)]
        need = [sb(f"need{i}", [P, GR], I32, z0) for i in range(2)]
        any_row = sb("any_row", [P, GR], F32, z0)
        raised = sb("raised", [P, GR], F32, z0)
        gate = [sb(f"gate{i}", [P, GR], I32, z0) for i in range(2)]
        fl = sb("fl", [P, 3], F32, z0)
        on = sb("on", [P, PART], F32, z0)
        off = sb("off", [P, PART], F32, z0)
        z0.close()

        pT_ring = sb("pT_ring", [P, 4 * 512])
        z1 = ExitStack()
        adj1 = [sb(f"adj1_{i}", [P, N], I32, z1) for i in range(2)]
        mask1 = [sb(f"mask1_{i}", [P, N], BF16, z1) for i in range(2)]
        Z1 = [sb(f"Z1_{i}", [P, N], F32, z1) for i in range(2)]
        hs = [sb(f"hs{i}", [P, P], F32, z1) for i in range(2)]
        w1c = sb("w1c", [P, 4], F32, z1)
        b1c = sb("b1c", [P, 4], F32, z1)
        zm = [sb(f"zm{i}", [P, 1], F32, z1) for i in range(2)]
        nm = [sb(f"nm{i}", [P, 1], F32, z1) for i in range(2)]
        rs = [sb(f"rs{i}", [P, 1], F32, z1) for i in range(2)]
        ri = sb("ri", [P, 1], F32, z1)
        zp = ExitStack()
        P1 = [sb(f"P1_{i}", [P, N], F32, zp) for i in range(2)]
        zp.close()
        zp = ExitStack()
        identb = sb("identb", [P, P], BF16, zp)
        hsplit = sb("hsplit", [P, T, 3, D], BF16, zp)
        aT_ring = sb("aT_ring", [P, T // 8, 8 * P], BF16, zp)
        zp.close()
        z1.close()
        z2 = ExitStack()
        adj2 = sb("adj2", [P, N], I32, z2)
        mask2 = sb("mask2", [P, N], BF16, z2)
        Z2 = [sb(f"Z2_{i}", [P, N], F32, z2) for i in range(2)]
        P2b = sb("P2b", [P, N], F32, z2)
        dbc = sb("dbc", [P, HEADS, N], F32, z2)
        w2s = sb("w2s", [P, D + HEADS], F32, z2)
        asd = sb("asd", [P, HEADS, 2, HD], F32, z2)
        wa = sb("wa", [P, D], F32, z2)
        wd = sb("wd", [P, HEADS], F32, z2)
        wrep = sb("wrep", [P, HEADS, P], F32, z2)
        si = sb("si", [P, T, HEADS], F32, z2)
        zm2 = [sb(f"zm2_{i}", [P, 1], F32, z2) for i in range(2)]
        nm2 = [sb(f"nm2_{i}", [P, 1], F32, z2) for i in range(2)]
        rs2 = [sb(f"rs2_{i}", [P, HEADS], F32, z2) for i in range(2)]
        ri2 = sb("ri2", [P, HEADS], F32, z2)
        z2.close()

        pz = ExitStack()
        pS = [ps(f"pS{i}", [P, 512], F32, pz) for i in range(2)]
        pX = [ps(f"pX{i}", [P, 512], F32, pz) for i in range(4)]
        pO = [ps(f"pO{i}", [P, 512], F32, pz) for i in range(2)]
        pz.close()
        pz = ExitStack()
        pXb_below = [ps(f"pXb_below{i}", [P, 512], F32, pz) for i in range(2)]
        pXb = [ps(f"pXb{i}", [P, 8 * P], BF16, pz) for i in range(4)]
        pz.close()
        pz = ExitStack()
        pT = [ps(f"prep_T{i}", [P, P], F32, pz) for i in range(2)]
        pW = [ps(f"prep_W{i}", [P, 3 * D], F32, pz) for i in range(2)]
        pz.close()
        pz = ExitStack()
        pK = [ps(f"pK{i}", [P, 8, D], F32, pz) for i in range(2)]
        pA = [ps(f"pA{i}", [P, 4, D], F32, pz) for i in range(2)]
        pN = ps("pN", [P, 512], F32, pz)
        squares = ps("squares", [P, N // SQ], F32, pz)
        pz.close()

        adj_v = adj.rearrange("(t p) j -> t p j", p=P)

        def adj_tile(t):
            return adj_v[t, :, :] if isinstance(t, int) else adj_v[bass.ds(t, 1), :, :].rearrange("a p j -> (a p) j")

        block = ctx.enter_context(nc.Block())

        def below(value, least):
            return isinstance(value, int) and value < least

        def row_stats_vector(v, src, q):
            with v.Fori(0, T // 4) as u:
                for k in range(4):
                    v.bn_stats(bst[:, 4 * u + k, :], src[:, 4 * u + k, :]).then_inc(q["own"], 1)
            v.wait_ge(q["own"], T)
            for t in range(T):
                v.bn_aggr(mv[:, t, :], bst[:, t, :]).then_inc(q["own"], 1)
            v.wait_ge(q["own"], 2 * T)
            v.tensor_scalar(std[:, :], mv[:, :, 1], LN_EPS, None, ALU.add).then_inc(q["var"], 1)
            v.wait_ge(q["var"], 2)
            v.reciprocal(rstd[:, :], std[:, :]).then_inc(q["own"], 1)
            v.wait_ge(q["own"], 2 * T + 1)
            v.scalar_tensor_tensor(nmr[:, :], mv[:, :, 0], -1.0, rstd[:, :], ALU.mult, ALU.mult)\
             .then_inc(q["stats"], 1)

        def root_scalar(a, q):
            a.wait_ge(q["var"], 1)
            a.activation(std[:, :], std[:, :], ACT.Sqrt).then_inc(q["var"], 1)

        def prep_vector(v, n):
            q = prep_sems[n]

            def weights(u, p):
                t = 2 * u + p
                v.wait_ge(q["w_ready"], t + 1)
                if n == 2:
                    v.tensor_copy(rows[:, t, :], pW[p][:, 0:D])
                    v.tensor_copy(si[:, t, :], pW[p][:, D:D + HEADS]).then_inc(q["w_out"], 1)
                if n == 0:
                    v.wait_ge(q["w_out"], t)
                    v.tensor_tensor(lin[:, :, :], pW[p][:, 0:2 * D].rearrange("p (a d) -> p a d", a=2),
                                    alin[:, :].unsqueeze(1).to_broadcast([P, 2, D]), ALU.mult).then_inc(q["lin"], 1)
                    v.wait_ge(q["lin"], t + 1)
                    v.tensor_reduce(li[:, t, :], lin[:, 0, :].rearrange("p (h d) -> p h d", h=HEADS), AX, ALU.add)
                    if not below(u, 1):
                        v.wait_ge(kvs_stored[p], 16 * u)
                    v.tensor_reduce(kvs[p][:, 2 * D:KV], lin[:, 1, :].rearrange("p (h d) -> p h d", h=HEADS),
                                    AX, ALU.add).then_inc(q["w_out"], 1)

            row_stats_vector(v, xs, q)
            if n in (0, 2):
                weights(0, 0)
                weights(0, 1)
                with v.Fori(1, T // 2) as u:
                    weights(u, 0)
                    weights(u, 1)

        def prep_scalar(a, n):
            q = prep_sems[n]

            def normed(t, p):
                if not below(t, 2) and n < 3:
                    a.wait_ge(q["hT_ready"], t - 1)
                a.activation(rows[:, t, :] if n == 3 else hrow[p][:, :], xs[:, t, :], ACT.Relu,
                             bias=nmr[:, bass.ds(t, 1)], scale=rstd[:, bass.ds(t, 1)]).then_inc(q["hrow_ready"], 1)
                if n == 1:
                    a.wait_ge(q["hrow_ready"], t + 1)
                    a.copy(rows[:, t, :], hrow[p][:, :])

            def weighed(u, p):
                t = 2 * u + p
                a.wait_ge(q["lin"], t + 1)
                if not below(t, 2):
                    a.wait_ge(kvs_stored[p], 16 * u)
                a.copy(cols[:, bass.ts(t, D)], pW[p][:, 0:D])
                a.copy(kvs[p][:, 0:2 * D], pW[p][:, D:3 * D]).then_inc(q["w_copied"], 1)

            def turned(t, p):
                a.wait_ge(q["hT_ready"], t + 1)
                if n in (0, 2):
                    if not below(t, 2):
                        a.wait_ge(q["w_ready"], t - 1)
                    a.copy(hcol[p][:, :], pT[p][:, :]).then_inc(q["hcol_ready"], 1)
                    if n == 2:
                        a.copy(cols[:, bass.ts(t, P)], pT[p][:, :])
                else:
                    a.copy(cols[:, bass.ts(t, P)], pT[p][:, :]).then_inc(q["hcol_ready"], 1)

            def two(u, last=False):
                for p in range(2):
                    t = 2 * u + p
                    if not (last and p == 1):
                        normed(t + 1, 1 - p)
                    if n < 3:
                        turned(t, p)
                    if n == 0 and not below(t, 1):
                        weighed(*((u, 0) if p else (u - 1, 1)))
            root_scalar(a, q)
            a.wait_ge(q["stats"], 1)
            normed(0, 0)
            two(0)
            with a.Fori(1, T // 2 - 1) as u:
                two(u)
            two(T // 2 - 1, True)
            if n == 0:
                weighed(T // 2 - 1, 1)

        def prep_tensor(e, n):
            q = prep_sems[n]

            def two(u):
                for p in range(2):
                    t = 2 * u + p
                    e.wait_ge(q["hrow_ready"], t + 1)
                    if not below(t, 2):
                        e.wait_ge(q["hcol_ready"], t - 1)
                    e.transpose(pT[p][:, :], hrow[p][:, :], ident[:, :]).then_inc(q["hT_ready"], 1)
                    if n in (0, 2):
                        w = wlrv[:, :] if n == 0 else w2s[:, :]
                        e.wait_ge(q["hcol_ready"], t + 1)
                        if not below(t, 2):
                            e.wait_ge(q["w_out"], t - 1)
                            if n == 0:
                                e.wait_ge(q["w_copied"], t - 1)
                        e.matmul(pW[p][:, 0:3 * D if n == 0 else D + HEADS], hcol[p][:, :], w, start=True, stop=True)\
                         .then_inc(q["w_ready"], 1)
            two(0)
            with e.Fori(1, T // 2) as u:
                two(u)

        def settled(eng):
            eng.sem_inc(waited, 1)

        EARLY = 7 * NSEG // 8

        def list_early(v, u, p, c):
            t = 2 * u + p
            v.wait_ge(adj_in[p], 16 * (u + 1))
            v.scalar_tensor_tensor(key[:, :], adjt[p][:, :], 0.0, iota[:, :], ALU.not_equal, ALU.mult,
                                   accum_out=ksum[:, bass.ds(t, 1)]).then_inc(s["own"], c.inc())
            v.wait_ge(s["own"], c.now())
            v.sem_inc(s["adj_free"], 1)
            for g in range(EARLY):
                ins = v.max(cand[:, 8 * g:8 * g + 8], key[:, SEG * g:SEG * (g + 1)])
            ins.then_inc(s["own"], c.inc())

        def list_late(v, u, p, c):
            t = 2 * u + p
            for g in range(EARLY, NSEG):
                ins = v.max(cand[:, 8 * g:8 * g + 8], key[:, SEG * g:SEG * (g + 1)])
            ins.then_inc(s["own"], c.inc())
            for r in range(SLOTS // 8):
                v.wait_ge(s["own"], c.now())
                settled(v)
                v.max(top[:, 8 * r:8 * r + 8], cand[:, :]).then_inc(s["own"], c.inc())
                if r < SLOTS // 8 - 1:
                    v.wait_ge(s["own"], c.now())
                    settled(v)
                    v.match_replace(cand[:, :], top[:, 8 * r:8 * r + 8], cand[:, :], 0.0)\
                     .then_inc(s["own"], c.inc())
            v.wait_ge(s["own"], c.now())
            if not below(u, 1):
                v.wait_ge(s["kl_sum"], 8 * (t - 1))
            v.tensor_scalar(idx[p][:, :], top[:, :], -1.0, float(N), ALU.mult, ALU.add)
            v.tensor_scalar(mb[p][:, :], top[:, :], 0.0, MASKED, ALU.is_equal, ALU.mult)
            v.tensor_copy(top0[:, bass.ds(t, 1)], top[:, 0:1])
            v.tensor_scalar(needed[p][:, :], top[:, :].rearrange("p (g e) -> p g e", e=8)[:, :, 0], 0.0, None, ALU.is_gt)
            v.tensor_reduce(tsum[:, bass.ds(t, 1)], top[:, :], AX, ALU.add).then_inc(s["lists"], 1)

        def a_vector(v, u, p, q, c):
            t = 2 * u + p
            seq = 2 * t + q
            v.wait_ge(s["kl_act"], 4 * (seq + 1))
            v.tensor_tensor(kl[q][:, :, :], kl[q][:, :, :], arow[:, :].unsqueeze(1).to_broadcast([P, PART, D]), ALU.mult)\
             .then_inc(s["own"], c.inc())
            v.wait_ge(s["own"], c.now())
            v.tensor_reduce(E[:, :, :], kl[q][:, :, :].rearrange("p s (h d) -> p s h d", h=HEADS), AX, ALU.add)\
             .then_inc(s["kl_used"], 1)
            v.wait_ge(s["kl_used"], seq + 1)
            v.wait_ge(s["lists"], t + 1)
            v.tensor_tensor(E[:, :, :], E[:, :, :], ga[q][:, :, 2 * D:KV], ALU.add).then_inc(s["own"], c.inc())
            v.wait_ge(s["own"], c.now())
            v.tensor_tensor(E[:, :, :], E[:, :, :], li[:, t, :].unsqueeze(1).to_broadcast([P, PART, HEADS]), ALU.add)\
             .then_inc(s["own"], c.inc())
            v.wait_ge(s["own"], c.now())
            v.tensor_tensor(E[:, :, :], E[:, :, :],
                            mb[p][:, q * PART:(q + 1) * PART].unsqueeze(2).to_broadcast([P, PART, HEADS]), ALU.add)\
             .then_inc(s["own"], c.inc())
            v.wait_ge(s["own"], c.now())
            m_out = mx[p][0] if q == 0 else cm
            v.tensor_reduce(m_out[:, :], E[:, :, :].rearrange("p s h -> p h s"), AX, ALU.max)\
             .then_inc(s["own"], c.inc())
            v.wait_ge(s["own"], c.now())
            if q == 1:
                v.tensor_tensor(mx[p][1][:, :], mx[p][0][:, :], cm[:, :], ALU.max).then_inc(s["own"], c.inc())
                v.wait_ge(s["own"], c.now())
                v.tensor_tensor(dm[p][:, :], mx[p][0][:, :], mx[p][1][:, :], ALU.subtract)
            v.tensor_tensor(E[:, :, :], E[:, :, :], mx[p][q][:, :].unsqueeze(1).to_broadcast([P, PART, HEADS]),
                            ALU.subtract).then_inc(s["e_ready"], 1)

        def b_vector(v, u, p, q):
            t = 2 * u + p
            seq = 2 * t + q
            v.wait_ge(s["p_ready"], seq + 1)
            for g in range(4):
                V = ga[q][:, 8 * g:8 * g + 8, D:2 * D].rearrange("p s (h d) -> p s h d", h=HEADS)
                v.tensor_tensor(V, V, Pr[:, 8 * g:8 * g + 8, :].unsqueeze(3).to_broadcast([P, 8, HEADS, HD]),
                                ALU.mult).then_inc(s["v_scaled"], 1)
            v.tensor_reduce(sm[p][q][:, :], Pr[:, :, :].rearrange("p s h -> p h s"), AX, ALU.add)\
             .then_inc(s["own_b"], 1)

        def fin_vector(v, u, p, c):
            t = 2 * u + p
            v.wait_ge(s["own_b"], 2 * (t + 1))
            v.wait_ge(s["p_scale"], t + 1)
            v.wait_ge(summed[3], 2 * (t + 1) + 1)
            v.tensor_reduce(o0[:, :], pA[0][:, :, :].rearrange("p k d -> p d k"), AX, ALU.add)
            v.tensor_reduce(o1[:, :], pA[1][:, :, :].rearrange("p k d -> p d k"), AX, ALU.add)\
             .then_inc(s["sums_read"], 1)
            v.tensor_tensor(den[:, :], sm[p][0][:, :], sc[p][:, :], ALU.mult).then_inc(s["own"], c.inc())
            v.wait_ge(s["sums_read"], t + 1)
            o0h = o0[:, :].rearrange("p (h d) -> p h d", h=HEADS)
            v.tensor_tensor(o0h, o0h, sc[p][:, :].unsqueeze(2).to_broadcast([P, HEADS, HD]), ALU.mult)\
             .then_inc(s["own"], c.inc())
            v.wait_ge(s["own"], c.now())
            v.tensor_tensor(den[:, :], den[:, :], sm[p][1][:, :], ALU.add).then_inc(s["own"], c.inc())
            v.tensor_tensor(o0[:, :], o0[:, :], o1[:, :], ALU.add).then_inc(s["own"], c.inc())
            v.wait_ge(s["own"], c.now())
            v.reciprocal(den[:, :], den[:, :]).then_inc(s["own"], c.inc())
            v.wait_ge(s["own"], c.now())
            v.tensor_tensor(rows[:, t, :].rearrange("p (h d) -> p h d", h=HEADS), o0h,
                            den[:, :].unsqueeze(2).to_broadcast([P, HEADS, HD]), ALU.mult).then_inc(s["own"], c.inc())

        s["own_b"] = sem("L0_own_b")
        NL_EARLY, NL_LATE, NA0, NA1, NF = 2, 16, 5, 6, 6
        NL = NL_EARLY + NL_LATE
        NB = NL + NA0 + NA1 + NF

        def counts(v, t, p):
            c = Count(2 * t)
            v.wait_ge(s["counted"], t + 1)
            v.wait_ge(s["count_own"], c.now())
            v.tensor_scalar(any_row[:, :], pN[:, 0:GR], 0.0, 16.0 * 8, ALU.is_gt, ALU.mult)\
             .then_inc(s["count_own"], c.inc())
            v.wait_ge(s["count_own"], c.now())
            if not below(t, 2):
                v.wait_ge(s["need_used"], t - 1)
            v.tensor_copy(need[p][:, :], any_row[:, :])
            v.tensor_tensor(raised[:, :], raised[:, :], any_row[:, :], ALU.add).then_inc(s["count_own"], c.inc())
            v.wait_ge(s["count_own"], c.now())
            v.tensor_copy(gate[p][:, :], raised[:, :]).then_inc(s["need"], 1)
            v.wait_ge(s["need"], t + 1)

        def l0_vector(v):
            v.wait_ge(consts, 4)
            for p in range(2):
                c = Count(NL * p)
                list_early(v, 0, p, c)
                list_late(v, 0, p, c)
                if p == 0:
                    counts(v, 0, 0)

            def tile(u, p, first=False, last=False):
                t = 2 * u + p
                c = Count(2 * NL + NB * t)
                up, pp = (u, 0) if p == 1 else (u - 1, 1)
                a_vector(v, u, p, 0, c)
                if not first:
                    fin_vector(v, up, pp, c)
                else:
                    c.n += NF
                    v.sem_inc(s["own"], NF)
                b_vector(v, u, p, 0)
                if not last:
                    list_early(v, u + 1, p, c)
                else:
                    c.n += NL_EARLY
                    v.sem_inc(s["own"], NL_EARLY)
                if not (last and p == 1):
                    counts(v, t + 1, 1 - p)
                a_vector(v, u, p, 1, c)
                b_vector(v, u, p, 1)
                if not last:
                    list_late(v, u + 1, p, c)
                else:
                    c.n += NL_LATE
                    v.sem_inc(s["own"], NL_LATE)
                assert c.n == NB, c.n
            tile(0, 0, first=True)
            tile(0, 1)
            with v.Fori(1, T // 2 - 1) as u:
                tile(u, 0)
                tile(u, 1)
            tile(T // 2 - 1, 0, last=True)
            tile(T // 2 - 1, 1, last=True)
            c = Count(2 * NL + NB * T)
            fin_vector(v, T // 2 - 1, 1, c)
            v.wait_ge(s["own"], c.now())

        def l0_scalar(a):
            a.wait_ge(consts, 4)

            def square(u, p):
                t = 2 * u + p
                a.wait_ge(adj_in[p], 16 * (u + 1))
                for k in range(SQ):
                    a.wait_ge(s["squared"], SQ * t + k)
                    settled(a)
                    a.activation(squares[:, :], adjt[p][:, k * (N // SQ):(k + 1) * (N // SQ)], ACT.Square,
                                 bias=mhalf[:, 0:1], accum_out=sq[:, k, bass.ds(t, 1)]).then_inc(s["squared"], 1)

            def relu(seq, q, g):
                a.wait_ge(s["kl_sum"], 4 * seq + g + 1)
                a.activation(kl[q][:, 8 * g:8 * g + 8, :], pK[g % 2][:, :, :], ACT.Relu).then_inc(s["kl_act"], 1)

            def tile(u, p, last=False):
                t = 2 * u + p
                for q in range(2):
                    seq = 2 * t + q
                    end = last and p == 1 and q == 1
                    if not end:
                        a.wait_ge(s["kl_used"], seq)
                        relu(seq + 1, 1 - q, 0)
                    a.wait_ge(s["e_ready"], seq + 1)
                    a.activation(Pr[:, :, :], E[:, :, :], ACT.Exp).then_inc(s["p_ready"], 1)
                    if q == 1:
                        a.activation(sc[p][:, :], dm[p][:, :], ACT.Exp).then_inc(s["p_scale"], 1)
                    if not end:
                        relu(seq + 1, 1 - q, 1)
                    if not end:
                        relu(seq + 1, 1 - q, 2)
                        relu(seq + 1, 1 - q, 3)
                    if q == 0 and not last:
                        square(u + 1, p)
            square(0, 0)
            square(0, 1)
            for g in range(4):
                relu(0, 0, g)
            with a.Fori(0, T // 2 - 1) as u:
                tile(u, 0)
                tile(u, 1)
            tile(T // 2 - 1, 0, last=True)
            tile(T // 2 - 1, 1, last=True)

        s["p_scale"] = sem("L0_p_scale")

        def l0_tensor(e):
            def sums(t, q, groups, p=None):
                seq = 2 * t + q
                wl = cols[:, bass.ts(t, D)].unsqueeze(1).to_broadcast([P, 4, D])
                for g in groups:
                    if q == 0:
                        e.wait_ge(gathered[q][g], 16 * 8 * (t + 1))
                    else:
                        e.wait_ge(s["need"], t + 1)
                        settled(e)
                        to = e.value_load(gate[p][0:1, GR // 2 + g:GR // 2 + g + 1], min_val=0, max_val=16 * 8 * T)
                        e.wait_ge(gathered[q][g], to)
                    if q or g >= 2 or not below(t, 1):
                        e.wait_ge(s["kl_act"], 4 * seq + g - 1)
                    for b in range(2):
                        k = 8 * g + 4 * b
                        e.matmul(pK[g % 2][:, 4 * b:4 * b + 4, :], ident[:, :], ga[q][:, k:k + 4, 0:D],
                                 start=True, stop=False)
                        ins = e.matmul(pK[g % 2][:, 4 * b:4 * b + 4, :], ident[:, :], wl, start=False, stop=True)
                    ins.then_inc(s["kl_sum"], 1)

            def total(t, q):
                e.wait_ge(s["sums_read"], t)
                for g in range(4):
                    e.wait_ge(s["v_scaled"], 4 * (2 * t + q) + g + 1)
                    for k in (2 * g, 2 * g + 1):
                        ins = e.matmul(pA[q][:, :, :], ident[:, :], ga[q][:, 4 * k:4 * k + 4, D:2 * D],
                                       start=(k == 0), stop=(k == PART // 4 - 1))
                    ins.then_inc(summed[g], 1)

            def count(t, p):
                e.wait_ge(s["lists"], t + 1)
                e.wait_ge(s["need"], t)
                e.matmul(pN[:, 0:GR], ones[:, :], needed[p][:, :], start=True, stop=True).then_inc(s["counted"], 1)

            def tile(u, p, last=False):
                t = 2 * u + p
                for q in range(2):
                    nxt = (t, 1) if q == 0 else None if last else (t + 1, 0)
                    if nxt:
                        sums(*nxt, range(0, 2), p)
                    total(t, q)
                    if q == 0 and not last:
                        count(t + 1, 1 - p)
                    if nxt:
                        sums(*nxt, range(2, 4), p)
            for g in range(4):
                e.sem_inc(summed[g], 1)
            count(0, 0)
            sums(0, 0, range(4))
            with e.Fori(0, T // 2 - 1) as u:
                tile(u, 0)
                tile(u, 1)
            tile(T // 2 - 1, 0)
            tile(T // 2 - 1, 1, last=True)

        def gather(g, p, q, k0):
            for k in range(k0, k0 + 8):
                g.indirect_dma_start(
                    out=ga[q][:, k, :], out_offset=None, in_=kv_dram[:, :],
                    in_offset=bass.IndirectOffsetOnAxis(ap=idx[p][:, q * PART + k:q * PART + k + 1], axis=0),
                    bounds_check=N - 1, oob_is_err=False).then_inc(gathered[q][k0 // 8], 16)

        def l0_gpsimd(g):
            with g.Fori(0, T // 2) as u:
                for p in range(2):
                    t = 2 * u + p
                    g.wait_ge(s["lists"], t + 1)
                    for n in range(GR):
                        q, k0 = n // 4, 8 * (n % 4)
                        if n == GR // 2:
                            g.wait_ge(s["need"], t + 1)
                        g.wait_ge(summed[k0 // 8], 2 * t + q)
                        settled(g)
                        if n < GR // 2:
                            gather(g, p, q, k0)
                        else:
                            rows_in = g.value_load(need[p][0:1, n:n + 1], min_val=0, max_val=16 * 8)
                            with g.If(rows_in > 0):
                                gather(g, p, q, k0)
                    g.sem_inc(s["need_used"], 1)

        def l0_sync(y):
            for p in range(2):
                y.dma_start(adjt[p][:, :], adj_tile(p)).then_inc(adj_in[p], 16)
            with y.Fori(1, T // 2) as u:
                for p in range(2):
                    t = 2 * u + p
                    y.wait_ge(s["squared"], SQ * (t - 1))
                    settled(y)
                    y.wait_ge(s["adj_free"], t - 1)
                    y.dma_start(adjt[p][:, :], adj_tile(t))\
                     .then_inc(adj_in[p], 16)

        def flags_vector(v):
            v.wait_ge(s["squared"], SQ * T)
            v.tensor_tensor(odd[:, 0, :], ksum[:, :], tsum[:, :], ALU.not_equal)
            v.tensor_scalar(odd[:, 1, :], top0[:, :], 0.0, None, ALU.is_equal)
            v.tensor_scalar(sq[:, :, :], sq[:, :, :], N / SQ / 4, None, ALU.not_equal).then_inc(s["flag_own"], 1)
            v.wait_ge(s["flag_own"], 1)
            v.tensor_reduce(fl[:, 0:2], odd[:, :, :], AX, ALU.max)
            v.tensor_reduce(fl[:, 2:3], sq[:, :, :].rearrange("p a t -> p (a t)"), AX, ALU.max).then_inc(s["flag_rows"], 1)
            v.wait_ge(s["flag_sum"], 1)
            v.tensor_copy(fl[:, 0:3], pA[1][:, 0, 0:3]).then_inc(s["flag_own"], 1)
            v.wait_ge(s["flag_own"], 2)
            v.tensor_tensor(flags[:, 0:1], fl[:, 0:1], fl[:, 1:2], ALU.add)
            v.tensor_copy(flags[:, 1:2], fl[:, 2:3]).then_inc(s["flags"], 1)

        def flags_tensor(e):
            e.wait_ge(s["flag_rows"], 1)
            e.matmul(pA[1][:, 0, 0:3], ones[:, :], fl[:, 0:3], start=True, stop=True).then_inc(s["flag_sum"], 1)

        def flag(eng, k):
            eng.wait_ge(s["flags"], 1)
            return eng.value_load(flags[0:1, k:k + 1], min_val=0, max_val=2 * N)

        d0 = layer_sems("0dense", "adj in0 in1 kl_sum kl_act own e_ready p_ready v_scaled summed done masks masks2")
        CH = N // (2 * PART)
        D_STEPS = 18

        def dense_parts(eng, tile_start, part, tile_end):
            with eng.Fori(0, T) as t:
                tile_start(t)
                with eng.Fori(0, CH) as c:
                    for q in range(2):
                        part(t, c, q, 2 * (CH * t + c) + q)
                tile_end(t)

        def dense_sync(y):
            def start(t):
                y.wait_ge(d0["done"], t)
                y.dma_start(adjt[0][:, :], adj_tile(t)).then_inc(d0["adj"], 16)

            def part(t, c, q, seq):
                y.wait_ge(d0["summed"], seq)
                src = kv_dram[bass.ds(c * (2 * PART) + q * PART, PART), :].rearrange("s d -> (s d)")
                y.dma_start(ga[q][:, :, :].rearrange("p s d -> p (s d)"),
                            src.unsqueeze(0).to_broadcast([P, PART * KV])).then_inc(d0[f"in{q}"], 16)
            dense_parts(y, start, part, lambda t: None)

        def dense_tensor(e):
            def part(t, c, q, seq):
                e.wait_ge(d0[f"in{q}"], 16 * (CH * t + c + 1))
                wl = cols[:, bass.ts(t, D)].unsqueeze(1).to_broadcast([P, 4, D])
                for g in range(4):
                    e.wait_ge(d0["kl_act"], 4 * seq + g)
                    for b in range(2):
                        k = 8 * g + 4 * b
                        e.matmul(pK[g % 2][:, 4 * b:4 * b + 4, :], ident[:, :], ga[q][:, k:k + 4, 0:D],
                                 start=True, stop=False)
                        ins = e.matmul(pK[g % 2][:, 4 * b:4 * b + 4, :], ident[:, :], wl, start=False, stop=True)
                    ins.then_inc(d0["kl_sum"], 1)
                e.wait_ge(d0["v_scaled"], seq + 1)
                for k in range(PART // 4):
                    ins = e.matmul(pA[q][:, :, :], ident[:, :], ga[q][:, 4 * k:4 * k + 4, D:2 * D],
                                   start=(k == 0), stop=(k == PART // 4 - 1))
                ins.then_inc(d0["summed"], 1)
            dense_parts(e, lambda t: None, part, lambda t: None)

        def dense_scalar(a):
            def part(t, c, q, seq):
                for g in range(4):
                    a.wait_ge(d0["kl_sum"], 4 * seq + g + 1)
                    a.activation(kl[0][:, 8 * g:8 * g + 8, :], pK[g % 2][:, :, :], ACT.Relu).then_inc(d0["kl_act"], 1)
                a.wait_ge(d0["e_ready"], seq + 1)
                a.activation(Pr[:, :, :], E[:, :, :], ACT.Exp)
                a.activation(sc[0][:, :], dm[0][:, :], ACT.Exp).then_inc(d0["p_ready"], 1)
            dense_parts(a, lambda t: None, part, lambda t: None)

        def dense_vector(v):
            m, total = mx[0][0], sm[0][0]
            o0h = o0[:, :].rearrange("p (h d) -> p h d", h=HEADS)

            def start(t):
                v.memset(m[:, :], -3e38)
                v.memset(total[:, :], 0.0)
                v.memset(o0[:, :], 0.0).then_inc(d0["masks"], 1)
                v.wait_ge(d0["adj"], 16 * (t + 1))
                v.wait_ge(d0["masks"], t + 1)
                settled(v)

            def part(t, c, q, seq):
                k = Count(D_STEPS * seq)
                own = d0["own"]

                def last():
                    v.wait_ge(own, k.now())
                wide = [P, PART, HEADS]
                v.tensor_scalar(on[:, :], adjt[0][:, bass.ds(c * (2 * PART) + q * PART, PART)], 0.0, None,
                                ALU.not_equal).then_inc(own, k.inc())
                last()
                v.tensor_scalar(off[:, :], on[:, :], -1.0, 1e9, ALU.add, ALU.mult).then_inc(own, k.inc())
                v.wait_ge(d0["kl_act"], 4 * (seq + 1))
                v.tensor_tensor(kl[0][:, :, :], kl[0][:, :, :], arow[:, :].unsqueeze(1).to_broadcast([P, PART, D]),
                                ALU.mult).then_inc(own, k.inc())
                last()
                v.tensor_reduce(E[:, :, :], kl[0][:, :, :].rearrange("p s (h d) -> p s h d", h=HEADS), AX, ALU.add)\
                 .then_inc(own, k.inc())
                for other, op in ((ga[q][:, :, 2 * D:KV], ALU.add),
                                  (li[:, t, :].unsqueeze(1).to_broadcast(wide), ALU.add),
                                  (on[:, :].unsqueeze(2).to_broadcast(wide), ALU.mult),
                                  (off[:, :].unsqueeze(2).to_broadcast(wide), ALU.add)):
                    last()
                    v.tensor_tensor(E[:, :, :], E[:, :, :], other, op).then_inc(own, k.inc())
                last()
                v.tensor_reduce(cm[:, :], E[:, :, :].rearrange("p s h -> p h s"), AX, ALU.max).then_inc(own, k.inc())
                last()
                v.tensor_tensor(cm[:, :], cm[:, :], m[:, :], ALU.max).then_inc(own, k.inc())
                last()
                v.tensor_tensor(dm[0][:, :], m[:, :], cm[:, :], ALU.subtract).then_inc(own, k.inc())
                last()
                v.tensor_copy(m[:, :], cm[:, :])
                v.tensor_tensor(E[:, :, :], E[:, :, :], cm[:, :].unsqueeze(1).to_broadcast(wide), ALU.subtract)\
                 .then_inc(d0["e_ready"], 1)
                v.wait_ge(d0["p_ready"], seq + 1)
                V = ga[q][:, :, D:2 * D].rearrange("p s (h d) -> p s h d", h=HEADS)
                v.tensor_tensor(V, V, Pr[:, :, :].unsqueeze(3).to_broadcast([P, PART, HEADS, HD]), ALU.mult)\
                 .then_inc(d0["v_scaled"], 1)
                v.tensor_reduce(sm[0][1][:, :], Pr[:, :, :].rearrange("p s h -> p h s"), AX, ALU.add)
                v.tensor_tensor(total[:, :], total[:, :], sc[0][:, :], ALU.mult).then_inc(own, k.inc())
                last()
                v.tensor_tensor(total[:, :], total[:, :], sm[0][1][:, :], ALU.add)
                v.tensor_tensor(o0h, o0h, sc[0][:, :].unsqueeze(2).to_broadcast([P, HEADS, HD]), ALU.mult)\
                 .then_inc(own, k.inc())
                v.wait_ge(d0["summed"], seq + 1)
                v.tensor_reduce(o1[:, :], pA[q][:, :, :].rearrange("p k d -> p d k"), AX, ALU.add)\
                 .then_inc(own, k.inc())
                last()
                v.tensor_tensor(o0[:, :], o0[:, :], o1[:, :], ALU.add).then_inc(own, k.inc())
                last()
                v.sem_inc(own, D_STEPS - k.n)

            def end(t):
                v.reciprocal(den[:, :], total[:, :]).then_inc(d0["masks2"], 1)
                v.wait_ge(d0["masks2"], t + 1)
                v.tensor_tensor(rows[:, t, :].rearrange("p (h d) -> p h d", h=HEADS), o0h,
                                den[:, :].unsqueeze(2).to_broadcast([P, HEADS, HD]), ALU.mult)\
                 .then_inc(d0["done"], 1)
                v.wait_ge(d0["done"], t + 1)
            dense_parts(v, start, part, end)

        end_sems = layer_sems("0end", "own var stats step")

        def l0_end_vector(v):
            row_stats_vector(v, rows, end_sems)
            v.wait_ge(end_sems["stats"], 1)

            c = Count(0)
            wide = [P, T, D]
            for other, op in ((rstd[:, :].unsqueeze(2), ALU.mult), (nmr[:, :].unsqueeze(2), ALU.add),
                              (grow[:, :].unsqueeze(1), ALU.mult), (brow[:, :].unsqueeze(1), ALU.add)):
                v.tensor_tensor(rows[:, :, :], rows[:, :, :], other.to_broadcast(wide), op)\
                 .then_inc(end_sems["step"], c.inc())
                v.wait_ge(end_sems["step"], c.now())
            v.scalar_tensor_tensor(xs[:, :, :], rows[:, :, :], 0.0, xs[:, :, :], ALU.max, ALU.add)\
             .then_inc(end_sems["step"], c.inc())
            v.wait_ge(end_sems["step"], c.now())
            v.sem_inc(layer_done[0], 1)

        GROUPS = T // 4

        def turn(e, pbuf, g):
            for k in range(4):
                j = 4 * g + k
                ins = e.transpose(pX[g % 4][:, k * P:(k + 1) * P], pbuf[:, j * P:(j + 1) * P], ident[:, :])
            return ins

        def tail_start(e, L, pbuf):
            e.wait_ge(L["p_ready"], 1)
            for g in range(4):
                turn(e, pbuf, g).then_inc(L["turned"], 1)

        def tail_tensor(e, L, seq, pbuf, pnext, product, signals=True):
            for g in range(GROUPS):
                e.wait_ge(L["evac"], GROUPS * seq + g + 1)
                for k in range(4):
                    j = 4 * g + k
                    ins = product(j, pT_ring[:, (j % 16) * P:(j % 16 + 1) * P])
                if g == GROUPS - 1 and signals:
                    ins.then_inc(L["o_ready"], 1)
                if g + 4 < GROUPS:
                    turn(e, pbuf, g + 4).then_inc(L["turned"], 1)
                elif pnext is not None:
                    if g + 4 == GROUPS:
                        e.wait_ge(L["p_ready"], seq + 2)
                    turn(e, pnext, g + 4 - GROUPS).then_inc(L["turned"], 1)

        def tail_evac(a, L, seq, half):
            for g in range(4 * half, 4 * half + 4):
                a.wait_ge(L["turned"], GROUPS * seq + g + 1)
                at = (g % 4) * 512
                a.copy(pT_ring[:, at:at + 512], pX[g % 4][:, :]).then_inc(L["evac"], 1)

        def product_rows(e, bank):
            return lambda j, pT: e.matmul(bank[:, 0:D], pT, rows[:, j, :], start=(j == 0), stop=(j == T - 1))

        TAIL = "p_ready turned evac o_ready o_read"

        def pairs(eng, tile):
            with eng.Fori(0, T // 2 - 1) as u:
                tile(u, 0, False)
                tile(u, 1, False)
            tile(T // 2 - 1, 0, True)
            tile(T // 2 - 1, 1, True)

        def peeled_pairs(eng, tile):
            tile(0, 0, False)
            tile(0, 1, False)
            with eng.Fori(1, T // 2 - 1) as u:
                tile(u, 0, False)
                tile(u, 1, False)
            tile(T // 2 - 1, 0, True)
            tile(T // 2 - 1, 1, True)

        L1 = layer_sems(1, TAIL + " adj0 adj1 mask w_in hs_ready s_ready z_ready zmax leaky own rcp")
        NEG1 = -9e15

        def l1_sync(y):
            y.wait_ge(layer_done[0], 1)
            y.dma_start(w1c[:, :], W1.rearrange("k d -> d k"), allow_slow_non_contiguous=True).then_inc(L1["w_in"], 16)
            y.dma_start(b1c[:, :], b1.unsqueeze(0).to_broadcast([P, 4])).then_inc(L1["w_in"], 16)
            with y.If(flag(y, 1) > 0):
                any_sync(y)
            with y.Else():
                binary_sync(y)

        def binary_sync(y):
            for p in range(2):
                y.dma_start(adj1[p][:, :], adj_tile(p)).then_inc(L1[f"adj{p}"], 16)
            with y.Fori(1, T // 2) as u:
                for p in range(2):
                    t = 2 * u + p
                    y.wait_ge(L1["mask"], t - 1)
                    y.dma_start(adj1[p][:, :], adj_tile(t)).then_inc(L1[f"adj{p}"], 16)

        def l1_vector(v):
            def mask(u, p):
                v.wait_ge(L1[f"adj{p}"], 16 * (u + 1))
                v.tensor_scalar(mask1[p][:, :], adj1[p][:, :], 1.0, NEG1, ALU.not_equal, ALU.mult)\
                 .then_inc(L1["mask"], 1)

            def scores(u, p):
                t = 2 * u + p
                v.wait_ge(L1["z_ready"], GROUPS * (t + 1))
                v.wait_ge(L1["mask"], t + 1)
                settled(v)
                v.tensor_tensor_reduce(Z1[p][:, :], Z1[p][:, :], mask1[p][:, :], 1.0, -3e38, ALU.add, ALU.max,
                                       zm[p][:, :]).then_inc(L1["zmax"], 1)
                v.wait_ge(L1["zmax"], t + 1)
                v.scalar_tensor_tensor(Z1[p][:, :], Z1[p][:, :], SLOPE, Z1[p][:, :], ALU.mult, ALU.max)
                v.scalar_tensor_tensor(nm[p][:, :], zm[p][:, :], SLOPE, zm[p][:, :], ALU.mult, ALU.max)\
                 .then_inc(L1["own"], 1)
                v.wait_ge(L1["own"], t + 1)
                v.tensor_scalar(nm[p][:, :], nm[p][:, :], -1.0, None, ALU.mult).then_inc(L1["leaky"], 1)

            def finish(u, p):
                t = 2 * u + p
                v.wait_ge(L1["p_ready"], t + 1)
                v.wait_ge(L1["o_read"], t)
                v.reciprocal(ri[:, :], rs[p][:, :]).then_inc(L1["rcp"], 1)
                v.wait_ge(L1["rcp"], t + 1)
                v.wait_ge(L1["o_ready"], t + 1)
                v.scalar_tensor_tensor(xs[:, t, :], pO[p][:, 0:D], ri[:, 0:1], xs[:, t, :], ALU.mult, ALU.add)\
                 .then_inc(L1["o_read"], 1)

            def tile(u, p, last):
                t = 2 * u + p
                if not (last and p == 1):
                    scores(u + p, 1 - p)
                if not last:
                    mask(u + 1, p)
                finish(u, p)
            mask(0, 0)
            mask(0, 1)
            scores(0, 0)
            pairs(v, tile)
            v.wait_ge(L1["o_read"], T)
            v.sem_inc(layer_done[1], 1)

        def l1_scalar(a):
            def lhs(u, p):
                t = 2 * u + p
                if not below(u, 1):
                    a.wait_ge(L1["s_ready"], GROUPS * (t - 1))
                a.activation(hs[p][:, :], cols[:, bass.ts(t, P)], ACT.Copy, scale=w1c[:, 0:1])\
                 .then_inc(L1["hs_ready"], 1)

            def evac_scores(u, p):
                t = 2 * u + p
                if not below(u, 1):
                    a.wait_ge(L1["p_ready"], t - 1)
                for c in range(GROUPS):
                    a.wait_ge(L1["s_ready"], GROUPS * t + c + 1)
                    a.activation(Z1[p][:, c * 512:(c + 1) * 512], pS[c % 2][:, :], ACT.Identity, bias=b1c[:, 0:1])\
                     .then_inc(L1["z_ready"], 1)

            def exps(u, p):
                t = 2 * u + p
                a.wait_ge(L1["leaky"], t + 1)
                if not below(u, 1):
                    a.wait_ge(L1["turned"], GROUPS * (t - 1))
                    a.wait_ge(L1["rcp"], t - 1)
                a.activation(P1[p][:, :], Z1[p][:, :], ACT.Exp, bias=nm[p][:, 0:1], accum_out=rs[p][:, 0:1])\
                 .then_inc(L1["p_ready"], 1)

            def tile(u, p, last):
                t = 2 * u + p
                tail_evac(a, L1, t, 0)
                if not last:
                    lhs(u + 1, p)
                    evac_scores(u + 1, p)
                if not (last and p == 1):
                    exps(u + p, 1 - p)
                tail_evac(a, L1, t, 1)
            for p in range(2):
                lhs(0, p)
                evac_scores(0, p)
            exps(0, 0)
            pairs(a, tile)

        def l1_tensor(e):
            def scores(u, p):
                t = 2 * u + p
                e.wait_ge(L1["hs_ready"], t + 1)
                for c in range(GROUPS):
                    if c >= 2 or not below(t, 1):
                        e.wait_ge(L1["z_ready"], GROUPS * t + c - 1)
                    e.matmul(pS[c % 2][:, :], hs[p][:, :], cols[:, c * 512:(c + 1) * 512], start=True, stop=True)\
                     .then_inc(L1["s_ready"], 1)

            def tile(u, p, last):
                if not last:
                    scores(u + 1, p)
                if not below(2 * u + p, 2):
                    e.wait_ge(L1["o_read"], 2 * u + p - 1)
                tail_tensor(e, L1, 2 * u + p, P1[p], None if last and p else P1[1 - p], product_rows(e, pO[p]))
            scores(0, 0)
            scores(0, 1)
            tail_start(e, L1, P1[0])
            peeled_pairs(e, tile)

        G1 = layer_sems("1any", TAIL + " adj hs_ready s_ready z_ready used sum own done")
        G1_STEPS = 14

        def any_sync(y):
            with y.Fori(0, T) as t:
                y.wait_ge(G1["o_read"], t)
                y.dma_start(adj1[0][:, :], adj_tile(t)).then_inc(G1["adj"], 16)

        def any_tensor(e):
            with e.Fori(0, T) as t:
                for k in range(4):
                    e.wait_ge(G1["hs_ready"], 4 * t + k + 1)
                    for c in range(GROUPS):
                        if k or c >= 2:
                            e.wait_ge(G1["z_ready"], GROUPS * (4 * t + k) + c - 1)
                        e.matmul(pS[c % 2][:, :], hs[0][:, :], cols[:, c * 512:(c + 1) * 512], start=True, stop=True)\
                         .then_inc(G1["s_ready"], 1)
                e.wait_ge(G1["p_ready"], t + 1)
                for g in range(4):
                    turn(e, P1[0], g).then_inc(G1["turned"], 1)
                e.wait_ge(G1["o_read"], t)
                tail_tensor(e, G1, t, P1[0], None, product_rows(e, pO[0]))

        def any_scalar(a):
            with a.Fori(0, T) as t:
                for k in range(4):
                    a.wait_ge(G1["s_ready"], GROUPS * (4 * t + k))
                    settled(a)
                    a.activation(hs[0][:, :], cols[:, bass.ts(t, P)], ACT.Copy, scale=w1c[:, k:k + 1])\
                     .then_inc(G1["hs_ready"], 1)
                    a.wait_ge(G1["used"], 4 * t + k)
                    for c in range(GROUPS):
                        a.wait_ge(G1["s_ready"], GROUPS * (4 * t + k) + c + 1)
                        a.activation(Z1[0][:, c * 512:(c + 1) * 512], pS[c % 2][:, :], ACT.Identity,
                                     bias=b1c[:, k:k + 1]).then_inc(G1["z_ready"], 1)
                a.wait_ge(G1["sum"], t + 1)
                a.activation(P1[0][:, :], Z1[1][:, :], ACT.Exp, accum_out=rs[0][:, 0:1]).then_inc(G1["p_ready"], 1)
                tail_evac(a, G1, t, 0)
                tail_evac(a, G1, t, 1)

        def any_vector(v):
            alpha, tmp, own = Z1[1], P1[1], G1["own"]
            with v.Fori(0, T) as t:
                k = Count(G1_STEPS * t)
                v.wait_ge(G1["adj"], 16 * (t + 1))
                v.tensor_scalar(alpha[:, :], adj1[0][:, :], 1.0, None, ALU.is_ge)
                v.tensor_scalar(tmp[:, :], adj1[0][:, :], 4.0, None, ALU.is_le).then_inc(own, k.inc())
                v.wait_ge(own, k.now())
                v.tensor_tensor(alpha[:, :], alpha[:, :], tmp[:, :], ALU.mult).then_inc(own, k.inc())
                v.wait_ge(own, k.now())
                v.tensor_scalar(alpha[:, :], alpha[:, :], -1.0, -NEG1, ALU.add, ALU.mult).then_inc(own, k.inc())
                for j in range(4):
                    v.wait_ge(G1["z_ready"], GROUPS * (4 * t + j + 1))
                    v.wait_ge(own, k.now())
                    v.scalar_tensor_tensor(tmp[:, :], Z1[0][:, :], SLOPE, Z1[0][:, :], ALU.mult, ALU.max)\
                     .then_inc(G1["used"], 1)
                    v.wait_ge(G1["used"], 4 * t + j + 1)
                    v.scalar_tensor_tensor(tmp[:, :], adj1[0][:, :], float(j + 1), tmp[:, :], ALU.is_equal, ALU.mult)\
                     .then_inc(own, k.inc())
                    v.wait_ge(own, k.now())
                    v.tensor_tensor(alpha[:, :], alpha[:, :], tmp[:, :], ALU.add).then_inc(own, k.inc())
                v.wait_ge(own, k.now())
                v.tensor_reduce(zm[0][:, :], alpha[:, :], AX, ALU.max).then_inc(own, k.inc())
                v.wait_ge(own, k.now())
                v.tensor_scalar(alpha[:, :], alpha[:, :], zm[0][:, 0:1], None, ALU.subtract).then_inc(G1["sum"], 1)
                v.wait_ge(G1["p_ready"], t + 1)
                v.reciprocal(ri[:, :], rs[0][:, :]).then_inc(own, k.inc())
                v.wait_ge(own, k.now())
                v.wait_ge(G1["o_ready"], t + 1)
                v.scalar_tensor_tensor(xs[:, t, :], pO[0][:, 0:D], ri[:, 0:1], xs[:, t, :], ALU.mult, ALU.add)\
                 .then_inc(G1["o_read"], 1)
                v.sem_inc(own, G1_STEPS - k.n)
            v.wait_ge(G1["o_read"], T)
            v.sem_inc(layer_done[1], 1)

        L2 = layer_sems(2, TAIL + " adj mask w_in wmade d_ready d_outV d_outA z_in own zmax leaky rcp scaled "
                        "z_own oT_in o_turned nan")
        P2 = [cols, P2b]
        oT, scaled = hcol, hrow

        def l2_sync(y):
            y.wait_ge(layer_done[1], 1)
            y.dma_start(w2s[:, 0:D], W2).then_inc(L2["w_in"], 16)
            y.dma_start(asd[:, :, :, :].rearrange("p h a f -> p (h a f)"),
                        a2.rearrange("h f -> (h f)").unsqueeze(0).to_broadcast([P, 2 * D])).then_inc(L2["w_in"], 16)
            y.dma_start(adj2[:, :], adj_tile(0)).then_inc(L2["adj"], 16)
            with y.Fori(1, T) as t:
                y.wait_ge(L2["mask"], t)
                y.dma_start(adj2[:, :], adj_tile(t)).then_inc(L2["adj"], 16)

        def l2_weights_vector(v):
            c = Count(0)
            v.wait_ge(L2["w_in"], 32)
            for side, to in ((0, w2s[:, D:D + HEADS]), (1, wd[:, :])):
                v.wait_ge(L2["wmade"], c.now())
                v.tensor_tensor(wa[:, :].rearrange("p (h f) -> p h f", h=HEADS),
                                w2s[:, 0:D].rearrange("p (h f) -> p h f", h=HEADS), asd[:, :, side, :], ALU.mult)\
                 .then_inc(L2["wmade"], c.inc())
                v.wait_ge(L2["wmade"], c.now())
                v.tensor_reduce(to, wa[:, :].rearrange("p (h f) -> p h f", h=HEADS), AX, ALU.add)\
                 .then_inc(L2["wmade"], c.inc())
            v.wait_ge(L2["wmade"], c.now())
            for h in range(HEADS):
                ins = v.tensor_scalar(wrep[:, h, :], ones[:, :], wd[:, h:h + 1], None, ALU.mult)
            ins.then_inc(L2["wmade"], c.inc())

        def l2_vector(v):
            for k in range(HEADS * GROUPS):
                if k % 2 == 0:
                    v.wait_ge(L2["d_ready"], k + 1)
                    v.tensor_copy(dbc[:, k // GROUPS, (k % GROUPS) * 512:(k % GROUPS + 1) * 512], pX[k % 4][:, :])\
                     .then_inc(L2["d_outV"], 1)

            def mask(t):
                v.wait_ge(L2["adj"], 16 * (t + 1))
                v.tensor_scalar(mask2[:, :], adj2[:, :], 0.0, MASKED, ALU.is_equal, ALU.mult)\
                 .then_inc(L2["mask"], 1)

            def leaky(t, h):
                seq, p = HEADS * t + h, h % 2
                if h == HEADS - 1:
                    v.wait_ge(L2["p_ready"], seq - 1)
                    v.tensor_scalar(Z2[p][:, :], dbc[:, h, :], si[:, t, h:h + 1], None, ALU.add)\
                     .then_inc(L2["z_own"], 1)
                    v.wait_ge(L2["z_own"], t + 1)
                else:
                    v.wait_ge(L2["z_in"], (HEADS - 1) * t + h + 1)
                v.scalar_tensor_tensor(Z2[p][:, :], Z2[p][:, :], SLOPE, Z2[p][:, :], ALU.mult, ALU.max)\
                 .then_inc(L2["own"], 1)

            def masked(t, h):
                seq, p = HEADS * t + h, h % 2
                if h == 0:
                    v.wait_ge(L2["mask"], t + 1)
                v.wait_ge(L2["own"], seq + 1)
                settled(v)
                v.tensor_tensor_reduce(Z2[p][:, :], Z2[p][:, :], mask2[:, :], 1.0, -3e38, ALU.add, ALU.max,
                                       zm2[p][:, :]).then_inc(L2["zmax"], 1)
                v.wait_ge(L2["zmax"], seq + 1)
                v.tensor_scalar(nm2[p][:, :], zm2[p][:, :], -1.0, None, ALU.mult).then_inc(L2["leaky"], 1)

            def finish(t, p):
                v.wait_ge(L2["p_ready"], HEADS * (t + 1))
                v.wait_ge(L2["o_read"], t)
                v.reciprocal(ri2[:, :], rs2[p][:, :]).then_inc(L2["rcp"], 1)
                v.wait_ge(L2["rcp"], t + 1)
                v.wait_ge(L2["o_turned"], t + 1)
                v.tensor_tensor(scaled[p][:, :].rearrange("p (h f) -> p h f", h=HEADS),
                                pS[p][:, 0:D].rearrange("p (h f) -> p h f", h=HEADS),
                                ri2[:, :].unsqueeze(2).to_broadcast([P, HEADS, HD]), ALU.mult)\
                 .then_inc(L2["scaled"], 1)
                v.wait_ge(L2["scaled"], t + 1)
                v.tensor_tensor(xs[:, t, :], scaled[p][:, :], xs[:, t, :], ALU.add).then_inc(L2["o_read"], 1)

            def tile(u, p, last):
                t = 2 * u + p
                last = last and p == 1
                for h in range(HEADS):
                    nxt = (t, h + 2) if h < HEADS - 2 else None if last else (t + 1, h - 2)
                    if h == HEADS - 2 and not last:
                        mask(t + 1)
                    if nxt:
                        leaky(*nxt)
                        masked(*nxt)
                    if h == 2 and not below(t, 1):
                        finish(t - 1, 1 - p)
            mask(0)
            for h in range(2):
                leaky(0, h)
                masked(0, h)
            peeled_pairs(v, tile)
            finish(T - 1, 1)
            c = Count(0)
            v.tensor_scalar(nan[:, :], top0[:, :], 0.0, 1e38, ALU.is_equal, ALU.mult).then_inc(L2["nan"], c.inc())
            v.wait_ge(L2["nan"], c.now())
            v.tensor_scalar(nan[:, :], nan[:, :], 1e38, None, ALU.mult).then_inc(L2["nan"], c.inc())
            v.wait_ge(L2["nan"], c.now())
            v.tensor_tensor(nan[:, :], nan[:, :], nan[:, :], ALU.subtract).then_inc(L2["nan"], c.inc())
            v.wait_ge(L2["nan"], c.now())
            v.wait_ge(L2["o_read"], T)
            v.tensor_tensor(xs[:, :, :], xs[:, :, :], nan[:, :].unsqueeze(2).to_broadcast([P, T, D]), ALU.add)\
             .then_inc(layer_done[2], 1)
            v.wait_ge(layer_done[2], 1)

        def l2_scalar(a):
            for k in range(HEADS * GROUPS):
                if k % 2 == 1:
                    a.wait_ge(L2["d_ready"], k + 1)
                    a.copy(dbc[:, k // GROUPS, (k % GROUPS) * 512:(k % GROUPS + 1) * 512], pX[k % 4][:, :])\
                     .then_inc(L2["d_outA"], 1)

            def sums(t, h):
                a.activation(Z2[h % 2][:, :], dbc[:, h, :], ACT.Identity, bias=si[:, t, h:h + 1])\
                 .then_inc(L2["z_in"], 1)

            def exps(t, h, q):
                seq, p = HEADS * t + h, h % 2
                a.wait_ge(L2["leaky"], seq + 1)
                if not below(seq, 2):
                    a.wait_ge(L2["turned"], GROUPS * (seq - 1))
                if not below(t, 2) and h == 0:
                    a.wait_ge(L2["rcp"], t - 1)
                a.activation(P2[p][:, :], Z2[p][:, :], ACT.Exp, bias=nm2[p][:, 0:1], accum_out=rs2[q][:, h:h + 1])\
                 .then_inc(L2["p_ready"], 1)

            def result(t, p):
                a.wait_ge(L2["o_ready"], t + 1)
                a.wait_ge(L2["o_turned"], t)
                a.copy(oT[p][:, :], pO[p][:, 0:P]).then_inc(L2["oT_in"], 1)

            def tile(u, p, last):
                t = 2 * u + p
                last = last and p == 1
                for h in range(HEADS):
                    tail_evac(a, L2, HEADS * t + h, 0)
                    if h == 0 and not below(t, 1):
                        result(t - 1, 1 - p)
                    if h < HEADS - 1:
                        exps(t, h + 1, p)
                    elif not last:
                        exps(t + 1, 0, 1 - p)
                    tail_evac(a, L2, HEADS * t + h, 1)
                    if not (last and h > 0) and h > 0:
                        a.wait_ge(L2["p_ready"], HEADS * t + h + 2)
                        sums(t + 1, h - 1)
            a.wait_ge(L2["d_outV"], HEADS * GROUPS // 2)
            a.wait_ge(L2["d_outA"], HEADS * GROUPS // 2)
            a.wait_ge(prep_sems[2]["w_out"], T)
            sums(0, 0)
            sums(0, 1)
            exps(0, 0, 0)
            a.wait_ge(L2["p_ready"], 1)
            sums(0, 2)
            peeled_pairs(a, tile)
            result(T - 1, 1)

        def l2_tensor(e):
            e.wait_ge(prep_sems[2]["w_out"], T)
            for k in range(HEADS * GROUPS):
                if k >= 4:
                    e.wait_ge(L2["d_outA" if k % 2 else "d_outV"], (k - 4) // 2 + 1)
                e.matmul(pX[k % 4][:, :], wrep[:, k // GROUPS, :], cols[:, (k % GROUPS) * 512:(k % GROUPS + 1) * 512],
                         start=True, stop=True).then_inc(L2["d_ready"], 1)

            def turn_result(t, p):
                e.wait_ge(L2["oT_in"], t + 1)
                e.wait_ge(L2["o_read"], t)
                e.transpose(pS[p][:, 0:P], oT[p][:, :], ident[:, :]).then_inc(L2["o_turned"], 1)

            def tile(u, p, last):
                t = 2 * u + p
                last = last and p == 1
                if not below(t, 2):
                    e.wait_ge(L2["oT_in"], t - 1)
                for h in range(HEADS):
                    if h == 1 and not below(t, 1):
                        turn_result(t - 1, 1 - p)
                    f = slice(h * HD, (h + 1) * HD)
                    tail_tensor(e, L2, HEADS * t + h, P2[h % 2], None if last and h == HEADS - 1 else P2[1 - h % 2],
                                lambda j, pT: e.matmul(pO[p][f, 0:P], rows[:, j, f], pT, start=(j == 0),
                                                       stop=(j == T - 1)), h == HEADS - 1)
            tail_start(e, L2, P2[0])
            peeled_pairs(e, tile)
            turn_result(T - 1, 1)

        L3 = layer_sems(3, TAIL + " adj0 adj1 own ident residual parts partsum")

        def l3_sync(y):
            for p in range(2):
                y.dma_start(adj1[p][:, :], adj_tile(p)).then_inc(L3[f"adj{p}"], 16)
            with y.Fori(1, T // 2) as u:
                for p in range(2):
                    t = 2 * u + p
                    y.wait_ge(L3["p_ready"], t - 1)
                    y.dma_start(adj1[p][:, :], adj_tile(t)).then_inc(L3[f"adj{p}"], 16)
            y.wait_ge(L3["o_read"], T)

        def l3_vector(v):
            def cast(u, p):
                t = 2 * u + p
                v.wait_ge(L3[f"adj{p}"], 16 * (u + 1))
                if not below(u, 1):
                    v.wait_ge(L3["turned"], GROUPS * (t - 1))
                v.tensor_copy(P1[p][:, :], adj1[p][:, :]).then_inc(L3["p_ready"], 1)

            def tile(u, p, last):
                t = 2 * u + p
                if not (last and p == 1):
                    cast(u + p, 1 - p)
                v.tensor_tensor(xs[:, t, :], xs[:, t, :], rows[:, t, :], ALU.add).then_inc(L3["own"], 1)
                v.wait_ge(L3["own"], t + 1)
                v.wait_ge(L3["o_ready"], t + 1)
                v.tensor_tensor(xs[:, t, :], pO[p][:, 0:D], xs[:, t, :], ALU.add).then_inc(L3["o_read"], 1)
            cast(0, 0)
            v.wait_ge(prep_sems[3]["hrow_ready"], T)
            pairs(v, tile)

        def l3_scalar(a):
            def tile(u, p, last):
                tail_evac(a, L3, 2 * u + p, 0)
                tail_evac(a, L3, 2 * u + p, 1)
            pairs(a, tile)

        def l3_tensor(e):
            tail_start(e, L3, P1[0])

            def tile(u, p, last):
                if not below(2 * u + p, 2):
                    e.wait_ge(L3["o_read"], 2 * u + p - 1)
                tail_tensor(e, L3, 2 * u + p, P1[p], None if last and p else P1[1 - p], product_rows(e, pO[p]))
            peeled_pairs(e, tile)

        BG = T // 8

        def binary_sum_vector(v):
            def cast(u, p):
                t = 2 * u + p
                v.wait_ge(L3[f"adj{p}"], 16 * (u + 1))
                if not below(t, 2):
                    v.wait_ge(L3["turned"], BG * (t - 1))
                v.tensor_copy(mask1[p][:, :], adj1[p][:, :]).then_inc(L3["p_ready"], 1)

            def tile(u, p, last):
                t = 2 * u + p
                if not last:
                    cast(u + 1, p)
                v.tensor_tensor(xs[:, t, :], xs[:, t, :], rows[:, t, :], ALU.add)
                v.wait_ge(L3["o_ready"], t + 1)
                v.wait_ge(L3["o_read"], t)
                v.tensor_reduce(hrow[0][:, :], pO[p][:, 0:3 * D].rearrange("p (a d) -> p d a", a=3), AX, ALU.add)\
                 .then_inc(L3["partsum"], 1)
                v.wait_ge(L3["partsum"], t + 1)
                v.tensor_tensor(xs[:, t, :], hrow[0][:, :], xs[:, t, :], ALU.add).then_inc(L3["o_read"], 1)
            v.tensor_copy(identb[:, :], ident[:, :]).then_inc(L3["ident"], 1)
            cast(0, 0)
            cast(0, 1)
            v.wait_ge(prep_sems[3]["hrow_ready"], T)
            rest = [rows, Z1[0], Z1[1]]
            flat = [b[:, :, :].rearrange("p t d -> p (t d)") if b is rows else b[:, :] for b in rest]
            for k in range(3):
                v.tensor_copy(hsplit[:, :, k, :], flat[k].rearrange("p (t d) -> p t d", d=D))\
                 .then_inc(L3["parts"], 1)
                if k < 2:
                    v.wait_ge(L3["parts"], k + 1)
                    v.tensor_tensor(flat[k + 1].rearrange("p (t d) -> p t d", d=D),
                                    flat[k].rearrange("p (t d) -> p t d", d=D), hsplit[:, :, k, :], ALU.subtract)\
                     .then_inc(L3["residual"], 1)
                    v.wait_ge(L3["residual"], k + 1)
            peeled_pairs(v, tile)

        def binary_sum_scalar(a):
            def tile(u, p, last):
                for g in range(BG):
                    a.wait_ge(L3["turned"], BG * (2 * u + p) + g + 1)
                    a.copy(aT_ring[:, g, :], pXb[g][:, :]).then_inc(L3["evac"], 1)
            pairs(a, tile)

        def binary_sum_tensor(e):
            def turn8(p, g):
                for k in range(8):
                    j = 8 * g + k
                    ins = e.transpose(pXb[g][:, k * P:(k + 1) * P], mask1[p][:, j * P:(j + 1) * P], identb[:, :])
                ins.then_inc(L3["turned"], 1)

            def tile(u, p, last):
                t = 2 * u + p
                if not below(t, 2):
                    e.wait_ge(L3["o_read"], t - 1)
                for g in range(BG):
                    e.wait_ge(L3["evac"], BG * t + g + 1)
                    for k in range(8):
                        j = 8 * g + k
                        ins = e.matmul(pO[p][:, 0:3 * D], aT_ring[:, g, k * P:(k + 1) * P],
                                       hsplit[:, j, :, :].rearrange("p a d -> p (a d)"), start=(j == 0),
                                       stop=(j == T - 1))
                    if g == BG - 1:
                        ins.then_inc(L3["o_ready"], 1)
                    if not (last and p == 1):
                        if g == 0:
                            e.wait_ge(L3["p_ready"], t + 2)
                        turn8(1 - p, g)
            e.wait_ge(L3["ident"], 1)
            e.wait_ge(L3["p_ready"], 1)
            for g in range(BG):
                turn8(0, g)
            e.wait_ge(L3["parts"], 3)
            peeled_pairs(e, tile)

        @block.sync
        def _(y):
            y.dma_start(xs[:, :, :], x_in.rearrange("(t p) d -> p t d", p=P)).then_inc(x_loaded, 16)
            for i, w in enumerate((W_l, W_r, W_v)):
                y.dma_start(wlrv[:, i * D:(i + 1) * D], w).then_inc(w_loaded, 16)
            for h in range(HEADS):
                y.dma_start(arow[:, h * HD:(h + 1) * HD], a0.unsqueeze(0).to_broadcast([P, HD])).then_inc(w_loaded, 16)
            y.dma_start(grow[:, :], ln_g.unsqueeze(0).to_broadcast([P, D])).then_inc(w_loaded, 16)
            y.dma_start(brow[:, :], ln_b.unsqueeze(0).to_broadcast([P, D])).then_inc(w_loaded, 16)
            q = prep_sems[0]
            kv_v = kv_dram.rearrange("(t p) d -> t p d", p=P)
            with y.Fori(0, T // 2) as u:
                for p in range(2):
                    t = 2 * u + p
                    y.wait_ge(q["w_copied"], t + 1)
                    y.wait_ge(q["w_out"], t + 1)
                    y.dma_start(kv_v[bass.ds(t, 1), :, :].rearrange("a p d -> (a p) d"), kvs[p][:, :])\
                     .then_inc(kvs_stored[p], 16)
            l0_sync(y)
            with y.If(flag(y, 0) > BAD_OVER):
                dense_sync(y)
            l1_sync(y)
            l2_sync(y)
            y.wait_ge(layer_done[2], 1)
            l3_sync(y)
            y.dma_start(out.rearrange("(t p) d -> p t d", p=P), xs[:, :, :]).then_inc(stored, 16)
            y.wait_ge(stored, 16)

        @block.gpsimd
        def _(g):
            g.memset(ident[:, :], 0.0).then_inc(consts, 1)
            g.memset(ones[:, :], 1.0)
            g.memset(mhalf[:, :], -0.5)
            g.memset(raised[:, :], 0.0)
            g.wait_ge(consts, 1)
            g.affine_select(out=ident[:, :], in_=ident[:, :], compare_op=ALU.not_equal, fill=1.0,
                            base=0, pattern=[[-1, P]], channel_multiplier=1).then_inc(consts, 1)
            g.iota(iota[:, :], [[-1, N]], base=N, channel_multiplier=0).then_inc(consts, 1)
            g.memset(ga[0][:, :, :], 0.0)
            g.memset(ga[1][:, :, :], 0.0).then_inc(consts, 1)
            g.wait_ge(consts, 4)
            for p in range(2):
                g.wait_ge(kvs_stored[p], 16 * (T // 2))
            l0_gpsimd(g)
        @block.vector
        def _(v):
            v.wait_ge(x_loaded, 16)
            v.wait_ge(w_loaded, 16 * 9)
            v.tensor_scalar(alin[:, :], arow[:, :], SLOPE, None, ALU.mult).then_inc(prep_sems[0]["arow"], 1)
            v.wait_ge(prep_sems[0]["arow"], 1)
            v.tensor_scalar(arow[:, :], arow[:, :], 1 - SLOPE, None, ALU.mult).then_inc(prep_sems[0]["arow"], 1)
            v.wait_ge(prep_sems[0]["arow"], 2)
            prep_vector(v, 0)
            l0_vector(v)
            flags_vector(v)
            with v.If(flag(v, 0) > BAD_OVER):
                dense_vector(v)
            l0_end_vector(v)
            prep_vector(v, 1)
            with v.If(flag(v, 1) > 0):
                any_vector(v)
            with v.Else():
                l1_vector(v)
            l2_weights_vector(v)
            prep_vector(v, 2)
            l2_vector(v)
            prep_vector(v, 3)
            with v.If(flag(v, 1) > 0):
                l3_vector(v)
            with v.Else():
                binary_sum_vector(v)

        @block.scalar
        def _(a):
            a.wait_ge(x_loaded, 16)
            prep_scalar(a, 0)
            l0_scalar(a)
            with a.If(flag(a, 0) > BAD_OVER):
                dense_scalar(a)
            root_scalar(a, end_sems)
            prep_scalar(a, 1)
            a.wait_ge(L1["w_in"], 32)
            a.wait_ge(prep_sems[1]["hcol_ready"], T)
            with a.If(flag(a, 1) > 0):
                any_scalar(a)
            with a.Else():
                l1_scalar(a)
            prep_scalar(a, 2)
            l2_scalar(a)
            prep_scalar(a, 3)
            with a.If(flag(a, 1) > 0):
                l3_scalar(a)
            with a.Else():
                binary_sum_scalar(a)

        @block.tensor
        def _(e):
            e.wait_ge(consts, 4)
            e.wait_ge(w_loaded, 16 * 9)
            prep_tensor(e, 0)
            l0_tensor(e)
            flags_tensor(e)
            with e.If(flag(e, 0) > BAD_OVER):
                dense_tensor(e)
            prep_tensor(e, 1)
            e.wait_ge(prep_sems[1]["hcol_ready"], T)
            with e.If(flag(e, 1) > 0):
                any_tensor(e)
            with e.Else():
                l1_tensor(e)
            e.wait_ge(L2["wmade"], 5)
            prep_tensor(e, 2)
            l2_tensor(e)
            e.wait_ge(prep_sems[3]["hrow_ready"], T)
            with e.If(flag(e, 1) > 0):
                l3_tensor(e)
            with e.Else():
                binary_sum_tensor(e)


_INS = ["x", "adj", "L0_gnn_W_l", "L0_gnn_W_r", "L0_gnn_W_v", "L0_gnn_a", "L0_gnn_ln_g", "L0_gnn_ln_b",
        "L1_gnn_W", "L1_gnn_b", "L2_gnn_W", "L2_gnn_a"]


def kernel(**inputs):
    import numpy as _np
    import concourse.bacc as _bacc
    from concourse import mybir as _mybir
    from concourse.bass_utils import run_bass_kernel_spmd as _run

    nc = _bacc.Bacc("TRN2", target_bir_lowering=False, num_devices=1)
    arrays, args = {}, []
    for name in _INS:
        a = _np.ascontiguousarray(inputs[name])
        arrays[f"in_{name}_dram"] = a
        args.append(nc.dram_tensor(f"in_{name}_dram", a.shape, _mybir.dt.from_np(a.dtype), kind="ExternalInput").ap())
    o = nc.dram_tensor("out_0_dram", (N, D), F32, kind="ExternalOutput").ap()
    build(nc, *args, o)
    r = _run(nc, [arrays], core_ids=[0])
    return r.results[0]["out_0_dram"]
```
